# Optimizing a Trainium2 kernel written in Bass

```python
import numpy as np
import jax
import jax.numpy as jnp

def _softmax(x, axis=-1):
    return jax.nn.softmax(x, axis=axis)

def _gelu(x):
    return jax.nn.gelu(x, approximate=True)

def _silu(x):
    return jax.nn.silu(x)

def _sigmoid(x):
    return jax.nn.sigmoid(x)

def _layernorm(x, axis=-1, eps=1e-05):
    m = jnp.mean(x, axis=axis, keepdims=True)
    v = jnp.var(x, axis=axis, keepdims=True)
    return (x - m) / jnp.sqrt(v + eps)

def _scatter_add(tgt, idx, src, axis=0):
    return tgt.at[idx].add(src)

def _segment_sum(src, seg, n):
    return jax.ops.segment_sum(src, seg, n)
kernel_name = 'mk_decoder_preln_d4_seqx_r8_465cfa'

def setup_inputs(seed: int=0):
    np.random.seed(seed)
    _w = jnp.asarray

    def _rec_inputs():
        import jax
        import jax.numpy as jnp
        _rk = jax.random.key(seed)
        x = 7.22e-05 + 1 * jax.random.normal(jax.random.fold_in(_rk, 1), (4, 512, 128), jnp.float32)
        _lenS = 512 - jax.random.randint(jax.random.fold_in(_rk, 7), (4,), 0, max(1, 512 // 4) + 1, jnp.int32)
        _lenS2 = 77 - jax.random.randint(jax.random.fold_in(_rk, 8), (4,), 0, max(1, 77 // 4) + 1, jnp.int32)
        _ctx_1024P = jax.random.normal(jax.random.fold_in(_rk, 11), (4, 16, 128), jnp.float32)
        _ctx_1024c = jax.random.dirichlet(jax.random.fold_in(_rk, 511), 0.3 * jnp.ones((16,), jnp.float32), (4, 77))
        _ctx_1024t = jnp.einsum('bsk,bkd->bsd', _ctx_1024c, _ctx_1024P)
        _ctx_1024t = _ctx_1024t * jax.lax.rsqrt(jnp.mean(jnp.square(_ctx_1024t)) + 1e-12) * 0.953939
        ctx_1024 = 4.13588e-05 + 0.999923 * (_ctx_1024t + 0.3 * jax.random.normal(jax.random.fold_in(_rk, 611), (4, 77, 128), jnp.float32))
        return (x, ctx_1024)
    x, ctx_1024 = _rec_inputs()

    def _L0_attn_setup():
        import jax, jax.numpy as jnp
        import numpy as np
        D_MODEL = 128
        NUM_HEADS = 16
        HEAD_DIM = D_MODEL // NUM_HEADS
        THETA = 10000.0
        B, S = (2, 256)

        def _apply_rope(t, cos, sin):
            te = t[..., 0::2]
            to = t[..., 1::2]
            re = te * cos - to * sin
            ro = te * sin + to * cos
            out = jnp.stack([re, ro], axis=-1)
            return out.reshape(t.shape)
        key = jax.random.key(seed)
        kx, kq, kk, kv, ko = jax.random.split(key, 5)
        std = 2.0 / (2 * D_MODEL) ** 0.5

        def w(k):
            return jnp.clip(std * jax.random.normal(k, (D_MODEL, D_MODEL), jnp.float32), -3.0 * std, 3.0 * std)
        return {'x': jax.random.normal(kx, (B, S, D_MODEL), jnp.float32), 'Wq': w(kq), 'Wk': w(kk), 'Wv': w(kv), 'Wo': w(ko)}
    _L0_attn_all = _L0_attn_setup()
    _L0_attn_in = {k: v for k, v in _L0_attn_all.items() if k in ('Wq', 'Wk', 'Wv', 'Wo')}
    del _L0_attn_all

    def _L0_xattn_setup():
        import jax, jax.numpy as jnp
        import numpy as np
        HIDDEN = 128
        HEADS = 16
        HEAD_DIM = HIDDEN // HEADS
        key = jax.random.key(seed)
        ks = jax.random.split(key, 11)
        B, S, D = (4, 256, 128)
        s = 0.02
        return {'query': jax.random.normal(ks[0], (B, S, D), jnp.float32), 'key': jax.random.normal(ks[1], (B, S, D), jnp.float32), 'value': jax.random.normal(ks[2], (B, S, D), jnp.float32), 'Wq': jax.random.normal(ks[3], (HIDDEN, D), jnp.float32) * s, 'bq': jnp.zeros((HIDDEN,), jnp.float32), 'Wk': jax.random.normal(ks[4], (HIDDEN, D), jnp.float32) * s, 'bk': jnp.zeros((HIDDEN,), jnp.float32), 'Wv': jax.random.normal(ks[5], (HIDDEN, D), jnp.float32) * s, 'bv': jnp.zeros((HIDDEN,), jnp.float32), 'Wo': jax.random.normal(ks[6], (HIDDEN, HIDDEN), jnp.float32) * s, 'bo': jnp.zeros((HIDDEN,), jnp.float32)}
    _L0_xattn_all = _L0_xattn_setup()
    _L0_xattn_in = {k: v for k, v in _L0_xattn_all.items() if k in ('Wq', 'bq', 'Wk', 'bk', 'Wv', 'bv', 'Wo', 'bo')}
    del _L0_xattn_all

    def _L0_ffn_setup():
        import jax, jax.numpy as jnp
        import numpy as np
        E, K, D, H = (8, 2, 128, 256)
        B, S = (1, 128)

        def _grouped_swiglu(x_sorted, counts, w1, w2, w3):
            if hasattr(jax.lax, 'ragged_dot'):
                gs = counts.astype(jnp.int32)
                h = jax.nn.silu(jax.lax.ragged_dot(x_sorted, w1, gs)) * jax.lax.ragged_dot(x_sorted, w3, gs)
                return jax.lax.ragged_dot(h, w2, gs)
            pos = jnp.arange(x_sorted.shape[0])
            eid = jnp.searchsorted(jnp.cumsum(counts), pos, side='right')
            out = jnp.zeros((x_sorted.shape[0], w2.shape[-1]), x_sorted.dtype)
            for e in range(w1.shape[0]):
                xm = jnp.where((eid == e)[:, None], x_sorted, 0.0)
                he = jax.nn.silu(xm @ w1[e]) * (xm @ w3[e])
                out = out + he @ w2[e]
            return out
        key = jax.random.key(seed)
        k0, k1, k2, k3, k4 = jax.random.split(key, 5)
        sD = 1.0 / np.sqrt(D)
        sH = 1.0 / np.sqrt(H)
        return {'hidden_states': jax.random.normal(k0, (B, S, D), jnp.float32), 'gate_w': jax.random.normal(k1, (E, D), jnp.float32) * sD, 'w1': jax.random.normal(k2, (E, D, H), jnp.float32) * sD, 'w2': jax.random.normal(k3, (E, H, D), jnp.float32) * sH, 'w3': jax.random.normal(k4, (E, D, H), jnp.float32) * sD}
    _L0_ffn_all = _L0_ffn_setup()
    _L0_ffn_in = {k: v for k, v in _L0_ffn_all.items() if k in ('gate_w', 'w1', 'w2', 'w3')}
    del _L0_ffn_all

    def _L1_attn_setup():
        import jax, jax.numpy as jnp
        import numpy as np
        import math
        EPS = 1e-06

        def favorplus_features(x, proj):
            xw = jnp.einsum('bhtd,hmd->bhtm', x, proj)
            xw = xw - jnp.max(xw, axis=-1, keepdims=True)
            x_norm_sq = jnp.sum(x * x, axis=-1, keepdims=True)
            return jnp.exp(xw) * jnp.exp(-0.5 * x_norm_sq) + EPS
        key = jax.random.key(seed)
        ks = jax.random.split(key, 6)
        B, T, d = (2, 512, 128)
        h, m = (16, 32)
        dk = d // h
        s = 1.0 / math.sqrt(d)
        return {'x': jax.random.normal(ks[0], (B, T, d), dtype=jnp.float32), 'Wq': jax.random.normal(ks[1], (d, d), dtype=jnp.float32) * s, 'Wk': jax.random.normal(ks[2], (d, d), dtype=jnp.float32) * s, 'Wv': jax.random.normal(ks[3], (d, d), dtype=jnp.float32) * s, 'Wo': jax.random.normal(ks[4], (d, d), dtype=jnp.float32) * s, 'bo': jnp.zeros((d,), dtype=jnp.float32), 'proj': jax.random.normal(ks[5], (h, m, dk), dtype=jnp.float32)}
    _L1_attn_all = _L1_attn_setup()
    _L1_attn_in = {k: v for k, v in _L1_attn_all.items() if k in ('Wq', 'Wk', 'Wv', 'Wo', 'bo', 'proj')}
    del _L1_attn_all

    def _L1_xattn_setup():
        import jax, jax.numpy as jnp
        import numpy as np
        DIM = 128
        NUM_HEADS = 16
        DIM_HEAD = 64
        INNER = NUM_HEADS * DIM_HEAD
        SCALE = DIM_HEAD ** (-0.5)

        def _layernorm(x, gamma, beta, eps=1e-05):
            mu = jnp.mean(x, axis=-1, keepdims=True)
            var = jnp.mean(jnp.square(x - mu), axis=-1, keepdims=True)
            return (x - mu) * jax.lax.rsqrt(var + eps) * gamma + beta
        key = jax.random.key(seed)
        ks = jax.random.split(key, 8)
        B, SQ, SK = (2, 256, 512)
        x = jax.random.normal(ks[0], (B, SQ, DIM), dtype=jnp.float32)
        context = jax.random.normal(ks[1], (B, SK, DIM), dtype=jnp.float32)
        ln_gamma = jnp.ones((DIM,), jnp.float32)
        ln_beta = jnp.zeros((DIM,), jnp.float32)
        w_q = jax.random.normal(ks[2], (DIM, INNER), dtype=jnp.float32) / np.sqrt(DIM)
        w_kv = jax.random.normal(ks[3], (DIM, 2 * INNER), dtype=jnp.float32) / np.sqrt(DIM)
        w_out = jax.random.normal(ks[4], (INNER, DIM), dtype=jnp.float32) / np.sqrt(INNER)
        b_out = jnp.zeros((DIM,), jnp.float32)
        gate = jnp.array([0.5], jnp.float32)
        return {'x': x, 'context': context, 'ln_gamma': ln_gamma, 'ln_beta': ln_beta, 'w_q': w_q, 'w_kv': w_kv, 'w_out': w_out, 'b_out': b_out, 'gate': gate}
    _L1_xattn_all = _L1_xattn_setup()
    _L1_xattn_in = {k: v for k, v in _L1_xattn_all.items() if k in ('ln_gamma', 'ln_beta', 'w_q', 'w_kv', 'w_out', 'b_out', 'gate')}
    del _L1_xattn_all

    def _L1_ffn_setup():
        import jax, jax.numpy as jnp
        import numpy as np
        SL, BS, HS, FF, E, TOPK = (256, 2, 128, 512, 8, 2)
        key = jax.random.key(seed)
        ks = jax.random.split(key, 6)
        T = SL * BS
        x = jax.random.normal(ks[0], (SL, BS, HS), jnp.float32)
        scores = jax.random.uniform(ks[1], (T, E), jnp.float32)
        expert_weights = jax.random.uniform(ks[2], (T, TOPK), jnp.float32)
        expert_indices = jax.random.randint(ks[3], (T, TOPK), 0, E, jnp.int32)
        w1 = jax.random.normal(ks[4], (E, HS, FF), jnp.float32) * (1.0 / np.sqrt(HS))
        w2 = jax.random.normal(ks[5], (E, FF, HS), jnp.float32) * (1.0 / np.sqrt(FF))
        bias = jnp.zeros((HS,), jnp.float32)
        return dict(x=x, scores=scores, expert_weights=expert_weights, expert_indices=expert_indices, w1=w1, w2=w2, bias=bias)
    _L1_ffn_all = _L1_ffn_setup()
    _L1_ffn_in = {k: v for k, v in _L1_ffn_all.items() if k in ('scores', 'expert_weights', 'expert_indices', 'w1', 'w2', 'bias')}
    del _L1_ffn_all

    def _L2_attn_setup():
        import jax, jax.numpy as jnp
        import numpy as np
        B, N, DIM = (4, 128, 128)
        H, DH = (16, 64)
        NUM_MEM = 64
        TOPK = 64
        SCALE = DH ** (-0.5)

        def _split_heads(t):
            b, n, _ = t.shape
            return t.reshape(b, n, H, DH).transpose(0, 2, 1, 3)
        key = jax.random.key(seed)
        ks = jax.random.split(key, 10)
        d_inner = H * DH
        return {'x': jax.random.normal(ks[0], (B, N, DIM), dtype=jnp.float32), 'Wq': jax.random.normal(ks[1], (d_inner, DIM), dtype=jnp.float32) * 0.02, 'Wk': jax.random.normal(ks[2], (d_inner, DIM), dtype=jnp.float32) * 0.02, 'Wv': jax.random.normal(ks[3], (d_inner, DIM), dtype=jnp.float32) * 0.02, 'pre_proj': jax.random.normal(ks[4], (H, H), dtype=jnp.float32) * 0.1, 'post_proj': jax.random.normal(ks[5], (H, H), dtype=jnp.float32) * 0.1, 'mem_k': jax.random.normal(ks[6], (H, NUM_MEM, DH), dtype=jnp.float32), 'mem_v': jax.random.normal(ks[7], (H, NUM_MEM, DH), dtype=jnp.float32), 'Wout': jax.random.normal(ks[8], (DIM, d_inner), dtype=jnp.float32) * 0.02, 'bout': jnp.zeros((DIM,), dtype=jnp.float32)}
    _L2_attn_all = _L2_attn_setup()
    _L2_attn_in = {k: v for k, v in _L2_attn_all.items() if k in ('Wq', 'Wk', 'Wv', 'pre_proj', 'post_proj', 'mem_k', 'mem_v', 'Wout', 'bout')}
    del _L2_attn_all

    def _L2_xattn_setup():
        import jax, jax.numpy as jnp
        import numpy as np
        D_MODEL = 128
        NUM_HEADS = 16
        D_K = D_MODEL // NUM_HEADS
        B, S = (4, 256)

        def _split_heads(x):
            b, s, _ = x.shape
            return x.reshape(b, s, NUM_HEADS, D_K).transpose(0, 2, 1, 3)
        key = jax.random.key(seed)
        ks = jax.random.split(key, 11)
        scale = 1.0 / np.sqrt(D_MODEL)
        inp = {'query': jax.random.normal(ks[0], (B, S, D_MODEL), jnp.float32), 'key_': jax.random.normal(ks[1], (B, S, D_MODEL), jnp.float32), 'value': jax.random.normal(ks[2], (B, S, D_MODEL), jnp.float32), 'w_q': jax.random.normal(ks[3], (D_MODEL, D_MODEL), jnp.float32) * scale, 'b_q': jnp.zeros((D_MODEL,), jnp.float32), 'w_k': jax.random.normal(ks[4], (D_MODEL, D_MODEL), jnp.float32) * scale, 'b_k': jnp.zeros((D_MODEL,), jnp.float32), 'w_v': jax.random.normal(ks[5], (D_MODEL, D_MODEL), jnp.float32) * scale, 'b_v': jnp.zeros((D_MODEL,), jnp.float32), 'w_o': jax.random.normal(ks[6], (D_MODEL, D_MODEL), jnp.float32) * scale, 'b_o': jnp.zeros((D_MODEL,), jnp.float32)}
        return inp
    _L2_xattn_all = _L2_xattn_setup()
    _L2_xattn_in = {k: v for k, v in _L2_xattn_all.items() if k in ('w_q', 'b_q', 'w_k', 'b_k', 'w_v', 'b_v', 'w_o', 'b_o')}
    del _L2_xattn_all

    def _L2_ffn_setup():
        import jax, jax.numpy as jnp
        import numpy as np
        B, S, H, F, E = (4, 256, 128, 512, 8)
        key = jax.random.key(seed)
        ks = jax.random.split(key, 8)
        s = 1.0 / np.sqrt(H)
        sf = 1.0 / np.sqrt(F)
        return {'x': jax.random.normal(ks[0], (B, S, H), jnp.float32), 'wr': jax.random.uniform(ks[1], (H, E), jnp.float32, -s, s), 'br': jax.random.uniform(ks[2], (E,), jnp.float32, -s, s), 'w1': jax.random.uniform(ks[3], (E, H, F), jnp.float32, -s, s), 'b1': jax.random.uniform(ks[4], (E, F), jnp.float32, -s, s), 'w2': jax.random.uniform(ks[5], (E, F, H), jnp.float32, -sf, sf), 'b2': jax.random.uniform(ks[6], (E, H), jnp.float32, -sf, sf)}
    _L2_ffn_all = _L2_ffn_setup()
    _L2_ffn_in = {k: v for k, v in _L2_ffn_all.items() if k in ('wr', 'br', 'w1', 'b1', 'w2', 'b2')}
    del _L2_ffn_all

    def _L3_attn_setup():
        import jax, jax.numpy as jnp
        import numpy as np
        import math
        D_MODEL = 128
        NUM_HEADS = 16
        B, L = (2, 256)
        PERIODS = (1.0, 30.0)
        WEIGHTS = (0.8, 0.4)
        SIGMAS = (0.5, 2.0)

        def _gaussian_mask(length):
            idx = jnp.arange(length, dtype=jnp.float32)
            delta = jnp.abs(idx[:, None] - idx[None, :])
            mask = jnp.zeros_like(delta)
            for p, w, sigma in zip(PERIODS, WEIGHTS, SIGMAS):
                if p < 0.2:
                    continue
                mask = mask + w * jnp.exp(-(delta - p) ** 2 / (2.0 * sigma ** 2))
            return mask
        key = jax.random.key(seed)
        ks = jax.random.split(key, 10)
        s = 1.0 / math.sqrt(D_MODEL)
        inp = {'x': jax.random.normal(ks[0], (B, L, D_MODEL), dtype=jnp.float32), 'Wq': jax.random.normal(ks[1], (D_MODEL, D_MODEL), dtype=jnp.float32) * s, 'bq': jax.random.normal(ks[2], (D_MODEL,), dtype=jnp.float32) * 0.01, 'Wk': jax.random.normal(ks[3], (D_MODEL, D_MODEL), dtype=jnp.float32) * s, 'bk': jax.random.normal(ks[4], (D_MODEL,), dtype=jnp.float32) * 0.01, 'Wv': jax.random.normal(ks[5], (D_MODEL, D_MODEL), dtype=jnp.float32) * s, 'bv': jax.random.normal(ks[6], (D_MODEL,), dtype=jnp.float32) * 0.01, 'Wo': jax.random.normal(ks[7], (D_MODEL, D_MODEL), dtype=jnp.float32) * s, 'bo': jax.random.normal(ks[8], (D_MODEL,), dtype=jnp.float32) * 0.01, 'prior_lambda': jnp.asarray(2.0, dtype=jnp.float32)}
        return inp
    _L3_attn_all = _L3_attn_setup()
    _L3_attn_in = {k: v for k, v in _L3_attn_all.items() if k in ('Wq', 'bq', 'Wk', 'bk', 'Wv', 'bv', 'Wo', 'bo', 'prior_lambda')}
    del _L3_attn_all

    def _L3_xattn_setup():
        import jax, jax.numpy as jnp
        import numpy as np
        EMB = 128
        HEADS = 16
        HEAD_DIM = EMB // HEADS
        key = jax.random.key(seed)
        ks = jax.random.split(key, 7)
        B, Q, KV = (2, 256, 512)
        s = 1.0 / np.sqrt(EMB)
        return {'x': jax.random.normal(ks[0], (B, Q, EMB), dtype=jnp.float32), 'context': jax.random.normal(ks[1], (B, KV, EMB), dtype=jnp.float32), 'Wq': jax.random.normal(ks[2], (EMB, EMB), dtype=jnp.float32) * s, 'Wk': jax.random.normal(ks[3], (EMB, EMB), dtype=jnp.float32) * s, 'Wv': jax.random.normal(ks[4], (EMB, EMB), dtype=jnp.float32) * s, 'Wo': jax.random.normal(ks[5], (EMB, EMB), dtype=jnp.float32) * s, 'bo': jax.random.normal(ks[6], (EMB,), dtype=jnp.float32) * 0.01}
    _L3_xattn_all = _L3_xattn_setup()
    _L3_xattn_in = {k: v for k, v in _L3_xattn_all.items() if k in ('Wq', 'Wk', 'Wv', 'Wo', 'bo')}
    del _L3_xattn_all

    def _L3_ffn_setup():
        import jax, jax.numpy as jnp
        import numpy as np
        D, H, E, K, S = (128, 256, 8, 2, 1)
        B, L = (4, 256)
        key = jax.random.key(seed)
        ks = jax.random.split(key, 9)
        std = 0.02
        return {'x': jax.random.normal(ks[0], (B, L, D), dtype=jnp.float32), 'router_w': jax.random.normal(ks[1], (E, D), dtype=jnp.float32) * std, 'experts_bias': jnp.zeros((E,), dtype=jnp.float32), 'w1': jax.random.normal(ks[2], (E, D, H), dtype=jnp.float32) * std, 'w3': jax.random.normal(ks[3], (E, D, H), dtype=jnp.float32) * std, 'w2': jax.random.normal(ks[4], (E, H, D), dtype=jnp.float32) * std, 'sw1': jax.random.normal(ks[5], (S, D, H), dtype=jnp.float32) * std, 'sw3': jax.random.normal(ks[6], (S, D, H), dtype=jnp.float32) * std, 'sw2': jax.random.normal(ks[7], (S, H, D), dtype=jnp.float32) * std}
    _L3_ffn_all = _L3_ffn_setup()
    _L3_ffn_in = {k: v for k, v in _L3_ffn_all.items() if k in ('router_w', 'experts_bias', 'w1', 'w3', 'w2', 'sw1', 'sw3', 'sw2')}
    del _L3_ffn_all
    return {'x': x, 'ctx_1024': ctx_1024, 'L0_attn_Wq': _L0_attn_in['Wq'], 'L0_attn_Wk': _L0_attn_in['Wk'], 'L0_attn_Wv': _L0_attn_in['Wv'], 'L0_attn_Wo': _L0_attn_in['Wo'], 'L0_xattn_Wq': _L0_xattn_in['Wq'], 'L0_xattn_bq': _L0_xattn_in['bq'], 'L0_xattn_Wk': _L0_xattn_in['Wk'], 'L0_xattn_bk': _L0_xattn_in['bk'], 'L0_xattn_Wv': _L0_xattn_in['Wv'], 'L0_xattn_bv': _L0_xattn_in['bv'], 'L0_xattn_Wo': _L0_xattn_in['Wo'], 'L0_xattn_bo': _L0_xattn_in['bo'], 'L0_ffn_gate_w': _L0_ffn_in['gate_w'], 'L0_ffn_w1': _L0_ffn_in['w1'], 'L0_ffn_w2': _L0_ffn_in['w2'], 'L0_ffn_w3': _L0_ffn_in['w3'], 'L1_attn_Wq': _L1_attn_in['Wq'], 'L1_attn_Wk': _L1_attn_in['Wk'], 'L1_attn_Wv': _L1_attn_in['Wv'], 'L1_attn_Wo': _L1_attn_in['Wo'], 'L1_attn_bo': _L1_attn_in['bo'], 'L1_attn_proj': _L1_attn_in['proj'], 'L1_xattn_ln_gamma': _L1_xattn_in['ln_gamma'], 'L1_xattn_ln_beta': _L1_xattn_in['ln_beta'], 'L1_xattn_w_q': _L1_xattn_in['w_q'], 'L1_xattn_w_kv': _L1_xattn_in['w_kv'], 'L1_xattn_w_out': _L1_xattn_in['w_out'], 'L1_xattn_b_out': _L1_xattn_in['b_out'], 'L1_xattn_gate': _L1_xattn_in['gate'], 'L1_ffn_scores': _L1_ffn_in['scores'], 'L1_ffn_expert_weights': _L1_ffn_in['expert_weights'], 'L1_ffn_expert_indices': _L1_ffn_in['expert_indices'], 'L1_ffn_w1': _L1_ffn_in['w1'], 'L1_ffn_w2': _L1_ffn_in['w2'], 'L1_ffn_bias': _L1_ffn_in['bias'], 'L2_attn_Wq': _L2_attn_in['Wq'], 'L2_attn_Wk': _L2_attn_in['Wk'], 'L2_attn_Wv': _L2_attn_in['Wv'], 'L2_attn_pre_proj': _L2_attn_in['pre_proj'], 'L2_attn_post_proj': _L2_attn_in['post_proj'], 'L2_attn_mem_k': _L2_attn_in['mem_k'], 'L2_attn_mem_v': _L2_attn_in['mem_v'], 'L2_attn_Wout': _L2_attn_in['Wout'], 'L2_attn_bout': _L2_attn_in['bout'], 'L2_xattn_w_q': _L2_xattn_in['w_q'], 'L2_xattn_b_q': _L2_xattn_in['b_q'], 'L2_xattn_w_k': _L2_xattn_in['w_k'], 'L2_xattn_b_k': _L2_xattn_in['b_k'], 'L2_xattn_w_v': _L2_xattn_in['w_v'], 'L2_xattn_b_v': _L2_xattn_in['b_v'], 'L2_xattn_w_o': _L2_xattn_in['w_o'], 'L2_xattn_b_o': _L2_xattn_in['b_o'], 'L2_ffn_wr': _L2_ffn_in['wr'], 'L2_ffn_br': _L2_ffn_in['br'], 'L2_ffn_w1': _L2_ffn_in['w1'], 'L2_ffn_b1': _L2_ffn_in['b1'], 'L2_ffn_w2': _L2_ffn_in['w2'], 'L2_ffn_b2': _L2_ffn_in['b2'], 'L3_attn_Wq': _L3_attn_in['Wq'], 'L3_attn_bq': _L3_attn_in['bq'], 'L3_attn_Wk': _L3_attn_in['Wk'], 'L3_attn_bk': _L3_attn_in['bk'], 'L3_attn_Wv': _L3_attn_in['Wv'], 'L3_attn_bv': _L3_attn_in['bv'], 'L3_attn_Wo': _L3_attn_in['Wo'], 'L3_attn_bo': _L3_attn_in['bo'], 'L3_attn_prior_lambda': _L3_attn_in['prior_lambda'], 'L3_xattn_Wq': _L3_xattn_in['Wq'], 'L3_xattn_Wk': _L3_xattn_in['Wk'], 'L3_xattn_Wv': _L3_xattn_in['Wv'], 'L3_xattn_Wo': _L3_xattn_in['Wo'], 'L3_xattn_bo': _L3_xattn_in['bo'], 'L3_ffn_router_w': _L3_ffn_in['router_w'], 'L3_ffn_experts_bias': _L3_ffn_in['experts_bias'], 'L3_ffn_w1': _L3_ffn_in['w1'], 'L3_ffn_w3': _L3_ffn_in['w3'], 'L3_ffn_w2': _L3_ffn_in['w2'], 'L3_ffn_sw1': _L3_ffn_in['sw1'], 'L3_ffn_sw3': _L3_ffn_in['sw3'], 'L3_ffn_sw2': _L3_ffn_in['sw2']}

def reference(x, ctx_1024, L0_attn_Wq, L0_attn_Wk, L0_attn_Wv, L0_attn_Wo, L0_xattn_Wq, L0_xattn_bq, L0_xattn_Wk, L0_xattn_bk, L0_xattn_Wv, L0_xattn_bv, L0_xattn_Wo, L0_xattn_bo, L0_ffn_gate_w, L0_ffn_w1, L0_ffn_w2, L0_ffn_w3, L1_attn_Wq, L1_attn_Wk, L1_attn_Wv, L1_attn_Wo, L1_attn_bo, L1_attn_proj, L1_xattn_ln_gamma, L1_xattn_ln_beta, L1_xattn_w_q, L1_xattn_w_kv, L1_xattn_w_out, L1_xattn_b_out, L1_xattn_gate, L1_ffn_scores, L1_ffn_expert_weights, L1_ffn_expert_indices, L1_ffn_w1, L1_ffn_w2, L1_ffn_bias, L2_attn_Wq, L2_attn_Wk, L2_attn_Wv, L2_attn_pre_proj, L2_attn_post_proj, L2_attn_mem_k, L2_attn_mem_v, L2_attn_Wout, L2_attn_bout, L2_xattn_w_q, L2_xattn_b_q, L2_xattn_w_k, L2_xattn_b_k, L2_xattn_w_v, L2_xattn_b_v, L2_xattn_w_o, L2_xattn_b_o, L2_ffn_wr, L2_ffn_br, L2_ffn_w1, L2_ffn_b1, L2_ffn_w2, L2_ffn_b2, L3_attn_Wq, L3_attn_bq, L3_attn_Wk, L3_attn_bk, L3_attn_Wv, L3_attn_bv, L3_attn_Wo, L3_attn_bo, L3_attn_prior_lambda, L3_xattn_Wq, L3_xattn_Wk, L3_xattn_Wv, L3_xattn_Wo, L3_xattn_bo, L3_ffn_router_w, L3_ffn_experts_bias, L3_ffn_w1, L3_ffn_w3, L3_ffn_w2, L3_ffn_sw1, L3_ffn_sw3, L3_ffn_sw2):
    import jax
    import jax.numpy as jnp

    def _L0_attn_ref(x, Wq, Wk, Wv, Wo):
        import jax, jax.numpy as jnp
        import numpy as np
        D_MODEL = 128
        NUM_HEADS = 16
        HEAD_DIM = D_MODEL // NUM_HEADS
        THETA = 10000.0
        B, S = (2, 256)

        def _apply_rope(t, cos, sin):
            te = t[..., 0::2]
            to = t[..., 1::2]
            re = te * cos - to * sin
            ro = te * sin + to * cos
            out = jnp.stack([re, ro], axis=-1)
            return out.reshape(t.shape)
        Bv, Sv, _ = x.shape

        def proj(W):
            return jnp.einsum('bsd,ed->bse', x, W).reshape(Bv, Sv, NUM_HEADS, HEAD_DIM).transpose(0, 2, 1, 3)
        q, k, v = (proj(Wq), proj(Wk), proj(Wv))
        pos = jnp.arange(Sv, dtype=jnp.float32)
        inv_freq = THETA ** (-jnp.arange(0, HEAD_DIM, 2, dtype=jnp.float32) / HEAD_DIM)
        ang = pos[:, None] * inv_freq[None, :]
        cos, sin = (jnp.cos(ang), jnp.sin(ang))
        q = _apply_rope(q, cos, sin)
        k = _apply_rope(k, cos, sin)
        scale = 1.0 / jnp.sqrt(jnp.float32(HEAD_DIM))
        scores = jnp.einsum('bhqd,bhkd->bhqk', q.astype(jnp.float32), k.astype(jnp.float32)) * scale
        causal = jnp.tril(jnp.ones((Sv, Sv), dtype=bool))
        scores = jnp.where(causal[None, None], scores, -jnp.inf)
        attn = jax.nn.softmax(scores, axis=-1)
        out = jnp.einsum('bhqk,bhkd->bhqd', attn, v.astype(jnp.float32))
        out = out.transpose(0, 2, 1, 3).reshape(Bv, Sv, D_MODEL)
        return jnp.einsum('bsd,ed->bse', out, Wo)

    def _L0_xattn_ref(query, key, value, Wq, bq, Wk, bk, Wv, bv, Wo, bo):
        import jax, jax.numpy as jnp
        import numpy as np
        HIDDEN = 128
        HEADS = 16
        HEAD_DIM = HIDDEN // HEADS
        B = query.shape[0]
        scale = jnp.sqrt(jnp.asarray(HEAD_DIM, query.dtype))
        Q = query @ Wq.T + bq
        K = key @ Wk.T + bk
        V = value @ Wv.T + bv

        def split(x):
            return x.reshape(B, -1, HEADS, HEAD_DIM).transpose(0, 2, 1, 3)
        Qh, Kh, Vh = (split(Q), split(K), split(V))
        energy = jnp.einsum('bhqd,bhkd->bhqk', Qh, Kh) / scale
        attn = jax.nn.softmax(energy, axis=-1)
        x = jnp.einsum('bhqk,bhkd->bhqd', attn, Vh)
        x = x.transpose(0, 2, 1, 3).reshape(B, -1, HIDDEN)
        return x @ Wo.T + bo

    def _L0_ffn_ref(hidden_states, gate_w, w1, w2, w3):
        import jax, jax.numpy as jnp
        import numpy as np
        E, K, D, H = (8, 2, 128, 256)
        B, S = (1, 128)

        def _grouped_swiglu(x_sorted, counts, w1, w2, w3):
            if hasattr(jax.lax, 'ragged_dot'):
                gs = counts.astype(jnp.int32)
                h = jax.nn.silu(jax.lax.ragged_dot(x_sorted, w1, gs)) * jax.lax.ragged_dot(x_sorted, w3, gs)
                return jax.lax.ragged_dot(h, w2, gs)
            pos = jnp.arange(x_sorted.shape[0])
            eid = jnp.searchsorted(jnp.cumsum(counts), pos, side='right')
            out = jnp.zeros((x_sorted.shape[0], w2.shape[-1]), x_sorted.dtype)
            for e in range(w1.shape[0]):
                xm = jnp.where((eid == e)[:, None], x_sorted, 0.0)
                he = jax.nn.silu(xm @ w1[e]) * (xm @ w3[e])
                out = out + he @ w2[e]
            return out
        x = hidden_states.reshape(-1, D)
        N = x.shape[0]
        scores = jax.nn.softmax(x @ gate_w.T, axis=-1)
        top_scores, sel = jax.lax.top_k(scores, K)
        sel_flat = sel.T.reshape(-1)
        scores_flat = top_scores.T.reshape(-1)
        order = jnp.argsort(sel_flat, stable=True)
        tok_sorted = order % N
        scores_sorted = scores_flat[order]
        counts = jnp.bincount(sel_flat, length=E)
        x_sorted = x[tok_sorted]
        y = _grouped_swiglu(x_sorted, counts, w1, w2, w3)
        weighted = y * scores_sorted[:, None]
        out = jnp.zeros((N, D), x.dtype).at[tok_sorted].add(weighted)
        return out.reshape(hidden_states.shape)

    def _L1_attn_ref(x, Wq, Wk, Wv, Wo, bo, proj):
        import jax, jax.numpy as jnp
        import numpy as np
        import math
        EPS = 1e-06

        def favorplus_features(x, proj):
            xw = jnp.einsum('bhtd,hmd->bhtm', x, proj)
            xw = xw - jnp.max(xw, axis=-1, keepdims=True)
            x_norm_sq = jnp.sum(x * x, axis=-1, keepdims=True)
            return jnp.exp(xw) * jnp.exp(-0.5 * x_norm_sq) + EPS
        B, T, d = x.shape
        h, m, dk = proj.shape

        def heads(W):
            y = jnp.einsum('btd,ed->bte', x, W)
            return y.reshape(B, T, h, dk).transpose(0, 2, 1, 3)
        Q = heads(Wq) / math.sqrt(dk)
        K = heads(Wk) / math.sqrt(dk)
        V = heads(Wv)
        inv_sqrt_m = 1.0 / math.sqrt(m)
        phiQ = favorplus_features(Q, proj) * inv_sqrt_m
        phiK = favorplus_features(K, proj) * inv_sqrt_m
        KV = jnp.einsum('bhtm,bhtd->bhmd', phiK, V)
        Ksum = jnp.sum(phiK, axis=2)
        num = jnp.einsum('bhtm,bhmd->bhtd', phiQ, KV)
        den = jnp.einsum('bhtm,bhm->bht', phiQ, Ksum)[..., None] + EPS
        out_heads = num / den
        merged = out_heads.transpose(0, 2, 1, 3).reshape(B, T, d)
        return jnp.einsum('btd,ed->bte', merged, Wo) + bo

    def _L1_xattn_ref(x, context, ln_gamma, ln_beta, w_q, w_kv, w_out, b_out, gate):
        import jax, jax.numpy as jnp
        import numpy as np
        DIM = 128
        NUM_HEADS = 16
        DIM_HEAD = 64
        INNER = NUM_HEADS * DIM_HEAD
        SCALE = DIM_HEAD ** (-0.5)

        def _layernorm(x, gamma, beta, eps=1e-05):
            mu = jnp.mean(x, axis=-1, keepdims=True)
            var = jnp.mean(jnp.square(x - mu), axis=-1, keepdims=True)
            return (x - mu) * jax.lax.rsqrt(var + eps) * gamma + beta
        B, SQ, _ = x.shape
        SK = context.shape[1]
        xn = _layernorm(x, ln_gamma, ln_beta)
        q = (xn @ w_q).reshape(B, SQ, NUM_HEADS, DIM_HEAD)
        kv = context @ w_kv
        k, v = jnp.split(kv, 2, axis=-1)
        k = k.reshape(B, SK, NUM_HEADS, DIM_HEAD)
        v = v.reshape(B, SK, NUM_HEADS, DIM_HEAD)
        scores = jnp.einsum('bqhd,bkhd->bhqk', q * SCALE, k)
        attn = jax.nn.softmax(scores, axis=-1)
        out = jnp.einsum('bhqk,bkhd->bqhd', attn, v).reshape(B, SQ, INNER)
        out = out @ w_out + b_out
        return out * jnp.tanh(gate[0])

    def _L1_ffn_ref(x, scores, expert_weights, expert_indices, w1, w2, bias):
        import jax, jax.numpy as jnp
        import numpy as np
        SL, BS, HS, FF, E, TOPK = (256, 2, 128, 512, 8, 2)
        sl, bs, hs = x.shape
        n_exp = w1.shape[0]
        top_k = expert_indices.shape[-1]
        xf = x.reshape(-1, hs)
        flat_idx = expert_indices.reshape(-1)
        flat_w = expert_weights.reshape(-1)
        order = jnp.argsort(flat_idx)
        tok = order // top_k
        tokens_per_expert = jnp.bincount(flat_idx, length=n_exp).astype(jnp.int32)
        xs = xf[tok]
        h = jax.nn.gelu(jax.lax.ragged_dot(xs, w1, tokens_per_expert), approximate=False)
        ys = jax.lax.ragged_dot(h, w2, tokens_per_expert)
        ys = ys * flat_w[order][:, None]
        out = jnp.zeros_like(xf).at[tok].add(ys)
        return out.reshape(sl, bs, hs) + bias

    def _L2_attn_ref(x, Wq, Wk, Wv, pre_proj, post_proj, mem_k, mem_v, Wout, bout):
        import jax, jax.numpy as jnp
        import numpy as np
        B, N, DIM = (4, 128, 128)
        H, DH = (16, 64)
        NUM_MEM = 64
        TOPK = 64
        SCALE = DH ** (-0.5)

        def _split_heads(t):
            b, n, _ = t.shape
            return t.reshape(b, n, H, DH).transpose(0, 2, 1, 3)
        b, n, _ = x.shape
        q = _split_heads(x @ Wq.T)
        k = _split_heads(x @ Wk.T)
        v = _split_heads(x @ Wv.T)
        mk = jnp.broadcast_to(mem_k[None], (b, H, NUM_MEM, DH))
        mv = jnp.broadcast_to(mem_v[None], (b, H, NUM_MEM, DH))
        k = jnp.concatenate([mk, k], axis=2)
        v = jnp.concatenate([mv, v], axis=2)
        j_len = n + NUM_MEM
        dots = jnp.einsum('bhid,bhjd->bhij', q, k) * SCALE
        dots = jnp.einsum('bhij,hk->bkij', dots, pre_proj)
        mask_value = -jnp.finfo(dots.dtype).max
        offset = j_len - n
        i_idx = jnp.arange(n)[:, None]
        j_idx = jnp.arange(j_len)[None, :]
        causal = j_idx > i_idx + offset
        dots = jnp.where(causal[None, None], mask_value, dots)
        kth = jax.lax.top_k(dots, TOPK)[0][..., -1:]
        dots = jnp.where(dots < kth, mask_value, dots)
        attn = jax.nn.softmax(dots, axis=-1)
        attn = jnp.einsum('bhij,hk->bkij', attn, post_proj)
        out = jnp.einsum('bhij,bhjd->bhid', attn, v)
        out = out.transpose(0, 2, 1, 3).reshape(b, n, H * DH)
        return out @ Wout.T + bout

    def _L2_xattn_ref(query, key_, value, w_q, b_q, w_k, b_k, w_v, b_v, w_o, b_o):
        import jax, jax.numpy as jnp
        import numpy as np
        D_MODEL = 128
        NUM_HEADS = 16
        D_K = D_MODEL // NUM_HEADS
        B, S = (4, 256)

        def _split_heads(x):
            b, s, _ = x.shape
            return x.reshape(b, s, NUM_HEADS, D_K).transpose(0, 2, 1, 3)
        Q = _split_heads(query @ w_q.T + b_q)
        K = _split_heads(key_ @ w_k.T + b_k)
        V = _split_heads(value @ w_v.T + b_v)
        scores = jnp.einsum('bhqd,bhkd->bhqk', Q, K) / jnp.sqrt(jnp.float32(D_K))
        probs = jax.nn.softmax(scores, axis=-1)
        attn = jnp.einsum('bhqk,bhkd->bhqd', probs, V)
        attn = attn.transpose(0, 2, 1, 3).reshape(query.shape[0], query.shape[1], D_MODEL)
        return attn @ w_o.T + b_o

    def _L2_ffn_ref(x, wr, br, w1, b1, w2, b2):
        import jax, jax.numpy as jnp
        import numpy as np
        B, S, H, F, E = (4, 256, 128, 512, 8)
        scores = jnp.einsum('bsh,he->bse', x, wr) + br
        expert_id = jnp.argmax(scores, axis=-1)
        h = jnp.einsum('bsh,ehf->ebsf', x, w1) + b1[:, None, None, :]
        h = jax.nn.gelu(h, approximate=False)
        y = jnp.einsum('ebsf,efh->ebsh', h, w2) + b2[:, None, None, :]
        one_hot = jax.nn.one_hot(expert_id, E, dtype=x.dtype)
        out = jnp.einsum('ebsh,bse->bsh', y, one_hot)
        return out

    def _L3_attn_ref(x, Wq, bq, Wk, bk, Wv, bv, Wo, bo, prior_lambda):
        import jax, jax.numpy as jnp
        import numpy as np
        import math
        D_MODEL = 128
        NUM_HEADS = 16
        B, L = (2, 256)
        PERIODS = (1.0, 30.0)
        WEIGHTS = (0.8, 0.4)
        SIGMAS = (0.5, 2.0)

        def _gaussian_mask(length):
            idx = jnp.arange(length, dtype=jnp.float32)
            delta = jnp.abs(idx[:, None] - idx[None, :])
            mask = jnp.zeros_like(delta)
            for p, w, sigma in zip(PERIODS, WEIGHTS, SIGMAS):
                if p < 0.2:
                    continue
                mask = mask + w * jnp.exp(-(delta - p) ** 2 / (2.0 * sigma ** 2))
            return mask
        Bx, Lx, D = x.shape
        H = NUM_HEADS
        hd = D // H

        def split_heads(t):
            return t.reshape(Bx, Lx, H, hd).transpose(0, 2, 1, 3)
        Q = split_heads(x @ Wq.T + bq)
        K = split_heads(x @ Wk.T + bk)
        V = split_heads(x @ Wv.T + bv)
        scores = jnp.einsum('bhqd,bhkd->bhqk', Q, K) / math.sqrt(hd)
        scores = scores + prior_lambda * _gaussian_mask(Lx)[None, None, :, :]
        attn = jax.nn.softmax(scores, axis=-1)
        out = jnp.einsum('bhqk,bhkd->bhqd', attn, V)
        out = out.transpose(0, 2, 1, 3).reshape(Bx, Lx, D)
        return out @ Wo.T + bo

    def _L3_xattn_ref(x, context, Wq, Wk, Wv, Wo, bo):
        import jax, jax.numpy as jnp
        import numpy as np
        EMB = 128
        HEADS = 16
        HEAD_DIM = EMB // HEADS
        B, Qlen, _ = x.shape
        KVlen = context.shape[1]
        scale = jnp.asarray(HEAD_DIM ** 0.5, x.dtype)
        q = (x @ Wq.T).reshape(B, Qlen, HEADS, HEAD_DIM).transpose(0, 2, 1, 3)
        k = (context @ Wk.T).reshape(B, KVlen, HEADS, HEAD_DIM).transpose(0, 2, 1, 3)
        v = (context @ Wv.T).reshape(B, KVlen, HEADS, HEAD_DIM).transpose(0, 2, 1, 3)
        scores = jnp.einsum('bhqd,bhkd->bhqk', q, k) / scale
        attn = jax.nn.softmax(scores, axis=-1)
        out = jnp.einsum('bhqk,bhkd->bhqd', attn, v)
        out = out.transpose(0, 2, 1, 3).reshape(B, Qlen, EMB)
        return out @ Wo.T + bo

    def _L3_ffn_ref(x, router_w, experts_bias, w1, w3, w2, sw1, sw3, sw2):
        import jax, jax.numpy as jnp
        import numpy as np
        D, H, E, K, S = (128, 256, 8, 2, 1)
        B, L = (4, 256)
        b, l, d = x.shape
        xf = x.reshape(-1, d)
        sg = jnp.einsum('td,sdh->tsh', xf, sw1)
        su = jnp.einsum('td,sdh->tsh', xf, sw3)
        shared_out = jnp.einsum('tsh,shd->td', jax.nn.silu(sg) * su, sw2)
        logits = xf @ router_w.T + experts_bias
        rw, sel = jax.lax.top_k(logits, K)
        rw = jax.nn.softmax(rw.astype(jnp.float32), axis=-1).astype(x.dtype)
        cw = (jax.nn.one_hot(sel, E, dtype=x.dtype) * rw[..., None]).sum(axis=1)
        g = jnp.einsum('td,edh->teh', xf, w1)
        u = jnp.einsum('td,edh->teh', xf, w3)
        eo = jax.nn.silu(g) * u
        moe_out = jnp.einsum('te,teh,ehd->td', cw, eo, w2)
        return (moe_out + shared_out).reshape(b, l, d)
    x = x + _L0_attn_ref(_layernorm(x, axis=-1), L0_attn_Wq, L0_attn_Wk, L0_attn_Wv, L0_attn_Wo)
    x = x + _L0_xattn_ref(_layernorm(x, axis=-1), ctx_1024, ctx_1024, L0_xattn_Wq, L0_xattn_bq, L0_xattn_Wk, L0_xattn_bk, L0_xattn_Wv, L0_xattn_bv, L0_xattn_Wo, L0_xattn_bo)
    x = x + _L0_ffn_ref(_layernorm(x, axis=-1), L0_ffn_gate_w, L0_ffn_w1, L0_ffn_w2, L0_ffn_w3)
    x = x + _L1_attn_ref(_layernorm(x, axis=-1), L1_attn_Wq, L1_attn_Wk, L1_attn_Wv, L1_attn_Wo, L1_attn_bo, L1_attn_proj)
    x = x + _L1_xattn_ref(_layernorm(x, axis=-1), ctx_1024, L1_xattn_ln_gamma, L1_xattn_ln_beta, L1_xattn_w_q, L1_xattn_w_kv, L1_xattn_w_out, L1_xattn_b_out, L1_xattn_gate)
    x = x + _L1_ffn_ref(_layernorm(x, axis=-1), L1_ffn_scores, L1_ffn_expert_weights, L1_ffn_expert_indices, L1_ffn_w1, L1_ffn_w2, L1_ffn_bias)
    x = x + _L2_attn_ref(_layernorm(x, axis=-1), L2_attn_Wq, L2_attn_Wk, L2_attn_Wv, L2_attn_pre_proj, L2_attn_post_proj, L2_attn_mem_k, L2_attn_mem_v, L2_attn_Wout, L2_attn_bout)
    x = x + _L2_xattn_ref(_layernorm(x, axis=-1), ctx_1024, ctx_1024, L2_xattn_w_q, L2_xattn_b_q, L2_xattn_w_k, L2_xattn_b_k, L2_xattn_w_v, L2_xattn_b_v, L2_xattn_w_o, L2_xattn_b_o)
    x = x + _L2_ffn_ref(_layernorm(x, axis=-1), L2_ffn_wr, L2_ffn_br, L2_ffn_w1, L2_ffn_b1, L2_ffn_w2, L2_ffn_b2)
    x = x + _L3_attn_ref(_layernorm(x, axis=-1), L3_attn_Wq, L3_attn_bq, L3_attn_Wk, L3_attn_bk, L3_attn_Wv, L3_attn_bv, L3_attn_Wo, L3_attn_bo, L3_attn_prior_lambda)
    x = x + _L3_xattn_ref(_layernorm(x, axis=-1), ctx_1024, L3_xattn_Wq, L3_xattn_Wk, L3_xattn_Wv, L3_xattn_Wo, L3_xattn_bo)
    x = x + _L3_ffn_ref(_layernorm(x, axis=-1), L3_ffn_router_w, L3_ffn_experts_bias, L3_ffn_w1, L3_ffn_w3, L3_ffn_w2, L3_ffn_sw1, L3_ffn_sw3, L3_ffn_sw2)
    return x

_drawn_inputs = setup_inputs


def setup_inputs(seed=0):
    import zlib

    import numpy as np

    out = dict(_drawn_inputs(seed))
    spreads = {'L0_xattn_bq': (0.0, 0.8),
     'L0_xattn_bk': (0.0, 0.8),
     'L0_xattn_bv': (0.0, 0.1),
     'L0_xattn_bo': (0.0, 0.1),
     'L1_attn_bo': (0.0, 0.1),
     'L1_xattn_ln_gamma': (1.0, 0.537),
     'L1_xattn_ln_beta': (0.0, 0.442),
     'L1_xattn_b_out': (0.0, 0.1),
     'L1_ffn_bias': (0.0, 0.1),
     'L2_attn_bout': (0.0, 0.1),
     'L2_xattn_b_q': (0.0, 0.292),
     'L2_xattn_b_k': (0.0, 0.8),
     'L2_xattn_b_v': (0.0, 0.1),
     'L2_xattn_b_o': (0.0, 0.1),
     'L3_ffn_experts_bias': (0.0, 0.8)}
    factors = {'L0_xattn_Wq': 8.0,
     'L0_xattn_Wk': 8.0,
     'L2_attn_Wq': 2.88,
     'L2_attn_Wk': 4.245,
     'L2_attn_Wv': 3.049,
     'L2_attn_pre_proj': 2.825,
     'L2_attn_mem_k': 2.897,
     'L2_ffn_b1': 4.638,
     'L2_ffn_b2': 3.342,
     'L3_attn_bq': 8.0,
     'L3_attn_bk': 8.0,
     'L3_attn_bv': 8.0,
     'L3_attn_bo': 8.0,
     'L3_xattn_bo': 8.0,
     'L3_ffn_router_w': 8.0,
     'L3_ffn_w1': 8.0,
     'L3_ffn_w3': 8.0,
     'L3_ffn_w2': 8.0,
     'L3_ffn_sw1': 8.0,
     'L3_ffn_sw3': 8.0,
     'L3_ffn_sw2': 8.0}
    for name, (base, spread) in spreads.items():
        noise = np.random.default_rng([zlib.crc32(name.encode()), seed]).standard_normal(out[name].shape)
        drawn = base * np.exp(spread * noise) if base else spread * noise
        out[name] = jnp.asarray(drawn.astype(out[name].dtype))
    for name, factor in factors.items():
        out[name] = (out[name] * factor).astype(out[name].dtype)
    return out
```

```python
from contextlib import ExitStack

import numpy as np
import concourse.bass as bass
from concourse import mybir

F32 = mybir.dt.float32
I32 = mybir.dt.int32
ALU = mybir.AluOpType
ACT = mybir.ActivationFunctionType
AX = mybir.AxisListType.X

P = 128
D = 128
B = 4
S = 512
NT = S // P
NH = 16
SC = 77
E = 8
BANK = 512
BIG = 3.0e38
SUBLAYERS = range(12)
FIRST_SEM = 200


def columns(*pieces):
    at, out = 0, {}
    for name, n in pieces:
        out[name] = (at, n)
        at += n
    return out, at


CONST, NCONST = columns(("ident", P), ("head8", NH), ("head64", NH), ("expert_no", E), ("minus_half", NT), ("later", 8))
ROPE, NROPE = columns(("cos", S), ("sin", S), ("swap", P), ("causal", NT * S))
PRIOR, NPRIOR = columns(("gauss", NT * S), ("lam", 1))
ATT8, NATT8 = columns(("wq", D), ("wk", D), ("wv", D), ("wo", D), ("bq", 1), ("bk", 1), ("bv", 1))
FAVOR, NFAVOR = columns(("wq", D), ("wk", D), ("wv", D), ("wo", D), ("proj", 32), ("blk", D * 4), ("blkh", NH * 4))
ATT64, NATT64 = columns(("wq", 1024), ("wk", 1024), ("wv", 1024), ("wo", 1024), ("bq", 8), ("bk", 8),
                        ("gamma", D), ("beta", D), ("gate", 1))
TALK, NTALK = columns(("wq", 1024), ("wk", 1024), ("wv", 1024), ("wo", 1024), ("memk", 512), ("memv", 1024),
                      ("pre", P), ("post", P))
FF0, NFF0 = columns(("w1", E * 256), ("w3", E * 256), ("w2", E * 256), ("router", E))
FF1, NFF1 = columns(("w1", E * 512), ("w2", E * 512), ("weights", NT * 2))
FF2, NFF2 = columns(("w1", E * 512), ("w2", E * 512), ("router", E), ("b1", E * 4))
FF3, NFF3 = columns(("w1", 9 * 256), ("w3", 9 * 256), ("w2", 9 * 256), ("router", E))
SELF_ROPE = {**ATT8, **{k: (c + NATT8, n) for k, (c, n) in ROPE.items()}}
SELF_PRIOR = {**ATT8, **{k: (c + NATT8, n) for k, (c, n) in PRIOR.items()}}
ARENA = max(NATT8 + NROPE, NATT8 + NPRIOR, NFAVOR, NATT64, NTALK, NFF0, NFF1, NFF2, NFF3)
ROWS, NROWS = columns(("zero", D), ("x0_bv", D), ("x0_bo", D), ("a1_bo", D), ("x1_bo", D), ("f1_b", D), ("a2_bo", D),
                      ("x2_bv", D), ("x2_bo", D), ("f2_br", E), ("f2_b2", E * D), ("a3_bv", D), ("a3_bo", D),
                      ("x3_bo", D), ("f3_br", E), ("x1_bv", 1024))
WIDTHS = [NATT8 + NROPE, NATT8, NFF0, NFAVOR, NATT64, NFF1, NTALK, NATT8, NFF2, NATT8 + NPRIOR, NATT8, NFF3]


class Core:

    def row(self, name, at=0, n=None):
        c, w = ROWS[name]
        return self.rows[0:1, c + at:c + at + (w if n is None else n)]

    def const(self, name):
        c, w = CONST[name]
        return self.consts[:, c:c + w]


class Chain:

    def __init__(self, engine, sem):
        self.engine, self.sem, self.n = engine, sem, 0

    def done(self, ins):
        ins.then_inc(self.sem, 1)
        self.n += 1

    def wait(self):
        self.engine.wait_ge(self.sem, self.n)


class Step:

    def __init__(self, core, ctx, index, pieces, at=0):
        self.core, self.nc, self.ctx, self.index = core, core.nc, ctx, index
        self.w = core.arena[index % 2]
        self.pieces = pieces
        self.sems = []

    def piece(self, name):
        c, w = self.pieces[name]
        return self.w[:, c:c + w]

    def sb(self, name, shape, dt=F32):
        return self.ctx.enter_context(self.nc.sbuf_tensor(f"{name}_{self.index}", shape, dt))

    def ps(self, name, shape):
        return self.ctx.enter_context(self.nc.psum_tensor(f"{name}_{self.index}", shape, F32))

    def sem(self, name):
        s = self.ctx.enter_context(self.nc.semaphore(f"{name}_{self.index}", num=FIRST_SEM + len(self.sems)))
        self.sems.append(s)
        return s

    def end_pass(self):
        nums = sorted(s.num for s in self.sems)
        assert nums == list(range(nums[0], nums[-1] + 1)), nums
        self.nc.all_engine_barrier(sems_to_clear=range(nums[0], nums[-1] + 1))


def begin(core, index, step):
    nc = core.nc
    with nc.Block() as block:

        @block.sync
        def _(sp):
            k = core.order.index(index)
            if k + 1 < len(core.order):
                nxt = core.order[k + 1]
                sp.dma_start(core.arena[nxt % 2][:, 0:WIDTHS[nxt]], core.packed[nxt]).then_inc(core.arrived[nxt % 2], 16)
            sp.wait_ge(core.arrived[index % 2], 16 * (k // 2 + 1))


class Norm:

    def __init__(self, st, affine=False):
        self.st, self.affine = st, affine
        self.stats = st.sb("ln_stats", [P, 2, NT, 6])
        self.mv = st.sb("ln_mv", [P, 2, NT, 2])
        self.var = st.sb("ln_var", [P, 2, NT])
        self.rstd = st.sb("ln_rstd", [P, 2, NT])
        self.xn = st.sb("xn", [P, NT, D])
        self.xnT = st.sb("xnT", [P, S])
        self.var_ready = st.sem("ln_var_ready")
        self.rstd_ready = st.sem("ln_rstd_ready")
        self.norm_ready = st.sem("ln_norm_ready")
        self.turned = st.sem("ln_turned")
        self.xnT_ready = st.sem("xnT_ready")

    def vector(self, dve, chain, b):
        core = self.st.core
        x = core.X[:, b]
        rounds = 2 if self.affine else 1
        for r in range(rounds):
            src = x if r == 0 else self.xn
            for t in range(NT):
                chain.done(dve.bn_stats(self.stats[:, r, t, :], src[:, t, :]))
            chain.wait()
            for t in range(NT):
                chain.done(dve.bn_aggr(self.mv[:, r, t, :], self.stats[:, r, t, :]))
            chain.wait()
            dve.tensor_scalar(self.var[:, r, :], self.mv[:, r, :, 1], 1e-5, None, ALU.add).then_inc(self.var_ready, 1)
            dve.wait_ge(self.rstd_ready, r + 1)
            last = r == rounds - 1
            for t in range(NT):
                ins = dve.tensor_scalar(self.xn[:, t, :], src[:, t, :], self.mv[:, r, t, 0:1], self.rstd[:, r, t:t + 1],
                                        ALU.subtract, ALU.mult)
                if last and not self.affine:
                    ins.then_inc(self.norm_ready, 1)
                else:
                    chain.done(ins)
            if not last:
                chain.wait()
        if self.affine:
            gamma, beta = self.st.piece("gamma"), self.st.piece("beta")
            chain.wait()
            for t in range(NT):
                chain.done(dve.tensor_tensor(self.xn[:, t, :], self.xn[:, t, :], gamma, ALU.mult))
            chain.wait()
            for t in range(NT):
                dve.tensor_tensor(self.xn[:, t, :], self.xn[:, t, :], beta, ALU.add).then_inc(self.norm_ready, 1)

    def gpsimd(self, pool):
        for r in range(2 if self.affine else 1):
            pool.wait_ge(self.var_ready, r + 1)
            pool.tensor_tensor(self.rstd[:, r, :], self.var[:, r, :], self.st.core.const("minus_half"),
                               ALU.pow).then_inc(self.rstd_ready, 1)

    def tensor(self, pe, bank):
        for t in range(NT):
            pe.wait_ge(self.norm_ready, t + 1)
            ins = pe.transpose(bank[:, t * P:(t + 1) * P], self.xn[:, t, :], self.st.core.const("ident"))
        ins.then_inc(self.turned, 1)

    def scalar(self, act, bank):
        act.wait_ge(self.turned, 1)
        act.activation(self.xnT[:], bank[:, 0:S], ACT.Copy).then_inc(self.xnT_ready, 1)


def self_attention(core, index, pieces, rows, rope):
    nc = core.nc
    dh = 8
    scale = float(dh) ** -0.5
    NU = NH * NT
    width = [P * (t + 1) if rope else S for t in range(NT)]
    with ExitStack() as ctx:
        st = Step(core, ctx, index, pieces)
        norm = Norm(st)
        QT, KT, VT = st.sb("QT", [P, S]), st.sb("KT", [P, S]), st.sb("VT", [P, S])
        KM = st.sb("KM", [P, NH, S])
        Vt = st.sb("Vt", [P, NT, D])
        raw = st.sb("raw", [P, 2, S])
        rot = st.sb("rot", [P, 2, S])
        addend = st.sb("addend", [P, NT, S])
        sc = st.sb("sc", [P, 2, NT, S])
        pr = st.sb("pr", [P, 3, NT, S])
        PTs = st.sb("PTs", [P, 6, S])
        mx, nb = st.sb("mx", [P, NU]), st.sb("nb", [P, NU])
        den, rden = st.sb("den", [P, NH, NT]), st.sb("rden", [P, NH, NT])
        O, OT = st.sb("O", [P, NT, D]), st.sb("OT", [P, S])
        ps_s = st.ps("ps_s", [P, 3, BANK])
        ps_t = st.ps("ps_t", [P, 3, BANK])
        ps_o = st.ps("ps_o", [P, BANK])
        ps_m = st.ps("ps_m", [P, BANK])
        dve_done, act_done = st.sem("dve_done"), st.sem("act_done")
        qkv_made, qkv_kept, swapped = st.sem("qkv_made"), st.sem("qkv_kept"), st.sem("swapped")
        keys_ready = st.sem("keys_ready")
        scored, shifted, bias_ready = st.sem("scored"), st.sem("shifted"), st.sem("bias_ready")
        exped, turned, kept_a, kept_v, weighted = (st.sem(n) for n in ("exped", "turned", "kept_a", "kept_v", "weighted"))
        o_ready, o_turned, oT_ready, out_made, v_turned, v_ready = (st.sem(n) for n in (
            "o_ready", "o_turned", "oT_ready", "out_made", "v_turned", "v_ready"))
        ident = core.const("ident")
        begin(core, index, st)
        if rope:
            addend_v = st.piece("causal").rearrange("p (t s) -> p t s", t=NT)
        else:
            addend_v = addend
            with nc.Block() as block:

                @block.vector
                def _(dve):
                    gauss = st.piece("gauss").rearrange("p (t s) -> p t s", t=NT)
                    lam = st.piece("lam")
                    for t in range(NT):
                        dve.tensor_scalar(addend[:, t, :], gauss[:, t, :], lam, 1.0 / scale, ALU.mult, ALU.mult)

        with nc.Fori(0, B) as b:
            with nc.Block() as block:

                @block.gpsimd
                def _(pool):
                    norm.gpsimd(pool)

                @block.tensor
                def _(pe):
                    norm.tensor(pe, ps_m)
                    pe.wait_ge(norm.xnT_ready, 1)
                    for i, (name, bank) in enumerate((("wq", ps_s[:, 0, :]), ("wk", ps_s[:, 1, :]), ("wv", ps_s[:, 2, :]))):
                        pe.matmul(bank, st.piece(name), norm.xnT[:], start=True, stop=True).then_inc(qkv_made, 1)
                    if rope:
                        pe.wait_ge(qkv_kept, 2)
                        for i in range(2):
                            pe.matmul(ps_t[:, i, :], st.piece("swap"), raw[:, i, :], start=True, stop=True).then_inc(swapped, 1)
                    pe.wait_ge(qkv_kept, 3)
                    for t in range(NT):
                        ins = pe.transpose(ps_m[:, t * P:(t + 1) * P], VT[:, t * P:(t + 1) * P], ident)
                    ins.then_inc(v_turned, 1)
                    pe.wait_ge(v_ready, 1)
                    pe.wait_ge(keys_ready, NH + (1 if rope else 0))
                    for step in range(NU + 12):
                        if step < NU:
                            u = step
                            h, t = divmod(u, NT)
                            if u >= 3:
                                pe.wait_ge(shifted, u - 2)
                            pe.matmul(ps_s[:, u % 3, 0:width[t]], QT[:, t * P:(t + 1) * P], KM[:, h, 0:width[t]],
                                      start=True, stop=True).then_inc(scored, 1)
                        u = step - 8
                        if 0 <= u < NU:
                            h, t = divmod(u, NT)
                            pe.wait_ge(exped, u + 1)
                            if u >= 3:
                                v = u - 3
                                pe.wait_ge(kept_v if v % 2 else kept_a, v // 2 + 1)
                            for k in range(width[t] // P):
                                ins = pe.transpose(ps_t[:, u % 3, k * P:(k + 1) * P], pr[:, h % 3, t, k * P:(k + 1) * P], ident)
                            ins.then_inc(turned, 1)
                        u = step - 12
                        if u >= 0:
                            h, t = divmod(u, NT)
                            pe.wait_ge(kept_v if u % 2 else kept_a, u // 2 + 1)
                            n = width[t] // P
                            for k in range(n):
                                ins = pe.matmul(ps_o[:, t * D + h * dh:t * D + (h + 1) * dh], PTs[:, u % 6, k * P:(k + 1) * P],
                                                Vt[:, k, h * dh:(h + 1) * dh], start=(k == 0), stop=(k == n - 1))
                            ins.then_inc(weighted, 1)
                    pe.wait_ge(o_ready, 1)
                    for t in range(NT):
                        ins = pe.transpose(ps_m[:, t * P:(t + 1) * P], O[:, t, :], ident)
                    ins.then_inc(o_turned, 1)
                    pe.wait_ge(oT_ready, 1)
                    for t in range(NT):
                        pe.matmul(ps_s[:, 0, t * D:(t + 1) * D], OT[:, t * P:(t + 1) * P], st.piece("wo"), start=True, stop=False)
                        ins = pe.matmul(ps_s[:, 0, t * D:(t + 1) * D], core.ones[:, :], core.row(rows["bo"]), start=False, stop=True)
                    ins.then_inc(out_made, 1)

                @block.scalar
                def _(act):
                    norm.scalar(act, ps_m)
                    dest = (raw[:, 0, :], raw[:, 1, :]) if rope else (QT[:], KT[:])
                    for i in range(2):
                        act.wait_ge(qkv_made, i + 1)
                        act.activation(dest[i], ps_s[:, i, :], ACT.Identity, bias=st.piece(("bq", "bk")[i])).then_inc(qkv_kept, 1)
                    act.wait_ge(qkv_made, 3)
                    act.activation(VT[:], ps_s[:, 2, :], ACT.Identity, bias=st.piece("bv")).then_inc(qkv_kept, 1)
                    for h in range(NH + 2):
                        if h < NH:
                            act.wait_ge(bias_ready, h + 1)
                            if h >= 3:
                                act.wait_ge(turned, NT * (h - 2))
                            for t in range(NT):
                                u = h * NT + t
                                act.activation(pr[:, h % 3, t, 0:width[t]], sc[:, h % 2, t, 0:width[t]], ACT.Exp,
                                               bias=nb[:, u:u + 1], scale=scale,
                                               accum_out=den[:, h, t:t + 1]).then_inc(exped, 1)
                        if h >= 2:
                            for t in (0, 2):
                                u = (h - 2) * NT + t
                                act.wait_ge(turned, u + 1)
                                if u >= 6:
                                    act.wait_ge(weighted, u - 5)
                                act.activation(PTs[:, u % 6, 0:width[t]], ps_t[:, u % 3, 0:width[t]], ACT.Copy).then_inc(kept_a, 1)
                    act.wait_ge(o_turned, 1)
                    act.activation(OT[:], ps_m[:], ACT.Copy).then_inc(oT_ready, 1)

                @block.vector
                def _(dve):
                    chain = Chain(dve, dve_done)
                    norm.vector(dve, chain, b)
                    if rope:
                        dve.wait_ge(qkv_kept, 2)
                        for i in range(2):
                            chain.done(dve.tensor_tensor((QT, KT)[i][:], raw[:, i, :], st.piece("cos"), ALU.mult))
                            dve.wait_ge(swapped, i + 1)
                            chain.done(dve.tensor_tensor(rot[:, i, :], ps_t[:, i, :], st.piece("sin"), ALU.mult))
                        chain.wait()
                        dve.tensor_tensor(QT[:], QT[:], rot[:, 0, :], ALU.add).then_inc(keys_ready, 1)
                        chain.done(dve.tensor_tensor(KT[:], KT[:], rot[:, 1, :], ALU.add))
                        chain.wait()
                    else:
                        dve.wait_ge(qkv_kept, 2)
                    for h in range(NH):
                        dve.tensor_scalar(KM[:, h, :], KT[:], core.const("head8")[:, h:h + 1], None, ALU.mult).then_inc(keys_ready, 1)
                    dve.wait_ge(v_turned, 1)
                    dve.tensor_copy(Vt[:].rearrange("p t d -> p (t d)"), ps_m[:]).then_inc(v_ready, 1)
                    for h in range(NH + 2):
                        if h < NH:
                            if h >= 2:
                                dve.wait_ge(exped, NT * (h - 1))
                            for t in range(NT):
                                u = h * NT + t
                                dve.wait_ge(scored, u + 1)
                                dve.tensor_tensor_reduce(sc[:, h % 2, t, 0:width[t]], ps_s[:, u % 3, 0:width[t]],
                                                         addend_v[:, t, 0:width[t]], 1.0, -BIG, ALU.add, ALU.max,
                                                         mx[:, u:u + 1]).then_inc(shifted, 1)
                            dve.wait_ge(shifted, NT * (h + 1))
                            dve.tensor_scalar(nb[:, h * NT:(h + 1) * NT], mx[:, h * NT:(h + 1) * NT], -scale, None,
                                              ALU.mult).then_inc(bias_ready, 1)
                        if h >= 2:
                            for t in (1, 3):
                                u = (h - 2) * NT + t
                                dve.wait_ge(turned, u + 1)
                                if u >= 6:
                                    dve.wait_ge(weighted, u - 5)
                                dve.tensor_copy(PTs[:, u % 6, 0:width[t]], ps_t[:, u % 3, 0:width[t]]).then_inc(kept_v, 1)
                    dve.wait_ge(exped, NU)
                    chain.done(dve.reciprocal(rden[:].rearrange("p h t -> p (h t)"), den[:].rearrange("p h t -> p (h t)")))
                    chain.wait()
                    dve.wait_ge(weighted, NU)
                    ov = O[:].rearrange("p t (h d) -> p t h d", h=NH)
                    pv = ps_o[:].rearrange("p (t h d) -> p t h d", t=NT, h=NH)
                    for t in range(NT):
                        ins = dve.tensor_tensor(ov[:, t], pv[:, t], rden[:, :, t].unsqueeze(2).to_broadcast([P, NH, dh]), ALU.mult)
                    ins.then_inc(o_ready, 1)
                    dve.wait_ge(out_made, 1)
                    dve.tensor_tensor(core.X[:, b].rearrange("p t d -> p (t d)"), ps_s[:, 0, :],
                                      core.X[:, b].rearrange("p t d -> p (t d)"), ALU.add)

            st.end_pass()


def cross_attention(core, index, pieces, rows, dh):
    nc = core.nc
    NJ = NH * dh // P
    scale = float(dh) ** -0.5
    wide = dh == 64
    G = 4
    head_mask = "head64" if wide else "head8"
    with ExitStack() as ctx:
        st = Step(core, ctx, index, pieces)
        norm = Norm(st, affine=wide)
        cT = st.sb("cT", [P, SC])
        QT = st.sb("QT", [P, NJ, S])
        KM = st.sb("KM", [P, NH, SC])
        V = st.sb("V", [SC, NJ * P])
        sc = st.sb("sc", [P, 2, NH, SC])
        pr = st.sb("pr", [P, 2, NH, SC])
        PTs = st.sb("PTs", [SC, 2, NH, P])
        mx, den, rden = st.sb("mx", [P, NT, NH]), st.sb("den", [P, NT, NH]), st.sb("rden", [P, NT, NH])
        O, OT = st.sb("O", [P, 2, NJ * P]), st.sb("OT", [P, 2, NJ, P])
        gate = st.sb("gate", [P, 1])
        ps_s = st.ps("ps_s", [P, 4, BANK])
        ps_t = st.ps("ps_t", [P, 2, BANK])
        ps_o = st.ps("ps_o", [P, 2, BANK])
        dve_done = st.sem("dve_done")
        ctx_ready, q_made, q_kept, k_made, k_kept, v_made, v_kept = (st.sem(n) for n in (
            "ctx_ready", "q_made", "q_kept", "k_made", "k_kept", "v_made", "v_kept"))
        scored, shifted, exped, summed, turned, kept = (st.sem(n) for n in (
            "scored", "shifted", "exped", "summed", "turned", "kept"))
        weighted, o_ready, o_turned, oT_ready, out_made, added = (st.sem(n) for n in (
            "weighted", "o_ready", "o_turned", "oT_ready", "out_made", "added"))
        ident = core.const("ident")
        begin(core, index, st)
        if wide:
            with nc.Block() as block:

                @block.scalar
                def _(act):
                    act.activation(gate[:], st.piece("gate"), ACT.Tanh)

        def weight(name, j):
            c, _ = pieces[name]
            return st.w[:, c + j * P:c + (j + 1) * P]

        NO = max(1, NJ // 4)
        with nc.Fori(0, B) as b:
            with nc.Block() as block:

                @block.gpsimd
                def _(pool):
                    norm.gpsimd(pool)

                @block.tensor
                def _(pe):
                    pe.wait_ge(ctx_ready, 1)
                    for j in range(NJ):
                        if j >= 2:
                            pe.wait_ge(k_kept, (j - 1) * (NH // NJ))
                        pe.matmul(ps_o[:, j % 2, 0:SC], weight("wk", j), cT[:], start=True, stop=True).then_inc(k_made, 1)
                    n = min(BANK, NJ * P)
                    c, _ = pieces["wv"]
                    for j in range(NJ * P // n):
                        pe.matmul(ps_s[0:SC, j, 0:n], cT[:], st.w[:, c + j * n:c + (j + 1) * n], start=True, stop=False)
                        pe.matmul(ps_s[0:SC, j, 0:n], core.ones[:, 0:SC], core.row(rows["bv"], j * n, n),
                                  start=False, stop=True).then_inc(v_made, 1)
                    norm.tensor(pe, ps_t[:, 0, :])
                    pe.wait_ge(norm.xnT_ready, 1)
                    for j in range(NJ):
                        if j >= 2:
                            pe.wait_ge(q_kept, j - 1)
                        pe.matmul(ps_s[:, 2 + j % 2, :], weight("wq", j), norm.xnT[:], start=True, stop=True).then_inc(q_made, 1)
                    pe.wait_ge(k_kept, NH)
                    pe.wait_ge(v_kept, NJ * P // n)
                    pe.wait_ge(q_kept, NJ)

                    def scores(t):
                        if t >= 1:
                            pe.wait_ge(shifted, t)
                        for g in range(NH // G):
                            if wide:
                                for h in range(g * G, (g + 1) * G):
                                    ins = pe.matmul(ps_s[:, g, (h % G) * SC:(h % G + 1) * SC], QT[:, h // 2, t * P:(t + 1) * P],
                                                    KM[:, h, :], start=True, stop=True)
                            else:
                                ins = pe.matmul(ps_s[:, g, 0:G * SC], QT[:, 0, t * P:(t + 1) * P],
                                                KM[:, g * G:(g + 1) * G, :].rearrange("p h s -> p (h s)"), start=True, stop=True)
                        ins.then_inc(scored, 1)

                    def turn(t):
                        pe.wait_ge(exped, t + 1)
                        for g in range(NH // G):
                            i = t * 4 + g
                            if i >= 2:
                                pe.wait_ge(kept, i - 1)
                            for h in range(g * G, (g + 1) * G):
                                ins = pe.transpose(ps_t[0:SC, i % 2, (h % G) * P:(h % G + 1) * P], pr[:, t % 2, h, :], ident)
                            ins.then_inc(turned, 1)

                    def weigh(t):
                        pe.wait_ge(kept, 4 * (t + 1))
                        if t >= 1:
                            pe.wait_ge(o_ready, t)
                        for h in range(NH):
                            at = h * dh
                            ins = pe.matmul(ps_o[:, at // BANK, at % BANK:at % BANK + dh], PTs[:, t % 2, h, :],
                                            V[:, at:at + dh], start=True, stop=True)
                        ins.then_inc(weighted, 1)

                    def project(t):
                        pe.wait_ge(o_ready, t + 1)
                        if t >= 1:
                            pe.wait_ge(added, t)
                        pe.wait_ge(kept, min(4 * (t + 2), 4 * NT))
                        for g in range(NO):
                            for j in range(g * 4, min((g + 1) * 4, NJ)):
                                ins = pe.transpose(ps_t[:, g, (j % 4) * P:(j % 4 + 1) * P], O[:, t % 2, j * P:(j + 1) * P], ident)
                        ins.then_inc(o_turned, 1)
                        pe.wait_ge(oT_ready, t + 1)
                        for j in range(NJ):
                            pe.matmul(ps_t[:, 0, 0:D], OT[:, t % 2, j, :], weight("wo", j), start=(j == 0), stop=False)
                        pe.matmul(ps_t[:, 0, 0:D], core.ones[:, :], core.row(rows["bo"]), start=False, stop=True).then_inc(out_made, 1)

                    scores(0)
                    for t in range(NT + 1):
                        if t < NT:
                            if t >= 2:
                                pe.wait_ge(added, t - 1)
                            turn(t)
                            if t + 1 < NT:
                                scores(t + 1)
                            weigh(t)
                        if t >= 1:
                            if t < NT:
                                pe.wait_ge(kept, 4 * (t + 1))
                            project(t - 1)

                @block.scalar
                def _(act):
                    act.activation(cT[:], core.ctxT[:, b], ACT.Copy).then_inc(ctx_ready, 1)
                    n = min(BANK, NJ * P)
                    for j in range(NJ * P // n):
                        act.wait_ge(v_made, j + 1)
                        act.activation(V[:, j * n:(j + 1) * n], ps_s[0:SC, j, 0:n], ACT.Copy).then_inc(v_kept, 1)
                    norm.scalar(act, ps_t[:, 0, :])
                    for j in range(NJ):
                        act.wait_ge(q_made, j + 1)
                        act.activation(QT[:, j, :], ps_s[:, 2 + j % 2, :], ACT.Identity, bias=st.piece("bq")[:, j:j + 1]).then_inc(q_kept, 1)
                    for t in range(NT + 1):
                        if t < NT:
                            act.wait_ge(shifted, t + 1)
                            if t >= 2:
                                act.wait_ge(turned, 4 * (t - 1))
                                act.wait_ge(summed, t - 1)
                            act.activation(pr[:, t % 2], sc[:, t % 2], ACT.Exp, scale=scale).then_inc(exped, 1)
                            for g in range(NH // G):
                                act.wait_ge(turned, 4 * t + g + 1)
                                if t >= 2:
                                    act.wait_ge(weighted, t - 1)
                                act.activation(PTs[:, t % 2, g * G:(g + 1) * G, :].rearrange("p h s -> p (h s)"),
                                               ps_t[0:SC, (4 * t + g) % 2, :], ACT.Copy).then_inc(kept, 1)
                        if t >= 1:
                            act.wait_ge(o_turned, t)
                            for g in range(NO):
                                m = min(4, NJ)
                                ins = act.activation(OT[:, (t - 1) % 2, g * 4:g * 4 + m, :].rearrange("p j s -> p (j s)"),
                                                     ps_t[:, g, 0:m * P], ACT.Copy)
                            ins.then_inc(oT_ready, 1)

                @block.vector
                def _(dve):
                    chain = Chain(dve, dve_done)
                    for j in range(NJ):
                        dve.wait_ge(k_made, j + 1)
                        for h in range(j * (NH // NJ), (j + 1) * (NH // NJ)):
                            dve.tensor_scalar(KM[:, h, :], ps_o[:, j % 2, 0:SC], st.piece("bk")[:, j:j + 1],
                                              core.const(head_mask)[:, h:h + 1], ALU.add, ALU.mult).then_inc(k_kept, 1)
                    norm.vector(dve, chain, b)

                    def shift(t):
                        dve.wait_ge(scored, t + 1)
                        v = ps_s[:, :, 0:G * SC].rearrange("p g (h s) -> p g h s", h=G)
                        chain.done(dve.tensor_reduce(mx[:, t, :].rearrange("p (g h) -> p g h", g=NH // G), v, AX, ALU.max))
                        chain.wait()
                        if t >= 2:
                            dve.wait_ge(exped, t - 1)
                        top = mx[:, t, :].rearrange("p (g h) -> p g h", g=NH // G).unsqueeze(3).to_broadcast([P, NH // G, G, SC])
                        dve.tensor_tensor(sc[:, t % 2].rearrange("p (g h) s -> p g h s", g=NH // G), v, top,
                                          ALU.subtract).then_inc(shifted, 1)

                    def normalise(t):
                        dve.wait_ge(exped, t + 1)
                        dve.tensor_reduce(den[:, t, :], pr[:, t % 2], AX, ALU.add).then_inc(summed, 1)
                        dve.wait_ge(summed, t + 1)
                        chain.done(dve.reciprocal(rden[:, t, :], den[:, t, :]))
                        chain.wait()
                        dve.wait_ge(weighted, t + 1)
                        if t >= 2:
                            dve.wait_ge(o_turned, t - 1)
                        src = ps_o[:].rearrange("p c n -> p (c n)")[:, 0:NJ * P].rearrange("p (h d) -> p h d", h=NH)
                        dve.tensor_tensor(O[:, t % 2].rearrange("p (h d) -> p h d", h=NH), src,
                                          rden[:, t, :].unsqueeze(2).to_broadcast([P, NH, dh]), ALU.mult).then_inc(o_ready, 1)

                    shift(0)
                    for t in range(NT + 1):
                        if t + 1 < NT:
                            shift(t + 1)
                        if t < NT:
                            normalise(t)
                        if t >= 1:
                            x = core.X[:, b, t - 1, :]
                            dve.wait_ge(out_made, t)
                            if wide:
                                dve.scalar_tensor_tensor(x, ps_t[:, 0, 0:D], gate[:], x, ALU.mult, ALU.add).then_inc(added, 1)
                            else:
                                dve.tensor_tensor(x, ps_t[:, 0, 0:D], x, ALU.add).then_inc(added, 1)

            st.end_pass()


def feed_forward(core, index, pieces, routing):
    nc = core.nc
    gated = "w3" in pieces
    NE = pieces["w1"][1] // (256 if gated else 512)
    H = pieces["w1"][1] // NE
    NK = H // P
    given = routing == "given"
    passes = 1 if given else B
    picks = {"softmax2": 2, "top2softmax": 2, "argmax": 1, "given": 0}[routing]
    with ExitStack() as ctx:
        st = Step(core, ctx, index, pieces)
        norm = Norm(st)
        hT = st.sb("hT", [P, 2, NK, S])
        act_h = st.sb("act_h", [P, 2, S])
        logit = st.sb("logit", [P, NT, 15])
        top = st.sb("top", [P, NT, 8])
        hit = st.sb("hit", [P, NT, 15])
        e_x = st.sb("e_x", [P, NT, E])
        small = st.sb("small", [P, 3, NT])
        cw = st.sb("cw", [P, NT, NE])
        idx = st.sb("idx", [P, NT, 2])
        cw2 = st.sb("cw2", [P, NT, E])
        ps_r = st.ps("ps_r", [P, BANK])
        ps_a = st.ps("ps_a", [P, 2, BANK])
        ps_g = st.ps("ps_g", [P, 2, BANK])
        ps_y = st.ps("ps_y", [P, 2, BANK])
        dve_done = st.sem("dve_done")
        routed, lx_ready, ex_ready, up_made, act_made, hid_ready, down_made, added = (st.sem(n) for n in (
            "routed", "lx_ready", "ex_ready", "up_made", "act_made", "hid_ready", "down_made", "added"))
        begin(core, index, st)

        def w_up(name, e, k):
            c, _ = pieces[name]
            return st.w[:, c + (e * NK + k) * P:c + (e * NK + k + 1) * P]

        with nc.Fori(0, passes) as b:
            with nc.Block() as block:

                @block.gpsimd
                def _(pool):
                    norm.gpsimd(pool)

                @block.tensor
                def _(pe):
                    norm.tensor(pe, ps_r)
                    pe.wait_ge(norm.xnT_ready, 1)
                    if not given:
                        c, _ = pieces["router"]
                        for t in range(NT):
                            bias = {"argmax": "f2_br", "top2softmax": "f3_br"}.get(routing)
                            ins = pe.matmul(ps_r[:, t * E:(t + 1) * E], norm.xnT[:, t * P:(t + 1) * P], st.w[:, c:c + E],
                                            start=True, stop=bias is None)
                            if bias:
                                ins = pe.matmul(ps_r[:, t * E:(t + 1) * E], core.ones[:, :], core.row(bias), start=False, stop=True)
                        ins.then_inc(routed, 1)

                    def up(e, k):
                        i = e * NK + k
                        if i >= 2:
                            pe.wait_ge(hid_ready, i - 1)
                        ins = pe.matmul(ps_a[:, i % 2, :], w_up("w1", e, k), norm.xnT[:], start=True, stop=True)
                        if gated:
                            ins = pe.matmul(ps_g[:, i % 2, :], w_up("w3", e, k), norm.xnT[:], start=True, stop=True)
                        ins.then_inc(up_made, 1)

                    def down(e):
                        pe.wait_ge(hid_ready, (e + 1) * NK)
                        if e >= 2:
                            pe.wait_ge(added, NT * (e - 1))
                        for t in range(NT):
                            for k in range(NK):
                                ins = pe.matmul(ps_y[:, e % 2, t * D:(t + 1) * D], hT[:, e % 2, k, t * P:(t + 1) * P],
                                                w_up("w2", e, k), start=(k == 0), stop=(k == NK - 1 and routing != "argmax"))
                            if routing == "argmax":
                                ins = pe.matmul(ps_y[:, e % 2, t * D:(t + 1) * D], core.ones[:, :],
                                                core.row("f2_b2", e * D, D), start=False, stop=True)
                        ins.then_inc(down_made, 1)

                    for e in range(NE + 1):
                        for k in range(NK):
                            if e < NE:
                                up(e, k)
                            if k == 0 and e >= 1:
                                down(e - 1)

                @block.scalar
                def _(act):
                    norm.scalar(act, ps_r)
                    if routing in ("softmax2", "top2softmax"):
                        act.wait_ge(lx_ready, 1)
                        act.activation(e_x[:], e_x[:], ACT.Exp).then_inc(ex_ready, 1)
                    for e in range(NE):
                        for k in range(NK):
                            i = e * NK + k
                            act.wait_ge(up_made, i + 1)
                            if gated:
                                if i >= 2:
                                    act.wait_ge(hid_ready, i - 1)
                                act.activation(act_h[:, i % 2, :], ps_a[:, i % 2, :], ACT.Silu).then_inc(act_made, 1)
                            else:
                                if e >= 2:
                                    act.wait_ge(down_made, e - 1)
                                bias = st.piece("b1")[:, i:i + 1] if "b1" in pieces else 0.0
                                act.activation(hT[:, e % 2, k, :], ps_a[:, i % 2, :], ACT.Gelu, bias=bias).then_inc(hid_ready, 1)

                @block.vector
                def _(dve):
                    chain = Chain(dve, dve_done)
                    norm.vector(dve, chain, b)
                    if NE > E:
                        chain.done(dve.memset(cw[:, :, E:NE], 1.0))
                    if given:
                        wt = st.piece("weights").rearrange("p (t k) -> p t k", t=NT)
                        chain.done(dve.tensor_copy(idx[:], core.indices[:]))
                        chain.wait()
                        for t in range(NT):
                            chain.done(dve.tensor_scalar(cw[:, t, :], core.const("expert_no"), idx[:, t, 0:1], wt[:, t, 0:1], ALU.is_equal, ALU.mult))
                            chain.done(dve.tensor_scalar(cw2[:, t, :], core.const("expert_no"), idx[:, t, 1:2], wt[:, t, 1:2], ALU.is_equal, ALU.mult))
                        chain.wait()
                        chain.done(dve.tensor_tensor(cw[:], cw[:], cw2[:], ALU.add))
                        chain.wait()
                    else:
                        chain.done(dve.memset(logit[:, :, E:15], -BIG))
                        dve.wait_ge(routed, 1)
                        chain.done(dve.tensor_copy(logit[:, :, 0:E], ps_r[:, 0:NT * E].rearrange("p (t e) -> p t e", t=NT)))
                        chain.wait()

                        def softmax():
                            chain.done(dve.tensor_reduce(small[:, 0, :], e_src(), AX, ALU.max))
                            chain.wait()
                            dve.tensor_tensor(e_x[:], e_src(), small[:, 0, :].unsqueeze(2).to_broadcast([P, NT, E]),
                                              ALU.subtract).then_inc(lx_ready, 1)
                            dve.wait_ge(ex_ready, 1)
                            chain.done(dve.tensor_reduce(small[:, 1, :], e_x[:], AX, ALU.add))
                            chain.wait()
                            chain.done(dve.reciprocal(small[:, 2, :], small[:, 1, :]))
                            chain.wait()
                            chain.done(dve.tensor_tensor(softmax_out(), e_x[:], small[:, 2, :].unsqueeze(2).to_broadcast([P, NT, E]), ALU.mult))
                            chain.wait()

                        def choose():
                            for t in range(NT):
                                chain.done(dve.max(top[:, t, :], logit[:, t, 0:E]))
                            chain.wait()
                            chain.done(dve.memset(top[:, :, picks:8], -BIG))
                            chain.wait()
                            for t in range(NT):
                                chain.done(dve.match_replace(hit[:, t, 0:15], top[:, t, :], logit[:, t, :], BIG))
                            chain.wait()
                            chain.done(dve.tensor_scalar(hit[:, :, 0:E], hit[:, :, 0:E], BIG, None, ALU.is_ge))
                            chain.wait()

                        if routing == "softmax2":
                            e_src = softmax_out = lambda: logit[:, :, 0:E]
                            softmax()
                            choose()
                            chain.done(dve.tensor_tensor(cw[:, :, 0:E], hit[:, :, 0:E], logit[:, :, 0:E], ALU.mult))
                        elif routing == "top2softmax":
                            choose()
                            chain.done(dve.tensor_scalar(cw2[:], hit[:, :, 0:E], BIG, BIG, ALU.mult, ALU.subtract))
                            chain.done(dve.tensor_tensor(logit[:, :, 0:E], logit[:, :, 0:E], hit[:, :, 0:E], ALU.mult))
                            chain.wait()
                            chain.done(dve.tensor_tensor(logit[:, :, 0:E], logit[:, :, 0:E], cw2[:], ALU.add))
                            chain.wait()
                            e_src = lambda: logit[:, :, 0:E]
                            softmax_out = lambda: cw[:, :, 0:E]
                            softmax()
                        else:
                            choose()
                            chain.done(dve.tensor_copy(cw[:], hit[:, :, 0:E]))
                        chain.wait()

                    def accumulate(e):
                        dve.wait_ge(down_made, e + 1)
                        for t in range(NT):
                            x = core.X[:, b, t, :]
                            if e >= 1:
                                dve.wait_ge(added, NT * (e - 1) + t + 1)
                            dve.scalar_tensor_tensor(x, ps_y[:, e % 2, t * D:(t + 1) * D], cw[:, t, e:e + 1], x,
                                                     ALU.mult, ALU.add).then_inc(added, 1)

                    for e in range(NE):
                        if gated:
                            for k in range(NK):
                                i = e * NK + k
                                dve.wait_ge(act_made, i + 1)
                                if e >= 2:
                                    dve.wait_ge(down_made, e - 1)
                                dve.tensor_tensor(hT[:, e % 2, k, :], act_h[:, i % 2, :], ps_g[:, i % 2, :], ALU.mult).then_inc(hid_ready, 1)
                        if e >= 1:
                            accumulate(e - 1)
                    accumulate(NE - 1)

            st.end_pass()
        if given:
            with nc.Block() as block:

                @block.tensor
                def _(pe):
                    pe.matmul(ps_r[:, 0:D], core.ones[:, :], core.row("f1_b"), start=True, stop=True).then_inc(routed, 1)

                @block.vector
                def _(dve):
                    dve.wait_ge(routed, 1)
                    x = core.X[:].rearrange("p b t d -> p (b t) d")
                    dve.tensor_tensor(x, ps_r[:, 0:D].unsqueeze(1).to_broadcast([P, B * NT, D]), x, ALU.add)

            st.end_pass()


def favor_attention(core, index):
    nc = core.nc
    pieces = FAVOR
    dh, M = 8, 32
    EPS = 1e-6
    F = NH * M
    NF = F // P
    with ExitStack() as ctx:
        st = Step(core, ctx, index, pieces)
        norm = Norm(st)
        proj = st.sb("proj", [P, NH, M])
        qkT = st.sb("qkT", [P, 2, S])
        sq = st.sb("sq", [P, 2, S])
        V1 = st.sb("V1", [P, NT, D + 1])
        sh = st.sb("sh", [P, 2, F])
        ph = st.sb("ph", [P, 2, F])
        phi = st.sb("phi", [P, 2, NT, F])
        mx, cc = st.sb("mx", [P, 2, NT, NH]), st.sb("cc", [P, 2, NT, NH])
        phT = st.sb("phT", [P, 2, NF, P])
        KV = st.sb("KV", [P, NF, D + NH])
        rden = st.sb("rden", [P, NT, NH])
        O, OT = st.sb("O", [P, NT, D]), st.sb("OT", [P, S])
        ps_f = st.ps("ps_f", [P, 2, BANK])
        ps_n = st.ps("ps_n", [P, BANK])
        ps_k = st.ps("ps_k", [P, 2, BANK])
        ps_t = st.ps("ps_t", [P, BANK])
        ps_o = st.ps("ps_o", [P, 2, BANK])
        dve_done = st.sem("dve_done")
        qkv_made, qkv_kept, v_turned, v_ready, n_made, f_made = (st.sem(n) for n in (
            "qkv_made", "qkv_kept", "v_turned", "v_ready", "n_made", "f_made"))
        shifted, exped, phi_ready, kv_made, kv_kept, kv_ready = (st.sem(n) for n in (
            "shifted", "exped", "phi_ready", "kv_made", "kv_kept", "kv_ready"))
        q_turned, qT_ready, weighted, o_ready, o_turned, oT_ready, out_made = (st.sem(n) for n in (
            "q_turned", "qT_ready", "weighted", "o_ready", "o_turned", "oT_ready", "out_made"))
        ident = core.const("ident")
        begin(core, index, st)
        with nc.Block() as block:

            @block.vector
            def _(dve):
                for h in range(NH):
                    dve.tensor_scalar(proj[:, h, :], st.piece("proj"), core.const("head8")[:, h:h + 1], None, ALU.mult)
                for t in range(NT):
                    dve.memset(V1[:, t, D:D + 1], 1.0)

        with nc.Fori(0, B) as b:
            with nc.Block() as block:

                @block.gpsimd
                def _(pool):
                    norm.gpsimd(pool)

                @block.tensor
                def _(pe):
                    norm.tensor(pe, ps_t)
                    pe.wait_ge(norm.xnT_ready, 1)
                    for name, bank in (("wk", ps_f[:, 0, :]), ("wq", ps_f[:, 1, :]), ("wv", ps_k[:, 0, :])):
                        pe.matmul(bank, st.piece(name), norm.xnT[:], start=True, stop=True).then_inc(qkv_made, 1)
                    pe.wait_ge(qkv_kept, 5)
                    for t in range(NT):
                        ins = pe.transpose(ps_t[:, t * P:(t + 1) * P], O[:, t, :], ident)
                    ins.then_inc(v_turned, 1)
                    for i in range(2):
                        for t in range(NT):
                            ins = pe.matmul(ps_n[:, (i * NT + t) * NH:(i * NT + t + 1) * NH], sq[:, i, t * P:(t + 1) * P],
                                            core.const("head8"), start=True, stop=True)
                    ins.then_inc(n_made, 1)
                    for u in range(2 * NT):
                        i, t = divmod(u, NT)
                        if u >= 2:
                            pe.wait_ge(shifted, u - 1)
                        pe.matmul(ps_f[:, u % 2, :], qkT[:, i, t * P:(t + 1) * P], proj[:].rearrange("p h m -> p (h m)"),
                                  start=True, stop=True).then_inc(f_made, 1)
                    pe.wait_ge(phi_ready, NT)
                    pe.wait_ge(v_ready, 1)
                    for j in range(NF):
                        if j >= 2:
                            pe.wait_ge(kv_kept, j - 1)
                        for t in range(NT):
                            ins = pe.matmul(ps_k[:, j % 2, 0:D + 1], phi[:, 0, t, j * P:(j + 1) * P], V1[:, t, :],
                                            start=(t == 0), stop=(t == NT - 1))
                        ins.then_inc(kv_made, 1)
                    for t in range(NT):
                        pe.wait_ge(phi_ready, NT + t + 1)
                        if t >= 1:
                            pe.wait_ge(qT_ready, t)
                        for j in range(NF):
                            ins = pe.transpose(ps_t[:, j * P:(j + 1) * P], phi[:, 1, t, j * P:(j + 1) * P], ident)
                        ins.then_inc(q_turned, 1)
                        pe.wait_ge(kv_ready, NF)
                        pe.wait_ge(kv_kept, NF)
                        pe.wait_ge(qT_ready, t + 1)
                        if t >= 2:
                            pe.wait_ge(o_ready, t - 1)
                        for j in range(NF):
                            ins = pe.matmul(ps_o[:, t % 2, 0:D + NH], phT[:, t % 2, j, :], KV[:, j, :],
                                            start=(j == 0), stop=(j == NF - 1))
                        ins.then_inc(weighted, 1)
                    pe.wait_ge(o_ready, NT)
                    for t in range(NT):
                        ins = pe.transpose(ps_t[:, t * P:(t + 1) * P], O[:, t, :], ident)
                    ins.then_inc(o_turned, 1)
                    pe.wait_ge(oT_ready, 1)
                    for t in range(NT):
                        pe.matmul(ps_n[:, t * D:(t + 1) * D], OT[:, t * P:(t + 1) * P], st.piece("wo"), start=True, stop=False)
                        ins = pe.matmul(ps_n[:, t * D:(t + 1) * D], core.ones[:, :], core.row("a1_bo"), start=False, stop=True)
                    ins.then_inc(out_made, 1)

                @block.scalar
                def _(act):
                    norm.scalar(act, ps_t)
                    scale = float(dh) ** -0.5
                    for i in range(2):
                        act.wait_ge(qkv_made, i + 1)
                        act.activation(qkT[:, i, :], ps_f[:, i, :], ACT.Copy, scale=scale).then_inc(qkv_kept, 1)
                        act.activation(sq[:, i, :], ps_f[:, i, :], ACT.Square, scale=scale).then_inc(qkv_kept, 1)
                    act.wait_ge(qkv_made, 3)
                    act.activation(O[:].rearrange("p t d -> p (t d)"), ps_k[:, 0, :], ACT.Copy).then_inc(qkv_kept, 1)
                    act.wait_ge(v_turned, 1)
                    act.activation(V1[:, :, 0:D], ps_t[:].rearrange("p (t d) -> p t d", t=NT), ACT.Copy).then_inc(v_ready, 1)
                    for u in range(2 * NT):
                        act.wait_ge(shifted, u + 1)
                        if u >= 2:
                            act.wait_ge(phi_ready, u - 1)
                        act.activation(ph[:, u % 2, :], sh[:, u % 2, :], ACT.Exp).then_inc(exped, 1)
                    for t in range(NT):
                        act.wait_ge(q_turned, t + 1)
                        if t >= 2:
                            act.wait_ge(weighted, t - 1)
                        act.activation(phT[:, t % 2].rearrange("p j s -> p (j s)"), ps_t[:], ACT.Copy).then_inc(qT_ready, 1)
                    act.wait_ge(o_turned, 1)
                    act.activation(OT[:], ps_t[:], ACT.Copy).then_inc(oT_ready, 1)

                @block.vector
                def _(dve):
                    chain = Chain(dve, dve_done)
                    norm.vector(dve, chain, b)
                    dve.wait_ge(n_made, 1)

                    def shift(u):
                        i, t = divmod(u, NT)
                        dve.wait_ge(f_made, u + 1)
                        f = ps_f[:, u % 2, :].rearrange("p (h m) -> p h m", h=NH)
                        chain.done(dve.tensor_reduce(mx[:, i, t, :], f, AX, ALU.max))
                        chain.wait()
                        chain.done(dve.scalar_tensor_tensor(cc[:, i, t, :], ps_n[:, u * NH:(u + 1) * NH], 0.5, mx[:, i, t, :],
                                                            ALU.mult, ALU.add))
                        chain.wait()
                        if u >= 2:
                            dve.wait_ge(exped, u - 1)
                        dve.tensor_tensor(sh[:, u % 2, :].rearrange("p (h m) -> p h m", h=NH), f,
                                          cc[:, i, t, :].unsqueeze(2).to_broadcast([P, NH, M]), ALU.subtract).then_inc(shifted, 1)

                    def feature(u):
                        i, t = divmod(u, NT)
                        dve.wait_ge(exped, u + 1)
                        dve.tensor_scalar(phi[:, i, t, :], ph[:, u % 2, :], EPS, float(M) ** -0.5, ALU.add, ALU.mult).then_inc(phi_ready, 1)

                    shift(0)
                    for u in range(2 * NT):
                        if u + 1 < 2 * NT:
                            shift(u + 1)
                        feature(u)
                    blk = st.piece("blk").rearrange("p (j n) -> p j n", j=NF)
                    blkh = st.piece("blkh").rearrange("p (j n) -> p j n", j=NF)
                    for j in range(NF):
                        dve.wait_ge(kv_made, j + 1)
                        dve.tensor_tensor(KV[:, j, 0:D], ps_k[:, j % 2, 0:D], blk[:, j, :], ALU.mult).then_inc(kv_ready, 1)
                        dve.tensor_scalar(KV[:, j, D:D + NH], blkh[:, j, :], ps_k[:, j % 2, D:D + 1], None, ALU.mult).then_inc(kv_kept, 1)
                    for t in range(NT):
                        dve.wait_ge(weighted, t + 1)
                        chain.done(dve.tensor_scalar(rden[:, t, :], ps_o[:, t % 2, D:D + NH], EPS, None, ALU.add))
                        chain.wait()
                        chain.done(dve.reciprocal(rden[:, t, :], rden[:, t, :]))
                        chain.wait()
                        dve.tensor_tensor(O[:, t, :].rearrange("p (h d) -> p h d", h=NH), ps_o[:, t % 2, 0:D].rearrange("p (h d) -> p h d", h=NH),
                                          rden[:, t, :].unsqueeze(2).to_broadcast([P, NH, dh]), ALU.mult).then_inc(o_ready, 1)
                    dve.wait_ge(out_made, 1)
                    x = core.X[:, b].rearrange("p t d -> p (t d)")
                    dve.tensor_tensor(x, ps_n[:], x, ALU.add)

            st.end_pass()


def talking_attention(core, index):
    nc = core.nc
    pieces = TALK
    dh, NM, TOP = 64, 64, 64
    NJ = NH * dh // P
    Q = 64
    R = 8
    NUNIT, NG = S // Q, Q // R
    NGROUP = NUNIT * NG
    LAG_E, LAG_M = 2, 4
    scale = float(dh) ** -0.5
    ROUNDS = TOP // 8
    NC = NT + 1

    def rows_of(q, c):
        return NM if c == NT else max(0, min(P, Q * (q + 1) - P * c))

    def chunks(q):
        return [c for c in range(NC) if rows_of(q, c)]

    def width(g):
        return NM + R * (g + 1)

    with ExitStack() as ctx:
        st = Step(core, ctx, index, pieces)
        norm = Norm(st)
        QT = st.sb("QT", [P, NJ, Q])
        KT = st.sb("KT", [P, NJ, S])
        V = st.sb("V", [P, NT, NJ * P])
        ST = st.sb("ST", [P, NC, NG, NH, R])
        S1 = st.sb("S1", [P, 2, NM + S])
        Dt = st.sb("Dt", [P, 4, NM + S])
        W = st.sb("W", [P, NM + S])
        Ex = st.sb("Ex", [P, 3, NM + S])
        A = st.sb("A", [P, 4, NM + S])
        top = st.sb("top", [P, 2, ROUNDS, 8])
        nb = st.sb("nb", [P, 4])
        den, rden = st.sb("den", [P, 2]), st.sb("rden", [P, 4])
        post = st.sb("post", [P, 3, P])
        AT = st.sb("AT", [P, NC, NH, Q])
        OT = st.sb("OT", [P, NJ, Q])
        ps_t = st.ps("ps_t", [P, 2, BANK])
        ps_m = st.ps("ps_m", [P, 2, BANK])
        ps_c = st.ps("ps_c", [P, 2, BANK])
        ps_o = st.ps("ps_o", [P, BANK])
        ps_x = st.ps("ps_x", [P, BANK])
        dve_done = st.sem("dve_done")
        made, kept, qk_made, st_kept, turned, s_kept, mixed, m_kept = (st.sem(n) for n in (
            "made", "kept", "qk_made", "st_kept", "turned", "s_kept", "mixed", "m_kept"))
        max_ready, nb_ready, exped, chosen, cleared, post_ready, back, at_kept = (st.sem(n) for n in (
            "max_ready", "nb_ready", "exped", "chosen", "cleared", "post_ready", "back", "at_kept"))
        weighted, oT_ready, out_made, added, q_made, q_kept = (st.sem(n) for n in (
            "weighted", "oT_ready", "out_made", "added", "q_made", "q_kept"))
        ident = core.const("ident")
        begin(core, index, st)
        wcol = {n: pieces[n][0] for n in pieces}
        memk = st.piece("memk").rearrange("p (j m) -> p j m", j=NJ)

        def keys(par, j, c, n):
            rows = slice(64 * par, 64 * par + 64)
            return memk[rows, j, :] if c == NT else KT[rows, j, c * P:c * P + n]

        def st_before(q):
            return sum(len(chunks(x)) for x in range(q))

        def back_parts(g):
            cs = chunks(g // NG)
            return [cs[:4], cs[4:]] if len(cs) > 4 else [cs]

        def back_before(g):
            return sum(len(back_parts(x)) for x in range(g))

        NPRE = NJ + 2 * NT

        with nc.Fori(0, B) as b:
            with nc.Block() as block:

                @block.gpsimd
                def _(pool):
                    norm.gpsimd(pool)
                    for g in range(NGROUP):
                        w, wu = width(g), NM + Q * (g // NG + 1)
                        pool.wait_ge(max_ready, g + 1)
                        if g >= 4:
                            pool.wait_ge(exped, g - 3)
                        pool.tensor_scalar(nb[:, g % 4:g % 4 + 1], top[:, g % 2, 0, 0:1], -scale, 0.0, ALU.mult, ALU.add).then_inc(nb_ready, 1)
                        if w < wu:
                            if g >= 4:
                                pool.wait_ge(back, back_before(g - 3))
                            pool.memset(A[:, g % 4, w:wu], 0.0).then_inc(cleared, 1)
                        pool.wait_ge(chosen, g + 1)
                        if g >= 3:
                            pool.wait_ge(back, back_before(g - 2))
                        pool.tensor_scalar(post[:, g % 3, :], st.piece("post"), rden[:, g % 4:g % 4 + 1], 0.0, ALU.mult,
                                           ALU.add).then_inc(post_ready, 1)

                @block.tensor
                def _(pe):
                    norm.tensor(pe, ps_x)
                    pe.wait_ge(norm.xnT_ready, 1)
                    for i in range(NPRE):
                        if i >= 2:
                            pe.wait_ge(kept, i - 1)
                        if i < NJ:
                            c = wcol["wk"] + i * P
                            pe.matmul(ps_c[:, i % 2, :], st.w[:, c:c + P], norm.xnT[:], start=True, stop=True).then_inc(made, 1)
                        else:
                            t, half = divmod(i - NJ, 2)
                            c = wcol["wv"] + half * BANK
                            pe.matmul(ps_c[:, i % 2, :], norm.xnT[:, t * P:(t + 1) * P], st.w[:, c:c + BANK],
                                      start=True, stop=True).then_inc(made, 1)
                    pe.wait_ge(kept, NPRE)

                    def unit_scores(q):
                        for j in range(NJ):
                            c = wcol["wq"] + j * P
                            ins = pe.matmul(ps_o[:, j * Q:(j + 1) * Q], st.w[:, c:c + P], norm.xnT[:, q * Q:(q + 1) * Q],
                                            start=True, stop=True)
                        ins.then_inc(q_made, 1)
                        pe.wait_ge(q_kept, q + 1)
                        for n, c in enumerate(chunks(q)):
                            r = rows_of(q, c)
                            pe.wait_ge(st_kept, st_before(q) + n)
                            for j in range(NJ):
                                for par in range(2):
                                    ins = pe.matmul(ps_c[0:r, par, j * Q:(j + 1) * Q], keys(par, j, c, r),
                                                    QT[64 * par:64 * par + 64, j, :], start=True, stop=True)
                            ins.then_inc(qk_made, 1)

                    def turn(g):
                        q, k = divmod(g, NG)
                        cs = chunks(q)
                        pe.wait_ge(st_kept, st_before(q + 1))
                        if g >= 1:
                            pe.wait_ge(s_kept, 2 * g)
                        for c in cs:
                            r = rows_of(q, c)
                            out = ps_t[:, 1, 0:NM] if c == NT else ps_t[:, 0, c * P:c * P + r]
                            ins = pe.transpose(out, ST[0:r, c, k].rearrange("p h r -> p (h r)"), ident[0:r, 0:r])
                        ins.then_inc(turned, 1)

                    def mix(g):
                        w = width(g)
                        pe.wait_ge(s_kept, 2 * (g + 1))
                        if g >= 1:
                            pe.wait_ge(m_kept, 2 * g)
                        pe.matmul(ps_m[:, 1, 0:NM], st.piece("pre"), S1[:, g % 2, 0:NM], start=True, stop=True)
                        pe.matmul(ps_m[:, 0, 0:w - NM], st.piece("pre"), S1[:, g % 2, NM:w], start=True, stop=True).then_inc(mixed, 1)

                    def mix_back(g):
                        q = g // NG
                        pe.wait_ge(post_ready, g + 1)
                        if g % NG != NG - 1:
                            pe.wait_ge(cleared, g + 1 - g // NG)
                        for i, part in enumerate(back_parts(g)):
                            n = back_before(g) + i
                            if n >= 2:
                                pe.wait_ge(at_kept, n - 1)
                            for x, c in enumerate(part):
                                r = rows_of(q, c)
                                cols = slice(0, NM) if c == NT else slice(NM + c * P, NM + c * P + r)
                                ins = pe.matmul(ps_c[0:r, n % 2, x * P:(x + 1) * P], A[:, g % 4, cols], post[:, g % 3, :],
                                                start=True, stop=True)
                            ins.then_inc(back, 1)

                    def unit_out(q):
                        pe.wait_ge(at_kept, back_before((q + 1) * NG))
                        cs = chunks(q)
                        for k in range(NH):
                            for n, c in enumerate(cs):
                                r = rows_of(q, c)
                                v = st.w[0:r, wcol["memv"] + k * dh:wcol["memv"] + (k + 1) * dh] if c == NT else V[0:r, c, k * dh:(k + 1) * dh]
                                ins = pe.matmul(ps_o[64 * (k % 2):64 * (k % 2) + 64, (k // 2) * Q:(k // 2 + 1) * Q], v,
                                                AT[0:r, c, k, :], start=(n == 0), stop=(n == len(cs) - 1))
                        ins.then_inc(weighted, 1)
                        pe.wait_ge(oT_ready, q + 1)
                        if q >= 1:
                            pe.wait_ge(added, q)
                        out = ps_x[64 * (q % 2):64 * (q % 2) + 64, 0:D]
                        for j in range(NJ):
                            c = wcol["wo"] + j * D
                            pe.matmul(out, OT[:, j, :], st.w[:, c:c + D], start=(j == 0), stop=False)
                        pe.matmul(out, core.ones[:, 0:Q], core.row("a2_bo"), start=False, stop=True).then_inc(out_made, 1)

                    for n in range(NGROUP + LAG_M):
                        if n < NGROUP:
                            if n % NG == 0:
                                if n >= LAG_M + 1:
                                    pe.wait_ge(at_kept, back_before(n - LAG_M))
                                unit_scores(n // NG)
                            turn(n)
                            mix(n)
                        g = n - LAG_M
                        if g >= 0:
                            if g == 0 or n % NG == 0:
                                pe.wait_ge(st_kept, st_before(min(n, NGROUP - 1) // NG + 1))
                            mix_back(g)
                            if g % NG == NG - 1:
                                unit_out(g // NG)

                @block.scalar
                def _(act):
                    norm.scalar(act, ps_x)
                    for i in range(NPRE):
                        act.wait_ge(made, i + 1)
                        if i < NJ:
                            dst = KT[:, i, :]
                        else:
                            t, half = divmod(i - NJ, 2)
                            dst = V[:, t, half * BANK:(half + 1) * BANK]
                        act.activation(dst, ps_c[:, i % 2, :], ACT.Copy).then_inc(kept, 1)

                    def keep_unit(q):
                        act.wait_ge(q_made, q + 1)
                        act.activation(QT[:].rearrange("p j s -> p (j s)"), ps_o[:], ACT.Copy).then_inc(q_kept, 1)
                        for n, c in enumerate(chunks(q)):
                            r = rows_of(q, c)
                            act.wait_ge(qk_made, st_before(q) + n + 1)
                            if q >= 1:
                                act.wait_ge(turned, q * NG)
                            act.activation(ST[0:r, c].rearrange("p k h r -> p h k r"),
                                           ps_c[0:r].rearrange("p a (j k r) -> p (a j) k r", j=NJ, k=NG), ACT.Copy).then_inc(st_kept, 1)

                    def keep_scores(g):
                        w = width(g)
                        act.wait_ge(turned, g + 1)
                        if g >= 2:
                            act.wait_ge(mixed, g - 1)
                        act.activation(S1[:, g % 2, 0:NM], ps_t[:, 1, 0:NM], ACT.Copy).then_inc(s_kept, 1)
                        act.activation(S1[:, g % 2, NM:w], ps_t[:, 0, 0:w - NM], ACT.Copy).then_inc(s_kept, 1)
                        act.wait_ge(mixed, g + 1)
                        if g >= 4:
                            act.wait_ge(chosen, g - 3)
                        act.activation(Dt[:, g % 4, 0:NM], ps_m[:, 1, 0:NM], ACT.Copy).then_inc(m_kept, 1)
                        act.activation(Dt[:, g % 4, NM:w], ps_m[:, 0, 0:w - NM], ACT.Copy).then_inc(m_kept, 1)

                    def exponentials(g):
                        w = width(g)
                        act.wait_ge(nb_ready, g + 1)
                        if g >= 3:
                            act.wait_ge(chosen, g - 2)
                        act.activation(Ex[:, g % 3, 0:w], Dt[:, g % 4, 0:w], ACT.Exp, bias=nb[:, g % 4:g % 4 + 1],
                                       scale=scale).then_inc(exped, 1)

                    def keep_back(g):
                        q, k = divmod(g, NG)
                        for i, part in enumerate(back_parts(g)):
                            n = back_before(g) + i
                            act.wait_ge(back, n + 1)
                            if q >= 1:
                                act.wait_ge(weighted, q)
                            full = [x for x, c in enumerate(part) if rows_of(q, c) == P]
                            rest = [x for x, c in enumerate(part) if rows_of(q, c) != P]
                            src = ps_c[:, n % 2, :].rearrange("p (c h r) -> p c h r", c=4, h=NH)
                            todo = []
                            if full:
                                todo.append((P, part[full[0]], full[0], len(full)))
                            todo += [(rows_of(q, part[x]), part[x], x, 1) for x in rest]
                            for r, c, x, m in todo:
                                for y in range(m):
                                    ins = act.activation(AT[0:r, c + y, :, k * R:(k + 1) * R], src[0:r, x + y], ACT.Copy)
                            ins.then_inc(at_kept, 1)

                    for n in range(NGROUP + LAG_M):
                        if n < NGROUP:
                            if n % NG == 0:
                                keep_unit(n // NG)
                            keep_scores(n)
                        if 0 <= n - LAG_E < NGROUP:
                            exponentials(n - LAG_E)
                        g = n - LAG_M
                        if g >= 0:
                            keep_back(g)
                            if g % NG == NG - 1:
                                act.wait_ge(weighted, g // NG + 1)
                                act.activation(OT[:].rearrange("p j s -> p (j s)"), ps_o[:], ACT.Copy).then_inc(oT_ready, 1)

                @block.vector
                def _(dve):
                    chain = Chain(dve, dve_done)
                    norm.vector(dve, chain, b)

                    def residual(q):
                        rows = slice(64 * (q % 2), 64 * (q % 2) + 64)
                        x = core.X[rows, b, q // 2, :]
                        dve.wait_ge(out_made, q + 1)
                        dve.tensor_tensor(x, ps_x[rows, 0:D], x, ALU.add).then_inc(added, 1)

                    for g in range(NGROUP):
                        w = width(g)
                        d, tp = Dt[:, g % 4, 0:w], top[:, g % 2]
                        dve.wait_ge(m_kept, 2 * (g + 1))
                        chain.done(dve.tensor_tensor(Dt[:, g % 4, w - R:w], Dt[:, g % 4, w - R:w], core.const("later"), ALU.add))
                        chain.wait()
                        if g >= 2:
                            dve.wait_ge(nb_ready, g - 1)
                        for r in range(ROUNDS):
                            src = d if r == 0 else W[:, 0:w]
                            ins = dve.max(tp[:, r, :], src)
                            if r == 0:
                                ins.then_inc(max_ready, 1)
                                dve.wait_ge(max_ready, g + 1)
                            else:
                                chain.done(ins)
                                chain.wait()
                            if r < ROUNDS - 1:
                                chain.done(dve.match_replace(W[:, 0:w], tp[:, r, :], src, -BIG))
                                chain.wait()
                        dve.wait_ge(exped, g + 1)
                        if g >= 4:
                            dve.wait_ge(back, back_before(g - 3))
                            dve.wait_ge(post_ready, g - 3)
                        chain.done(dve.scalar_tensor_tensor(A[:, g % 4, 0:w], d, tp[:, ROUNDS - 1, 7:8], Ex[:, g % 3, 0:w], ALU.is_ge,
                                                            ALU.mult, accum_out=den[:, g % 2:g % 2 + 1]))
                        chain.wait()
                        dve.reciprocal(rden[:, g % 4:g % 4 + 1], den[:, g % 2:g % 2 + 1]).then_inc(chosen, 1)
                        if g % NG == NG - 1 and g >= 2 * NG - 1:
                            residual(g // NG - 1)
                    residual(NUNIT - 1)

            st.end_pass()


def build(nc, ins, out):
    core = Core()
    core.nc = nc
    core.order = list(SUBLAYERS)
    core.packed = {i: ins[f"w{i}"] for i in core.order}
    with ExitStack() as ctx:
        def sb(name, shape, dt=F32):
            return ctx.enter_context(nc.sbuf_tensor(name, shape, dt))

        core.X = sb("X", [P, B, NT, D])
        core.consts = sb("consts", [P, NCONST])
        core.rows = sb("rows", [1, NROWS])
        core.ones = sb("ones", [1, P])
        core.ctxT = sb("ctxT", [P, B, SC])
        core.indices = sb("indices", [P, NT, 2], I32)
        core.arena = [sb("arena_even", [P, ARENA]), sb("arena_odd", [P, ARENA])]
        core.arrived = [ctx.enter_context(nc.semaphore("arrived_even")), ctx.enter_context(nc.semaphore("arrived_odd"))]
        loaded = ctx.enter_context(nc.semaphore("loaded"))
        stored = ctx.enter_context(nc.semaphore("stored"))
        with nc.Block() as block:

            @block.sync
            def _(sp):
                first = core.order[0]
                sp.dma_start(core.X[:].rearrange("p b t d -> p (b t d)"), ins["x"]).then_inc(loaded, 16)
                sp.dma_start(core.consts[:], ins["consts"]).then_inc(loaded, 16)
                sp.dma_start(core.arena[first % 2][:, 0:WIDTHS[first]], core.packed[first]).then_inc(core.arrived[first % 2], 16)
                sp.dma_start(core.rows[:], ins["rows"]).then_inc(loaded, 16)
                sp.dma_start(core.ctxT[:].rearrange("p b s -> p (b s)"), ins["ctxT"]).then_inc(loaded, 16)
                sp.dma_start(core.indices[:].rearrange("p t k -> p (t k)"), ins["indices"]).then_inc(loaded, 16)
                sp.wait_ge(loaded, 5 * 16)

            @block.vector
            def _(dve):
                dve.memset(core.ones[:], 1.0)

        for i in core.order:
            PROGRAMS[i](core, i)
        with nc.Block() as block:

            @block.sync
            def _(sp):
                sp.dma_start(out, core.X[:].rearrange("p b t d -> p (b t d)")).then_inc(stored, 16)
                sp.wait_ge(stored, 16)


PROGRAMS = {
    0: lambda c, i: self_attention(c, i, SELF_ROPE, {"bo": "zero"}, True),
    1: lambda c, i: cross_attention(c, i, ATT8, {"bv": "x0_bv", "bo": "x0_bo"}, 8),
    2: lambda c, i: feed_forward(c, i, FF0, "softmax2"),
    3: lambda c, i: favor_attention(c, i),
    4: lambda c, i: cross_attention(c, i, ATT64, {"bv": "x1_bv", "bo": "x1_bo"}, 64),
    5: lambda c, i: feed_forward(c, i, FF1, "given"),
    6: lambda c, i: talking_attention(c, i),
    7: lambda c, i: cross_attention(c, i, ATT8, {"bv": "x2_bv", "bo": "x2_bo"}, 8),
    8: lambda c, i: feed_forward(c, i, FF2, "argmax"),
    9: lambda c, i: self_attention(c, i, SELF_PRIOR, {"bo": "a3_bo"}, False),
    10: lambda c, i: cross_attention(c, i, ATT8, {"bv": "zero", "bo": "x3_bo"}, 8),
    11: lambda c, i: feed_forward(c, i, FF3, "top2softmax"),
}


def _tokens(x):
    return x.reshape(-1, P, x.shape[-1]).transpose(1, 0, 2).reshape(P, -1)


def _pack(pieces, given):
    total = max(c + n for c, n in pieces.values())
    out = np.zeros((P, total), np.float32)
    for name, (c, n) in pieces.items():
        if name in given:
            a = given[name]
            out[:a.shape[0], c:c + n] = a.reshape(a.shape[0], n)
    return out


def _spread_heads(w, heads):
    out = np.zeros((NH, 8, NH, 8), np.float32)
    w = w[heads]
    for i in range(8):
        out[:, i, :, i] = w
    return out.reshape(P, P)


def _constants():
    p = np.arange(P)
    consts = _pack(CONST, {
        "ident": np.eye(P, dtype=np.float32),
        "head8": (p[:, None] // 8 == np.arange(NH)[None]).astype(np.float32),
        "head64": (p[:, None] // 64 == np.arange(NH)[None] % 2).astype(np.float32),
        "expert_no": np.broadcast_to(np.arange(E, dtype=np.float32), (P, E)),
        "minus_half": np.full((P, NT), -0.5, np.float32),
        "later": np.where(np.arange(8)[None] > p[:, None] % 8, -BIG, 0.0).astype(np.float32),
    })
    pos = np.arange(S, dtype=np.float32)
    freq = np.float32(10000.0) ** (-np.arange(0, 8, 2, dtype=np.float32) / np.float32(8))
    angle = (pos[:, None] * freq[None]).astype(np.float32)[:, (p % 8) // 2].T
    sign = np.where(p % 2 == 0, -1.0, 1.0).astype(np.float32)[:, None]
    swap = (p[:, None] == (p ^ 1)[None]).astype(np.float32)
    q = (np.arange(NT)[None, :, None] * P + p[:, None, None]).astype(np.float32)
    k = np.arange(S, dtype=np.float32)[None, None]
    causal = np.where(k > q, -BIG, 0.0).astype(np.float32)
    gauss = np.zeros((P, NT, S), np.float32)
    for period, weight, sigma in ((1.0, 0.8, 0.5), (30.0, 0.4, 2.0)):
        gauss = gauss + np.float32(weight) * np.exp(-(np.abs(q - k) - np.float32(period)) ** 2 / np.float32(2.0 * sigma ** 2))
    rope = {"cos": np.cos(angle), "sin": np.sin(angle) * sign, "swap": swap, "causal": causal.reshape(P, -1)}
    return consts, rope, gauss.reshape(P, -1).astype(np.float32)


def _layouts(a):
    consts, rope, gauss = _constants()

    p, j = np.arange(P), np.arange(4)
    own = (4 * j[None, :, None] + p[:, None, None] // 32 == np.arange(NH)[None, None]).astype(np.float32)
    favor_blocks, favor_heads = np.repeat(own, 8, axis=2).reshape(P, -1), own.reshape(P, -1)

    def att(prefix, names, bq=None, bk=None, bv=None):
        g = {k: a[prefix + n].T for k, n in zip(("wq", "wk", "wv", "wo"), names)}
        for k, n in (("bq", bq), ("bk", bk), ("bv", bv)):
            if n:
                g[k] = a[prefix + n].reshape(P, 1)
        return g

    def up(w):
        return w.transpose(1, 0, 2).reshape(P, -1)

    def down(w):
        e, h, d = w.shape
        return w.reshape(e, h // P, P, d).transpose(2, 0, 1, 3).reshape(P, -1)

    def tiles(w):
        return w.reshape(-1, P, w.shape[1]).transpose(1, 0, 2).reshape(P, -1)

    cap = ("Wq", "Wk", "Wv", "Wo")
    low = ("w_q", "w_k", "w_v", "w_o")
    spread = lambda v: np.broadcast_to(v, (P, v.shape[-1]))
    kv = a["L1_xattn_w_kv"]
    ins = {
        "w0": _pack(SELF_ROPE, {**att("L0_attn_", cap), **rope}),
        "w1": _pack(ATT8, att("L0_xattn_", cap, "bq", "bk")),
        "w2": _pack(FF0, {"w1": up(a["L0_ffn_w1"]), "w3": up(a["L0_ffn_w3"]), "w2": down(a["L0_ffn_w2"]),
                          "router": a["L0_ffn_gate_w"].T}),
        "w3": _pack(FAVOR, {**att("L1_attn_", cap), "proj": a["L1_attn_proj"].transpose(0, 2, 1).reshape(P, 32),
                            "blk": favor_blocks, "blkh": favor_heads}),
        "w4": _pack(ATT64, {"wq": a["L1_xattn_w_q"], "wk": kv[:, :1024], "wv": kv[:, 1024:], "wo": tiles(a["L1_xattn_w_out"]),
                            "gamma": spread(a["L1_xattn_ln_gamma"]), "beta": spread(a["L1_xattn_ln_beta"]),
                            "gate": spread(a["L1_xattn_gate"])}),
        "w5": _pack(FF1, {"w1": up(a["L1_ffn_w1"]), "w2": down(a["L1_ffn_w2"]),
                          "weights": _tokens(a["L1_ffn_expert_weights"])}),
        "w6": _pack(TALK, {"wq": a["L2_attn_Wq"].T, "wk": a["L2_attn_Wk"].T, "wv": a["L2_attn_Wv"].T,
                           "wo": tiles(a["L2_attn_Wout"].T),
                           "memk": a["L2_attn_mem_k"].reshape(8, 2, 64, 64).transpose(1, 3, 0, 2).reshape(P, 512),
                           "memv": a["L2_attn_mem_v"].transpose(1, 0, 2).reshape(64, 1024),
                           "pre": _spread_heads(a["L2_attn_pre_proj"], [*range(0, NH, 2), *range(1, NH, 2)]), "post": _spread_heads(a["L2_attn_post_proj"], list(range(NH)))}),
        "w7": _pack(ATT8, att("L2_xattn_", low, "b_q", "b_k")),
        "w8": _pack(FF2, {"w1": up(a["L2_ffn_w1"]), "w2": down(a["L2_ffn_w2"]), "router": a["L2_ffn_wr"],
                          "b1": a["L2_ffn_b1"].reshape(E, 4, P).transpose(2, 0, 1).reshape(P, -1)}),
        "w9": _pack(SELF_PRIOR, {**att("L3_attn_", cap, "bq", "bk", "bv"), "gauss": gauss,
                                 "lam": np.broadcast_to(a["L3_attn_prior_lambda"].reshape(1, 1), (P, 1))}),
        "w10": _pack(ATT8, att("L3_xattn_", cap)),
        "w11": _pack(FF3, {k: (up if k != "w2" else down)(np.concatenate([a["L3_ffn_" + k], a["L3_ffn_s" + k]]))
                           for k in ("w1", "w3", "w2")} | {"router": a["L3_ffn_router_w"].T}),
    }
    rows = np.zeros((1, NROWS), np.float32)
    for name, source in (("x0_bv", "L0_xattn_bv"), ("x0_bo", "L0_xattn_bo"), ("a1_bo", "L1_attn_bo"), ("x1_bo", "L1_xattn_b_out"),
                         ("f1_b", "L1_ffn_bias"), ("a2_bo", "L2_attn_bout"), ("x2_bv", "L2_xattn_b_v"), ("x2_bo", "L2_xattn_b_o"),
                         ("f2_br", "L2_ffn_br"), ("f2_b2", "L2_ffn_b2"), ("a3_bv", "L3_attn_bv"), ("a3_bo", "L3_attn_bo"),
                         ("x3_bo", "L3_xattn_bo"), ("f3_br", "L3_ffn_experts_bias")):
        c, n = ROWS[name]
        rows[0, c:c + n] = a[source].reshape(-1)
    ins |= {"x": _tokens(a["x"]), "consts": consts, "rows": rows, "ctxT": a["ctx_1024"].transpose(2, 0, 1).reshape(P, -1),
            "indices": _tokens(a["L1_ffn_expert_indices"])}
    return ins


def kernel(**inputs):
    import concourse.bacc as bacc
    from concourse.bass_utils import run_bass_kernel_spmd as run

    arrays = _layouts({k: np.asarray(v) for k, v in inputs.items()})
    nc = bacc.Bacc("TRN2", target_bir_lowering=False, num_devices=1)
    used = {k: np.ascontiguousarray(v) for k, v in arrays.items() if not (k[0] == "w" and int(k[1:]) not in SUBLAYERS)}
    ins = {k: nc.dram_tensor(f"{k}_dram", v.shape, mybir.dt.from_np(v.dtype), kind="ExternalInput").ap()
           for k, v in used.items()}
    out = nc.dram_tensor("out_dram", (P, B * NT * D), F32, kind="ExternalOutput").ap()
    build(nc, ins, out)
    r = run(nc, [{f"{k}_dram": v for k, v in used.items()}], core_ids=[0])
    return np.ascontiguousarray(r.results[0]["out_dram"].reshape(P, B, NT, D).transpose(1, 2, 0, 3).reshape(B, S, D))
```

```python
from contextlib import ExitStack

import numpy as np
import concourse.bass as bass
from concourse import mybir

F32 = mybir.dt.float32
I32 = mybir.dt.int32
ALU = mybir.AluOpType
ACT = mybir.ActivationFunctionType
AX = mybir.AxisListType.X

P = 128
D = 128
B = 4
S = 512
NT = S // P
NH = 16
SC = 77
E = 8
BANK = 512
BIG = 3.0e38
SUBLAYERS = range(12)
FIRST_SEM = 200


def columns(*pieces):
    at, out = 0, {}
    for name, n in pieces:
        out[name] = (at, n)
        at += n
    return out, at


CONST, NCONST = columns(("ident", P), ("head8", NH), ("head64", NH), ("expert_no", E), ("minus_half", NT), ("later", 8))
ROPE, NROPE = columns(("cos", S), ("sin", S), ("swap", P), ("causal", NT * S))
PRIOR, NPRIOR = columns(("gauss", NT * S), ("lam", 1))
ATT8, NATT8 = columns(("wq", D), ("wk", D), ("wv", D), ("wo", D), ("bq", 1), ("bk", 1), ("bv", 1))
FAVOR, NFAVOR = columns(("wq", D), ("wk", D), ("wv", D), ("wo", D), ("proj", 32), ("blk", D * 4), ("blkh", NH * 4))
ATT64, NATT64 = columns(("wq", 1024), ("wk", 1024), ("wv", 1024), ("wo", 1024), ("bq", 8), ("bk", 8),
                        ("gamma", D), ("beta", D), ("gate", 1))
TALK, NTALK = columns(("wq", 1024), ("wk", 1024), ("wv", 1024), ("wo", 1024), ("memk", 512), ("memv", 1024),
                      ("pre", P), ("post", P))
FF0, NFF0 = columns(("w1", E * 256), ("w3", E * 256), ("w2", E * 256), ("router", E))
FF1, NFF1 = columns(("w1", E * 512), ("w2", E * 512), ("weights", NT * 2))
FF2, NFF2 = columns(("w1", E * 512), ("w2", E * 512), ("router", E), ("b1", E * 4))
FF3, NFF3 = columns(("w1", 9 * 256), ("w3", 9 * 256), ("w2", 9 * 256), ("router", E))
SELF_ROPE = {**ATT8, **{k: (c + NATT8, n) for k, (c, n) in ROPE.items()}}
SELF_PRIOR = {**ATT8, **{k: (c + NATT8, n) for k, (c, n) in PRIOR.items()}}
ARENA = max(NATT8 + NROPE, NATT8 + NPRIOR, NFAVOR, NATT64, NTALK, NFF0, NFF1, NFF2, NFF3)
ROWS, NROWS = columns(("zero", D), ("x0_bv", D), ("x0_bo", D), ("a1_bo", D), ("x1_bo", D), ("f1_b", D), ("a2_bo", D),
                      ("x2_bv", D), ("x2_bo", D), ("f2_br", E), ("f2_b2", E * D), ("a3_bv", D), ("a3_bo", D),
                      ("x3_bo", D), ("f3_br", E), ("x1_bv", 1024))
WIDTHS = [NATT8 + NROPE, NATT8, NFF0, NFAVOR, NATT64, NFF1, NTALK, NATT8, NFF2, NATT8 + NPRIOR, NATT8, NFF3]


class Core:

    def row(self, name, at=0, n=None):
        c, w = ROWS[name]
        return self.rows[0:1, c + at:c + at + (w if n is None else n)]

    def const(self, name):
        c, w = CONST[name]
        return self.consts[:, c:c + w]


class Chain:

    def __init__(self, engine, sem):
        self.engine, self.sem, self.n = engine, sem, 0

    def done(self, ins):
        ins.then_inc(self.sem, 1)
        self.n += 1

    def wait(self):
        self.engine.wait_ge(self.sem, self.n)


class Step:

    def __init__(self, core, ctx, index, pieces):
        self.core, self.nc, self.ctx, self.index = core, core.nc, ctx, index
        self.pieces = pieces
        if pieces:
            self.w = core.arena[index % 2]
        self.sems = []

    def piece(self, name):
        c, w = self.pieces[name]
        return self.w[:, c:c + w]

    def sb(self, name, shape, dt=F32):
        return self.ctx.enter_context(self.nc.sbuf_tensor(f"{name}_{self.index}", shape, dt))

    def ps(self, name, shape):
        return self.ctx.enter_context(self.nc.psum_tensor(f"{name}_{self.index}", shape, F32))

    def sem(self, name):
        s = self.ctx.enter_context(self.nc.semaphore(f"{name}_{self.index}", num=FIRST_SEM + len(self.sems)))
        self.sems.append(s)
        return s

    def end_pass(self):
        nums = sorted(s.num for s in self.sems)
        assert nums == list(range(nums[0], nums[-1] + 1)), nums
        self.nc.all_engine_barrier(sems_to_clear=range(nums[0], nums[-1] + 1))


def begin(core, index, step):
    nc = core.nc
    with nc.Block() as block:

        @block.sync
        def _(sp):
            k = core.order.index(index)
            if k + 1 < len(core.order):
                nxt = core.order[k + 1]
                sp.dma_start(core.arena[nxt % 2][:, 0:WIDTHS[nxt]], core.packed[nxt]).then_inc(core.arrived[nxt % 2], 16)
            sp.wait_ge(core.arrived[index % 2], 16 * (k // 2 + 1))


class Norm:

    def __init__(self, st, affine=False):
        self.st, self.affine = st, affine
        self.xnT = st.sb("xnT", [P, S])
        self.affine_ready = st.sem("ln_affine_ready")
        self.var_ready = st.sem("ln_var_ready")
        self.rstd_ready = st.sem("ln_rstd_ready")
        self.turned = st.sem("ln_turned")
        self.xnT_ready = st.sem("xnT_ready")
        self.round = 0

    def statistics(self, dve, chain, src):
        core = self.st.core
        for t in range(NT):
            chain.done(dve.bn_stats(core.ln_stats[:, t, :], src[:, t, :]))
        chain.wait()
        for t in range(NT):
            chain.done(dve.bn_aggr(core.ln_mv[:, t, :], core.ln_stats[:, t, :]))
        chain.wait()
        dve.tensor_scalar(core.ln_var[:], core.ln_mv[:, :, 1], 1e-5, None, ALU.add).then_inc(self.var_ready, 1)
        self.round += 1

    def normalise(self, dve, chain, src):
        core = self.st.core
        dve.wait_ge(self.rstd_ready, self.round)
        for t in range(NT):
            chain.done(dve.tensor_scalar(core.xn[:, t, :], src[:, t, :], core.ln_mv[:, t, 0:1], core.ln_rstd[:, t:t + 1],
                                         ALU.subtract, ALU.mult))

    def second(self, dve, chain):
        xn = self.st.core.xn
        self.statistics(dve, chain, xn)
        self.normalise(dve, chain, xn)
        chain.wait()
        for t in range(NT):
            chain.done(dve.tensor_tensor(xn[:, t, :], xn[:, t, :], self.st.piece("gamma"), ALU.mult))
        chain.wait()
        for t in range(NT):
            dve.tensor_tensor(xn[:, t, :], xn[:, t, :], self.st.piece("beta"), ALU.add).then_inc(self.affine_ready, 1)

    def next_statistics(self, dve, chain, b):
        self.statistics(dve, chain, self.st.core.X[:, (b + 1) % B])

    def next_normalise(self, dve, chain, b):
        dve.wait_ge(self.turned, 1)
        self.normalise(dve, chain, self.st.core.X[:, (b + 1) % B])

    def gpsimd(self, pool, rounds=1):
        core = self.st.core
        for r in range(rounds):
            pool.wait_ge(self.var_ready, r + 1)
            pool.tensor_tensor(core.ln_rstd[:], core.ln_var[:], core.const("minus_half"), ALU.pow).then_inc(self.rstd_ready, 1)

    def tensor(self, pe, bank):
        if self.affine:
            pe.wait_ge(self.affine_ready, NT)
        for t in range(NT):
            ins = pe.transpose(bank[:, t * P:(t + 1) * P], self.st.core.xn[:, t, :], self.st.core.const("ident"))
        ins.then_inc(self.turned, 1)

    def scalar(self, act, bank):
        act.wait_ge(self.turned, 1)
        act.activation(self.xnT[:], bank[:, 0:S], ACT.Copy).then_inc(self.xnT_ready, 1)


def normalise_first(core, name):
    with ExitStack() as ctx:
        st = Step(core, ctx, name, {})
        norm = Norm(st)
        done = st.sem("dve_done")
        with core.nc.Block() as block:

            @block.vector
            def _(dve):
                chain = Chain(dve, done)
                norm.statistics(dve, chain, core.X[:, 0])
                norm.normalise(dve, chain, core.X[:, 0])

            @block.gpsimd
            def _(pool):
                norm.gpsimd(pool)

        st.end_pass()


def self_attention(core, index, pieces, rows, rope):
    nc = core.nc
    dh = 8
    scale = float(dh) ** -0.5
    NU = NH * NT
    width = [P * (t + 1) if rope else S for t in range(NT)]
    TURN, KEEP, WEIGH = 4, 4, 8
    NSC, NPR, NPT = 3, 6, 6
    with ExitStack() as ctx:
        st = Step(core, ctx, index, pieces)
        norm = Norm(st)
        QT, KT, VT = st.sb("QT", [P, S]), st.sb("KT", [P, S]), st.sb("VT", [P, S])
        KM = st.sb("KM", [P, NH, S])
        Vt = st.sb("Vt", [P, NT, D])
        raw = st.sb("raw", [P, 2, S])
        rot = st.sb("rot", [P, 2, S])
        addend = st.sb("addend", [P, NT, S])
        sc = st.sb("sc", [P, NSC, S])
        pr = st.sb("pr", [P, NPR, S])
        PTs = st.sb("PTs", [P, NPT, S])
        low = st.sb("low", [P, NU])
        den, rden = st.sb("den", [P, NH, NT]), st.sb("rden", [P, NH, NT])
        O, OT = st.sb("O", [P, NT, D]), st.sb("OT", [P, S])
        ps_s = st.ps("ps_s", [P, 3, BANK])
        ps_t = st.ps("ps_t", [P, 3, BANK])
        ps_o = st.ps("ps_o", [P, BANK])
        ps_m = st.ps("ps_m", [P, BANK])
        dve_done = st.sem("dve_done")
        qkv_made, qkv_kept, swapped = st.sem("qkv_made"), st.sem("qkv_kept"), st.sem("swapped")
        keys_ready = st.sem("keys_ready")
        scored, shifted = st.sem("scored"), st.sem("shifted")
        exped, turned, kept_a, kept_v, weighted = (st.sem(n) for n in ("exped", "turned", "kept_a", "kept_v", "weighted"))
        o_ready, o_turned, oT_ready, out_made, v_turned, v_ready = (st.sem(n) for n in (
            "o_ready", "o_turned", "oT_ready", "out_made", "v_turned", "v_ready"))
        ident = core.const("ident")
        begin(core, index, st)
        if rope:
            addend_v = st.piece("causal").rearrange("p (t s) -> p t s", t=NT)
        else:
            addend_v = addend
            with nc.Block() as block:

                @block.vector
                def _(dve):
                    gauss = st.piece("gauss").rearrange("p (t s) -> p t s", t=NT)
                    for t in range(NT):
                        dve.tensor_scalar(addend[:, t, :], gauss[:, t, :], st.piece("lam"), -1.0, ALU.mult, ALU.mult)

        def kept(engine, u):
            engine.wait_ge(kept_v if u % 2 else kept_a, u // 2 + 1)

        with nc.Fori(0, B) as b:
            with nc.Block() as block:

                @block.gpsimd
                def _(pool):
                    norm.gpsimd(pool)

                @block.tensor
                def _(pe):
                    norm.tensor(pe, ps_m)
                    pe.wait_ge(norm.xnT_ready, 1)
                    for name, bank in (("wk", ps_s[:, 1, :]), ("wq", ps_s[:, 0, :]), ("wv", ps_s[:, 2, :])):
                        pe.matmul(bank, st.piece(name), norm.xnT[:], start=True, stop=True).then_inc(qkv_made, 1)
                    if rope:
                        for i in (1, 0):
                            pe.wait_ge(qkv_kept, 2 - i)
                            pe.matmul(ps_t[:, i, :], st.piece("swap"), raw[:, i, :], start=True, stop=True).then_inc(swapped, 1)
                    pe.wait_ge(qkv_kept, 3)
                    for t in range(NT):
                        ins = pe.transpose(ps_m[:, t * P:(t + 1) * P], VT[:, t * P:(t + 1) * P], ident)
                    ins.then_inc(v_turned, 1)
                    for step in range(NU + WEIGH):
                        u = step
                        if u < NU:
                            h, t = divmod(u, NT)
                            if t == 0:
                                pe.wait_ge(keys_ready, h + 1 + (1 if rope else 0))
                            if u >= 3:
                                pe.wait_ge(shifted, u - 2)
                            pe.matmul(ps_s[:, u % 3, 0:width[t]], QT[:, t * P:(t + 1) * P], KM[:, h, 0:width[t]],
                                      start=True, stop=True).then_inc(scored, 1)
                        u = step - TURN
                        if 0 <= u < NU:
                            t = u % NT
                            pe.wait_ge(exped, u + 1)
                            if u >= 3:
                                kept(pe, u - 3)
                            for k in range(width[t] // P):
                                ins = pe.transpose(ps_t[:, u % 3, k * P:(k + 1) * P], pr[:, u % NPR, k * P:(k + 1) * P], ident)
                            ins.then_inc(turned, 1)
                        u = step - WEIGH
                        if u >= 0:
                            h, t = divmod(u, NT)
                            if u == 0:
                                pe.wait_ge(v_ready, 1)
                            kept(pe, u)
                            n = width[t] // P
                            for k in range(n):
                                ins = pe.matmul(ps_o[:, t * D + h * dh:t * D + (h + 1) * dh], PTs[:, u % NPT, k * P:(k + 1) * P],
                                                Vt[:, k, h * dh:(h + 1) * dh], start=(k == 0), stop=(k == n - 1))
                            ins.then_inc(weighted, 1)
                    for t in range(NT):
                        pe.wait_ge(o_ready, t + 1)
                        ins = pe.transpose(ps_m[:, t * P:(t + 1) * P], O[:, t, :], ident)
                    ins.then_inc(o_turned, 1)
                    pe.wait_ge(oT_ready, 1)
                    for t in range(NT):
                        pe.matmul(ps_s[:, 0, t * D:(t + 1) * D], OT[:, t * P:(t + 1) * P], st.piece("wo"), start=True, stop=False)
                        ins = pe.matmul(ps_s[:, 0, t * D:(t + 1) * D], core.ones[:, :], core.row(rows["bo"]), start=False, stop=True)
                    ins.then_inc(out_made, 1)

                @block.scalar
                def _(act):
                    norm.scalar(act, ps_m)
                    dest = (raw[:, 0, :], raw[:, 1, :]) if rope else (QT[:], KT[:])
                    for n, i in enumerate((1, 0)):
                        act.wait_ge(qkv_made, n + 1)
                        act.activation(dest[i], ps_s[:, i, :], ACT.Identity, bias=st.piece(("bq", "bk")[i])).then_inc(qkv_kept, 1)
                    act.wait_ge(qkv_made, 3)
                    act.activation(VT[:], ps_s[:, 2, :], ACT.Identity, bias=st.piece("bv")).then_inc(qkv_kept, 1)
                    for step in range(NU + KEEP):
                        u = step
                        if u < NU:
                            h, t = divmod(u, NT)
                            act.wait_ge(shifted, u + 1)
                            if u >= NPR:
                                act.wait_ge(turned, u - NPR + 1)
                            act.activation(pr[:, u % NPR, 0:width[t]], sc[:, u % NSC, 0:width[t]], ACT.Exp,
                                           bias=low[:, u:u + 1], scale=-1.0, accum_out=den[:, h, t:t + 1]).then_inc(exped, 1)
                        u = step - KEEP
                        if u >= 0 and u % 2 == 0:
                            act.wait_ge(turned, u + 1)
                            if u >= NPT:
                                act.wait_ge(weighted, u - NPT + 1)
                            n = width[u % NT]
                            act.activation(PTs[:, u % NPT, 0:n], ps_t[:, u % 3, 0:n], ACT.Copy).then_inc(kept_a, 1)
                    act.wait_ge(o_turned, 1)
                    act.activation(OT[:], ps_m[:], ACT.Copy).then_inc(oT_ready, 1)

                @block.vector
                def _(dve):
                    chain = Chain(dve, dve_done)
                    if rope:
                        for n, i in enumerate((1, 0)):
                            dve.wait_ge(qkv_kept, n + 1)
                            chain.done(dve.tensor_tensor((QT, KT)[i][:], raw[:, i, :], st.piece("cos"), ALU.mult))
                            dve.wait_ge(swapped, n + 1)
                            chain.done(dve.tensor_tensor(rot[:, i, :], ps_t[:, i, :], st.piece("sin"), ALU.mult))
                        chain.wait()
                        chain.done(dve.tensor_tensor(KT[:], KT[:], rot[:, 1, :], ALU.add))
                        dve.tensor_tensor(QT[:], QT[:], rot[:, 0, :], ALU.add).then_inc(keys_ready, 1)
                        chain.wait()
                    else:
                        dve.wait_ge(qkv_kept, 2)

                    def mask_keys(h):
                        dve.tensor_scalar(KM[:, h, :], KT[:], core.const("head8")[:, h:h + 1], -scale, ALU.mult,
                                          ALU.mult).then_inc(keys_ready, 1)

                    mask_keys(0)
                    mask_keys(1)
                    dve.wait_ge(v_turned, 1)
                    dve.tensor_copy(Vt[:].rearrange("p t d -> p (t d)"), ps_m[:]).then_inc(v_ready, 1)
                    for step in range(NU + KEEP):
                        u = step
                        if u < NU:
                            h, t = divmod(u, NT)
                            if t == 0 and h + 2 < NH:
                                mask_keys(h + 2)
                            dve.wait_ge(scored, u + 1)
                            if u >= NSC:
                                dve.wait_ge(exped, u - NSC + 1)
                            dve.tensor_tensor_reduce(sc[:, u % NSC, 0:width[t]], ps_s[:, u % 3, 0:width[t]],
                                                     addend_v[:, t, 0:width[t]], 1.0, BIG, ALU.add, ALU.min,
                                                     low[:, u:u + 1]).then_inc(shifted, 1)
                        u = step - KEEP
                        if u >= 0 and u % 2 == 1:
                            dve.wait_ge(turned, u + 1)
                            if u >= NPT:
                                dve.wait_ge(weighted, u - NPT + 1)
                            n = width[u % NT]
                            dve.tensor_copy(PTs[:, u % NPT, 0:n], ps_t[:, u % 3, 0:n]).then_inc(kept_v, 1)
                        if step == NU - 8:
                            norm.next_statistics(dve, chain, b)
                        if step == NU - 4:
                            norm.next_normalise(dve, chain, b)
                    dve.wait_ge(exped, NU)
                    chain.done(dve.reciprocal(rden[:].rearrange("p h t -> p (h t)"), den[:].rearrange("p h t -> p (h t)")))
                    chain.wait()
                    dve.wait_ge(weighted, NU)
                    ov = O[:].rearrange("p t (h d) -> p t h d", h=NH)
                    pv = ps_o[:].rearrange("p (t h d) -> p t h d", t=NT, h=NH)
                    for t in range(NT):
                        dve.tensor_tensor(ov[:, t], pv[:, t], rden[:, :, t].unsqueeze(2).to_broadcast([P, NH, dh]),
                                          ALU.mult).then_inc(o_ready, 1)
                    dve.wait_ge(out_made, 1)
                    x = core.X[:, b].rearrange("p t d -> p (t d)")
                    dve.tensor_tensor(x, ps_s[:, 0, :], x, ALU.add)

            st.end_pass()


def cross_attention(core, index, pieces, rows, dh):
    nc = core.nc
    NJ = NH * dh // P
    scale = float(dh) ** -0.5
    wide = dh == 64
    G = 4
    head_mask = "head64" if wide else "head8"
    with ExitStack() as ctx:
        st = Step(core, ctx, index, pieces)
        norm = Norm(st, affine=wide)
        cT = st.sb("cT", [P, SC])
        QT = st.sb("QT", [P, NJ, S])
        KM = st.sb("KM", [P, NH, SC])
        V = st.sb("V", [SC, NJ * P])
        sc = st.sb("sc", [P, 2, NH, SC])
        pr = st.sb("pr", [P, 2, NH, SC])
        PTs = st.sb("PTs", [SC, 2, NH, P])
        mx, den, rden = st.sb("mx", [P, NT, NH]), st.sb("den", [P, NT, NH]), st.sb("rden", [P, NT, NH])
        O, OT = st.sb("O", [P, 2, NJ * P]), st.sb("OT", [P, 2, NJ, P])
        gate = st.sb("gate", [P, 1])
        ps_s = st.ps("ps_s", [P, 4, BANK])
        ps_t = st.ps("ps_t", [P, 2, BANK])
        ps_o = st.ps("ps_o", [P, 2, BANK])
        dve_done = st.sem("dve_done")
        ctx_ready, q_made, q_kept, k_made, k_kept, v_made, v_kept = (st.sem(n) for n in (
            "ctx_ready", "q_made", "q_kept", "k_made", "k_kept", "v_made", "v_kept"))
        scored, shifted, exped, summed, turned, kept = (st.sem(n) for n in (
            "scored", "shifted", "exped", "summed", "turned", "kept"))
        weighted, o_ready, o_turned, oT_ready, out_made, added = (st.sem(n) for n in (
            "weighted", "o_ready", "o_turned", "oT_ready", "out_made", "added"))
        ident = core.const("ident")
        begin(core, index, st)
        if wide:
            with nc.Block() as block:

                @block.scalar
                def _(act):
                    act.activation(gate[:], st.piece("gate"), ACT.Tanh)

        def weight(name, j):
            c, _ = pieces[name]
            return st.w[:, c + j * P:c + (j + 1) * P]

        NO = max(1, NJ // 4)
        with nc.Fori(0, B) as b:
            with nc.Block() as block:

                @block.gpsimd
                def _(pool):
                    norm.gpsimd(pool, 2 if wide else 1)

                @block.tensor
                def _(pe):
                    pe.wait_ge(ctx_ready, 1)
                    for j in range(NJ):
                        if j >= 2:
                            pe.wait_ge(k_kept, (j - 1) * (NH // NJ))
                        pe.matmul(ps_o[:, j % 2, 0:SC], weight("wk", j), cT[:], start=True, stop=True).then_inc(k_made, 1)
                    n = min(BANK, NJ * P)
                    c, _ = pieces["wv"]
                    for j in range(NJ * P // n):
                        pe.matmul(ps_s[0:SC, j, 0:n], cT[:], st.w[:, c + j * n:c + (j + 1) * n], start=True, stop=False)
                        pe.matmul(ps_s[0:SC, j, 0:n], core.ones[:, 0:SC], core.row(rows["bv"], j * n, n),
                                  start=False, stop=True).then_inc(v_made, 1)
                    norm.tensor(pe, ps_t[:, 0, :])
                    pe.wait_ge(norm.xnT_ready, 1)
                    for j in range(NJ):
                        if j >= 2:
                            pe.wait_ge(q_kept, j - 1)
                        pe.matmul(ps_s[:, 2 + j % 2, :], weight("wq", j), norm.xnT[:], start=True, stop=True).then_inc(q_made, 1)
                    pe.wait_ge(k_kept, NH)
                    pe.wait_ge(v_kept, NJ * P // n)
                    pe.wait_ge(q_kept, NJ)

                    def scores(t):
                        if t >= 1:
                            pe.wait_ge(shifted, t)
                        for g in range(NH // G):
                            if wide:
                                for h in range(g * G, (g + 1) * G):
                                    ins = pe.matmul(ps_s[:, g, (h % G) * SC:(h % G + 1) * SC], QT[:, h // 2, t * P:(t + 1) * P],
                                                    KM[:, h, :], start=True, stop=True)
                            else:
                                ins = pe.matmul(ps_s[:, g, 0:G * SC], QT[:, 0, t * P:(t + 1) * P],
                                                KM[:, g * G:(g + 1) * G, :].rearrange("p h s -> p (h s)"), start=True, stop=True)
                        ins.then_inc(scored, 1)

                    def turn(t):
                        pe.wait_ge(exped, t + 1)
                        for g in range(NH // G):
                            i = t * 4 + g
                            if i >= 2:
                                pe.wait_ge(kept, i - 1)
                            for h in range(g * G, (g + 1) * G):
                                ins = pe.transpose(ps_t[0:SC, i % 2, (h % G) * P:(h % G + 1) * P], pr[:, t % 2, h, :], ident)
                            ins.then_inc(turned, 1)

                    def weigh(t):
                        pe.wait_ge(kept, 4 * (t + 1))
                        if t >= 1:
                            pe.wait_ge(o_ready, t)
                        for h in range(NH):
                            at = h * dh
                            ins = pe.matmul(ps_o[:, at // BANK, at % BANK:at % BANK + dh], PTs[:, t % 2, h, :],
                                            V[:, at:at + dh], start=True, stop=True)
                        ins.then_inc(weighted, 1)

                    def project(t):
                        pe.wait_ge(o_ready, t + 1)
                        if t >= 1:
                            pe.wait_ge(added, t)
                        pe.wait_ge(kept, min(4 * (t + 2), 4 * NT))
                        for g in range(NO):
                            for j in range(g * 4, min((g + 1) * 4, NJ)):
                                ins = pe.transpose(ps_t[:, g, (j % 4) * P:(j % 4 + 1) * P], O[:, t % 2, j * P:(j + 1) * P], ident)
                        ins.then_inc(o_turned, 1)
                        pe.wait_ge(oT_ready, t + 1)
                        for j in range(NJ):
                            pe.matmul(ps_t[:, 0, 0:D], OT[:, t % 2, j, :], weight("wo", j), start=(j == 0), stop=False)
                        pe.matmul(ps_t[:, 0, 0:D], core.ones[:, :], core.row(rows["bo"]), start=False, stop=True).then_inc(out_made, 1)

                    scores(0)
                    for t in range(NT + 1):
                        if t < NT:
                            if t >= 2:
                                pe.wait_ge(added, t - 1)
                            turn(t)
                            if t + 1 < NT:
                                scores(t + 1)
                            weigh(t)
                        if t >= 1:
                            if t < NT:
                                pe.wait_ge(kept, 4 * (t + 1))
                            project(t - 1)

                @block.scalar
                def _(act):
                    act.activation(cT[:], core.ctxT[:, b], ACT.Copy).then_inc(ctx_ready, 1)
                    n = min(BANK, NJ * P)
                    for j in range(NJ * P // n):
                        act.wait_ge(v_made, j + 1)
                        act.activation(V[:, j * n:(j + 1) * n], ps_s[0:SC, j, 0:n], ACT.Copy).then_inc(v_kept, 1)
                    norm.scalar(act, ps_t[:, 0, :])
                    for j in range(NJ):
                        act.wait_ge(q_made, j + 1)
                        act.activation(QT[:, j, :], ps_s[:, 2 + j % 2, :], ACT.Identity, bias=st.piece("bq")[:, j:j + 1]).then_inc(q_kept, 1)
                    for t in range(NT + 1):
                        if t < NT:
                            act.wait_ge(shifted, t + 1)
                            if t >= 2:
                                act.wait_ge(turned, 4 * (t - 1))
                                act.wait_ge(summed, t - 1)
                            act.activation(pr[:, t % 2], sc[:, t % 2], ACT.Exp, scale=scale).then_inc(exped, 1)
                            for g in range(NH // G):
                                act.wait_ge(turned, 4 * t + g + 1)
                                if t >= 2:
                                    act.wait_ge(weighted, t - 1)
                                act.activation(PTs[:, t % 2, g * G:(g + 1) * G, :].rearrange("p h s -> p (h s)"),
                                               ps_t[0:SC, (4 * t + g) % 2, :], ACT.Copy).then_inc(kept, 1)
                        if t >= 1:
                            act.wait_ge(o_turned, t)
                            for g in range(NO):
                                m = min(4, NJ)
                                ins = act.activation(OT[:, (t - 1) % 2, g * 4:g * 4 + m, :].rearrange("p j s -> p (j s)"),
                                                     ps_t[:, g, 0:m * P], ACT.Copy)
                            ins.then_inc(oT_ready, 1)

                @block.vector
                def _(dve):
                    chain = Chain(dve, dve_done)
                    for j in range(NJ):
                        dve.wait_ge(k_made, j + 1)
                        for h in range(j * (NH // NJ), (j + 1) * (NH // NJ)):
                            dve.tensor_scalar(KM[:, h, :], ps_o[:, j % 2, 0:SC], st.piece("bk")[:, j:j + 1],
                                              core.const(head_mask)[:, h:h + 1], ALU.add, ALU.mult).then_inc(k_kept, 1)
                    if wide:
                        norm.second(dve, chain)

                    def shift(t):
                        dve.wait_ge(scored, t + 1)
                        v = ps_s[:, :, 0:G * SC].rearrange("p g (h s) -> p g h s", h=G)
                        chain.done(dve.tensor_reduce(mx[:, t, :].rearrange("p (g h) -> p g h", g=NH // G), v, AX, ALU.max))
                        chain.wait()
                        if t >= 2:
                            dve.wait_ge(exped, t - 1)
                        top = mx[:, t, :].rearrange("p (g h) -> p g h", g=NH // G).unsqueeze(3).to_broadcast([P, NH // G, G, SC])
                        dve.tensor_tensor(sc[:, t % 2].rearrange("p (g h) s -> p g h s", g=NH // G), v, top,
                                          ALU.subtract).then_inc(shifted, 1)

                    def normalise(t):
                        dve.wait_ge(exped, t + 1)
                        dve.tensor_reduce(den[:, t, :], pr[:, t % 2], AX, ALU.add).then_inc(summed, 1)
                        dve.wait_ge(summed, t + 1)
                        chain.done(dve.reciprocal(rden[:, t, :], den[:, t, :]))
                        chain.wait()
                        dve.wait_ge(weighted, t + 1)
                        if t >= 2:
                            dve.wait_ge(o_turned, t - 1)
                        src = ps_o[:].rearrange("p c n -> p (c n)")[:, 0:NJ * P].rearrange("p (h d) -> p h d", h=NH)
                        dve.tensor_tensor(O[:, t % 2].rearrange("p (h d) -> p h d", h=NH), src,
                                          rden[:, t, :].unsqueeze(2).to_broadcast([P, NH, dh]), ALU.mult).then_inc(o_ready, 1)

                    shift(0)
                    for t in range(NT + 1):
                        if t + 1 < NT:
                            shift(t + 1)
                        if t < NT:
                            normalise(t)
                        if t == 1:
                            norm.next_statistics(dve, chain, b)
                        if t == 2:
                            norm.next_normalise(dve, chain, b)
                        if t >= 1:
                            x = core.X[:, b, t - 1, :]
                            dve.wait_ge(out_made, t)
                            if wide:
                                dve.scalar_tensor_tensor(x, ps_t[:, 0, 0:D], gate[:], x, ALU.mult, ALU.add).then_inc(added, 1)
                            else:
                                dve.tensor_tensor(x, ps_t[:, 0, 0:D], x, ALU.add).then_inc(added, 1)

            st.end_pass()


def feed_forward(core, index, pieces, routing):
    nc = core.nc
    gated = "w3" in pieces
    NE = pieces["w1"][1] // (256 if gated else 512)
    H = pieces["w1"][1] // NE
    NK = H // P
    given = routing == "given"
    passes = 1 if given else B
    picks = {"softmax2": 2, "top2softmax": 2, "argmax": 1, "given": 0}[routing]
    with ExitStack() as ctx:
        st = Step(core, ctx, index, pieces)
        norm = Norm(st)
        hT = st.sb("hT", [P, 2, NK, S])
        act_h = st.sb("act_h", [P, 2, S])
        logit = st.sb("logit", [P, NT, 15])
        top = st.sb("top", [P, NT, 8])
        hit = st.sb("hit", [P, NT, 15])
        e_x = st.sb("e_x", [P, NT, E])
        small = st.sb("small", [P, 3, NT])
        cw = st.sb("cw", [P, NT, NE])
        idx = st.sb("idx", [P, NT, 2])
        cw2 = st.sb("cw2", [P, NT, E])
        ps_r = st.ps("ps_r", [P, BANK])
        ps_a = st.ps("ps_a", [P, 2, BANK])
        ps_g = st.ps("ps_g", [P, 2, BANK])
        ps_y = st.ps("ps_y", [P, 2, BANK])
        dve_done = st.sem("dve_done")
        routed, lx_ready, ex_ready, up_made, act_made, hid_ready, down_made, added = (st.sem(n) for n in (
            "routed", "lx_ready", "ex_ready", "up_made", "act_made", "hid_ready", "down_made", "added"))
        begin(core, index, st)

        def w_up(name, e, k):
            c, _ = pieces[name]
            return st.w[:, c + (e * NK + k) * P:c + (e * NK + k + 1) * P]

        with nc.Fori(0, passes) as b:
            with nc.Block() as block:

                @block.gpsimd
                def _(pool):
                    norm.gpsimd(pool, 0 if given else 1)

                @block.tensor
                def _(pe):
                    norm.tensor(pe, ps_r)
                    pe.wait_ge(norm.xnT_ready, 1)
                    if not given:
                        c, _ = pieces["router"]
                        for t in range(NT):
                            bias = {"argmax": "f2_br", "top2softmax": "f3_br"}.get(routing)
                            ins = pe.matmul(ps_r[:, t * E:(t + 1) * E], norm.xnT[:, t * P:(t + 1) * P], st.w[:, c:c + E],
                                            start=True, stop=bias is None)
                            if bias:
                                ins = pe.matmul(ps_r[:, t * E:(t + 1) * E], core.ones[:, :], core.row(bias), start=False, stop=True)
                        ins.then_inc(routed, 1)

                    def up(e, k):
                        i = e * NK + k
                        if i >= 2:
                            pe.wait_ge(hid_ready, i - 1)
                        ins = pe.matmul(ps_a[:, i % 2, :], w_up("w1", e, k), norm.xnT[:], start=True, stop=True)
                        if gated:
                            ins = pe.matmul(ps_g[:, i % 2, :], w_up("w3", e, k), norm.xnT[:], start=True, stop=True)
                        ins.then_inc(up_made, 1)

                    def down(e):
                        pe.wait_ge(hid_ready, (e + 1) * NK)
                        if e >= 2:
                            pe.wait_ge(added, NT * (e - 1))
                        for t in range(NT):
                            for k in range(NK):
                                ins = pe.matmul(ps_y[:, e % 2, t * D:(t + 1) * D], hT[:, e % 2, k, t * P:(t + 1) * P],
                                                w_up("w2", e, k), start=(k == 0), stop=(k == NK - 1 and routing != "argmax"))
                            if routing == "argmax":
                                ins = pe.matmul(ps_y[:, e % 2, t * D:(t + 1) * D], core.ones[:, :],
                                                core.row("f2_b2", e * D, D), start=False, stop=True)
                        ins.then_inc(down_made, 1)

                    for e in range(NE + 1):
                        for k in range(NK):
                            if e < NE:
                                up(e, k)
                            if k == 0 and e >= 1:
                                down(e - 1)

                @block.scalar
                def _(act):
                    norm.scalar(act, ps_r)
                    if routing in ("softmax2", "top2softmax"):
                        act.wait_ge(lx_ready, 1)
                        act.activation(e_x[:], e_x[:], ACT.Exp).then_inc(ex_ready, 1)
                    for e in range(NE):
                        for k in range(NK):
                            i = e * NK + k
                            act.wait_ge(up_made, i + 1)
                            if gated:
                                if i >= 2:
                                    act.wait_ge(hid_ready, i - 1)
                                act.activation(act_h[:, i % 2, :], ps_a[:, i % 2, :], ACT.Silu).then_inc(act_made, 1)
                            else:
                                if e >= 2:
                                    act.wait_ge(down_made, e - 1)
                                bias = st.piece("b1")[:, i:i + 1] if "b1" in pieces else 0.0
                                act.activation(hT[:, e % 2, k, :], ps_a[:, i % 2, :], ACT.Gelu, bias=bias).then_inc(hid_ready, 1)

                @block.vector
                def _(dve):
                    chain = Chain(dve, dve_done)
                    if NE > E:
                        chain.done(dve.memset(cw[:, :, E:NE], 1.0))
                    if given:
                        wt = st.piece("weights").rearrange("p (t k) -> p t k", t=NT)
                        chain.done(dve.tensor_copy(idx[:], core.indices[:]))
                        chain.wait()
                        for t in range(NT):
                            chain.done(dve.tensor_scalar(cw[:, t, :], core.const("expert_no"), idx[:, t, 0:1], wt[:, t, 0:1], ALU.is_equal, ALU.mult))
                            chain.done(dve.tensor_scalar(cw2[:, t, :], core.const("expert_no"), idx[:, t, 1:2], wt[:, t, 1:2], ALU.is_equal, ALU.mult))
                        chain.wait()
                        chain.done(dve.tensor_tensor(cw[:], cw[:], cw2[:], ALU.add))
                        chain.wait()
                    else:
                        chain.done(dve.memset(logit[:, :, E:15], -BIG))
                        dve.wait_ge(routed, 1)
                        chain.done(dve.tensor_copy(logit[:, :, 0:E], ps_r[:, 0:NT * E].rearrange("p (t e) -> p t e", t=NT)))
                        chain.wait()

                        def softmax():
                            chain.done(dve.tensor_reduce(small[:, 0, :], e_src(), AX, ALU.max))
                            chain.wait()
                            dve.tensor_tensor(e_x[:], e_src(), small[:, 0, :].unsqueeze(2).to_broadcast([P, NT, E]),
                                              ALU.subtract).then_inc(lx_ready, 1)
                            dve.wait_ge(ex_ready, 1)
                            chain.done(dve.tensor_reduce(small[:, 1, :], e_x[:], AX, ALU.add))
                            chain.wait()
                            chain.done(dve.reciprocal(small[:, 2, :], small[:, 1, :]))
                            chain.wait()
                            chain.done(dve.tensor_tensor(softmax_out(), e_x[:], small[:, 2, :].unsqueeze(2).to_broadcast([P, NT, E]), ALU.mult))
                            chain.wait()

                        def choose():
                            for t in range(NT):
                                chain.done(dve.max(top[:, t, :], logit[:, t, 0:E]))
                            chain.wait()
                            chain.done(dve.memset(top[:, :, picks:8], -BIG))
                            chain.wait()
                            for t in range(NT):
                                chain.done(dve.match_replace(hit[:, t, 0:15], top[:, t, :], logit[:, t, :], BIG))
                            chain.wait()
                            chain.done(dve.tensor_scalar(hit[:, :, 0:E], hit[:, :, 0:E], BIG, None, ALU.is_ge))
                            chain.wait()

                        if routing == "softmax2":
                            e_src = softmax_out = lambda: logit[:, :, 0:E]
                            softmax()
                            choose()
                            chain.done(dve.tensor_tensor(cw[:, :, 0:E], hit[:, :, 0:E], logit[:, :, 0:E], ALU.mult))
                        elif routing == "top2softmax":
                            choose()
                            chain.done(dve.tensor_scalar(cw2[:], hit[:, :, 0:E], BIG, BIG, ALU.mult, ALU.subtract))
                            chain.done(dve.tensor_tensor(logit[:, :, 0:E], logit[:, :, 0:E], hit[:, :, 0:E], ALU.mult))
                            chain.wait()
                            chain.done(dve.tensor_tensor(logit[:, :, 0:E], logit[:, :, 0:E], cw2[:], ALU.add))
                            chain.wait()
                            e_src = lambda: logit[:, :, 0:E]
                            softmax_out = lambda: cw[:, :, 0:E]
                            softmax()
                        else:
                            choose()
                            chain.done(dve.tensor_copy(cw[:], hit[:, :, 0:E]))
                        chain.wait()

                    def accumulate(e):
                        dve.wait_ge(down_made, e + 1)
                        for t in range(NT):
                            x = core.X[:, b, t, :]
                            if e >= 1:
                                dve.wait_ge(added, NT * (e - 1) + t + 1)
                            dve.scalar_tensor_tensor(x, ps_y[:, e % 2, t * D:(t + 1) * D], cw[:, t, e:e + 1], x,
                                                     ALU.mult, ALU.add).then_inc(added, 1)

                    for e in range(NE):
                        if gated:
                            for k in range(NK):
                                i = e * NK + k
                                dve.wait_ge(act_made, i + 1)
                                if e >= 2:
                                    dve.wait_ge(down_made, e - 1)
                                dve.tensor_tensor(hT[:, e % 2, k, :], act_h[:, i % 2, :], ps_g[:, i % 2, :], ALU.mult).then_inc(hid_ready, 1)
                        if e >= 1:
                            accumulate(e - 1)
                        if e == 4 and not given:
                            norm.next_statistics(dve, chain, b)
                        if e == 5 and not given:
                            norm.next_normalise(dve, chain, b)
                    accumulate(NE - 1)

            st.end_pass()
        if given:
            with nc.Block() as block:

                @block.tensor
                def _(pe):
                    pe.matmul(ps_r[:, 0:D], core.ones[:, :], core.row("f1_b"), start=True, stop=True).then_inc(routed, 1)

                @block.vector
                def _(dve):
                    dve.wait_ge(routed, 1)
                    x = core.X[:].rearrange("p b t d -> p (b t) d")
                    dve.tensor_tensor(x, ps_r[:, 0:D].unsqueeze(1).to_broadcast([P, B * NT, D]), x, ALU.add)

            st.end_pass()
    if given:
        normalise_first(core, f"after_{index}")


def favor_attention(core, index):
    nc = core.nc
    pieces = FAVOR
    dh, M = 8, 32
    EPS = 1e-6
    F = NH * M
    NF = F // P
    with ExitStack() as ctx:
        st = Step(core, ctx, index, pieces)
        norm = Norm(st)
        proj = st.sb("proj", [P, NH, M])
        qkT = st.sb("qkT", [P, 2, S])
        sq = st.sb("sq", [P, 2, S])
        V1 = st.sb("V1", [P, NT, D + 1])
        sh = st.sb("sh", [P, 2, F])
        ph = st.sb("ph", [P, 2, F])
        phi = st.sb("phi", [P, 2, NT, F])
        mx, cc = st.sb("mx", [P, 2, NT, NH]), st.sb("cc", [P, 2, NT, NH])
        phT = st.sb("phT", [P, 2, NF, P])
        KV = st.sb("KV", [P, NF, D + NH])
        rden = st.sb("rden", [P, NT, NH])
        O, OT = st.sb("O", [P, NT, D]), st.sb("OT", [P, S])
        ps_f = st.ps("ps_f", [P, 2, BANK])
        ps_n = st.ps("ps_n", [P, BANK])
        ps_k = st.ps("ps_k", [P, 2, BANK])
        ps_t = st.ps("ps_t", [P, BANK])
        ps_o = st.ps("ps_o", [P, 2, BANK])
        dve_done = st.sem("dve_done")
        qkv_made, qkv_kept, v_turned, v_ready, n_made, f_made = (st.sem(n) for n in (
            "qkv_made", "qkv_kept", "v_turned", "v_ready", "n_made", "f_made"))
        shifted, exped, phi_ready, kv_made, kv_kept, kv_ready = (st.sem(n) for n in (
            "shifted", "exped", "phi_ready", "kv_made", "kv_kept", "kv_ready"))
        q_turned, qT_ready, weighted, o_ready, o_turned, oT_ready, out_made = (st.sem(n) for n in (
            "q_turned", "qT_ready", "weighted", "o_ready", "o_turned", "oT_ready", "out_made"))
        ident = core.const("ident")
        begin(core, index, st)
        with nc.Block() as block:

            @block.vector
            def _(dve):
                for h in range(NH):
                    dve.tensor_scalar(proj[:, h, :], st.piece("proj"), core.const("head8")[:, h:h + 1], None, ALU.mult)
                for t in range(NT):
                    dve.memset(V1[:, t, D:D + 1], 1.0)

        with nc.Fori(0, B) as b:
            with nc.Block() as block:

                @block.gpsimd
                def _(pool):
                    norm.gpsimd(pool)

                @block.tensor
                def _(pe):
                    norm.tensor(pe, ps_t)
                    pe.wait_ge(norm.xnT_ready, 1)
                    for name, bank in (("wk", ps_f[:, 0, :]), ("wq", ps_f[:, 1, :]), ("wv", ps_k[:, 0, :])):
                        pe.matmul(bank, st.piece(name), norm.xnT[:], start=True, stop=True).then_inc(qkv_made, 1)
                    pe.wait_ge(qkv_kept, 5)
                    for t in range(NT):
                        ins = pe.transpose(ps_t[:, t * P:(t + 1) * P], O[:, t, :], ident)
                    ins.then_inc(v_turned, 1)
                    for i in range(2):
                        for t in range(NT):
                            ins = pe.matmul(ps_n[:, (i * NT + t) * NH:(i * NT + t + 1) * NH], sq[:, i, t * P:(t + 1) * P],
                                            core.const("head8"), start=True, stop=True)
                    ins.then_inc(n_made, 1)
                    for u in range(2 * NT):
                        i, t = divmod(u, NT)
                        if u >= 2:
                            pe.wait_ge(shifted, u - 1)
                        pe.matmul(ps_f[:, u % 2, :], qkT[:, i, t * P:(t + 1) * P], proj[:].rearrange("p h m -> p (h m)"),
                                  start=True, stop=True).then_inc(f_made, 1)
                    pe.wait_ge(phi_ready, NT)
                    pe.wait_ge(v_ready, 1)
                    for j in range(NF):
                        if j >= 2:
                            pe.wait_ge(kv_kept, j - 1)
                        for t in range(NT):
                            ins = pe.matmul(ps_k[:, j % 2, 0:D + 1], phi[:, 0, t, j * P:(j + 1) * P], V1[:, t, :],
                                            start=(t == 0), stop=(t == NT - 1))
                        ins.then_inc(kv_made, 1)
                    for t in range(NT):
                        pe.wait_ge(phi_ready, NT + t + 1)
                        if t >= 1:
                            pe.wait_ge(qT_ready, t)
                        for j in range(NF):
                            ins = pe.transpose(ps_t[:, j * P:(j + 1) * P], phi[:, 1, t, j * P:(j + 1) * P], ident)
                        ins.then_inc(q_turned, 1)
                        pe.wait_ge(kv_ready, NF)
                        pe.wait_ge(kv_kept, NF)
                        pe.wait_ge(qT_ready, t + 1)
                        if t >= 2:
                            pe.wait_ge(o_ready, t - 1)
                        for j in range(NF):
                            ins = pe.matmul(ps_o[:, t % 2, 0:D + NH], phT[:, t % 2, j, :], KV[:, j, :],
                                            start=(j == 0), stop=(j == NF - 1))
                        ins.then_inc(weighted, 1)
                    pe.wait_ge(o_ready, NT)
                    for t in range(NT):
                        ins = pe.transpose(ps_t[:, t * P:(t + 1) * P], O[:, t, :], ident)
                    ins.then_inc(o_turned, 1)
                    pe.wait_ge(oT_ready, 1)
                    for t in range(NT):
                        pe.matmul(ps_n[:, t * D:(t + 1) * D], OT[:, t * P:(t + 1) * P], st.piece("wo"), start=True, stop=False)
                        ins = pe.matmul(ps_n[:, t * D:(t + 1) * D], core.ones[:, :], core.row("a1_bo"), start=False, stop=True)
                    ins.then_inc(out_made, 1)

                @block.scalar
                def _(act):
                    norm.scalar(act, ps_t)
                    scale = float(dh) ** -0.5
                    for i in range(2):
                        act.wait_ge(qkv_made, i + 1)
                        act.activation(qkT[:, i, :], ps_f[:, i, :], ACT.Copy, scale=scale).then_inc(qkv_kept, 1)
                        act.activation(sq[:, i, :], ps_f[:, i, :], ACT.Square, scale=scale).then_inc(qkv_kept, 1)
                    act.wait_ge(qkv_made, 3)
                    act.activation(O[:].rearrange("p t d -> p (t d)"), ps_k[:, 0, :], ACT.Copy).then_inc(qkv_kept, 1)
                    act.wait_ge(v_turned, 1)
                    act.activation(V1[:, :, 0:D], ps_t[:].rearrange("p (t d) -> p t d", t=NT), ACT.Copy).then_inc(v_ready, 1)
                    for u in range(2 * NT):
                        act.wait_ge(shifted, u + 1)
                        if u >= 2:
                            act.wait_ge(phi_ready, u - 1)
                        act.activation(ph[:, u % 2, :], sh[:, u % 2, :], ACT.Exp).then_inc(exped, 1)
                    for t in range(NT):
                        act.wait_ge(q_turned, t + 1)
                        if t >= 2:
                            act.wait_ge(weighted, t - 1)
                        act.activation(phT[:, t % 2].rearrange("p j s -> p (j s)"), ps_t[:], ACT.Copy).then_inc(qT_ready, 1)
                    act.wait_ge(o_turned, 1)
                    act.activation(OT[:], ps_t[:], ACT.Copy).then_inc(oT_ready, 1)

                @block.vector
                def _(dve):
                    chain = Chain(dve, dve_done)
                    dve.wait_ge(n_made, 1)

                    def shift(u):
                        i, t = divmod(u, NT)
                        dve.wait_ge(f_made, u + 1)
                        f = ps_f[:, u % 2, :].rearrange("p (h m) -> p h m", h=NH)
                        chain.done(dve.tensor_reduce(mx[:, i, t, :], f, AX, ALU.max))
                        chain.wait()
                        chain.done(dve.scalar_tensor_tensor(cc[:, i, t, :], ps_n[:, u * NH:(u + 1) * NH], 0.5, mx[:, i, t, :],
                                                            ALU.mult, ALU.add))
                        chain.wait()
                        if u >= 2:
                            dve.wait_ge(exped, u - 1)
                        dve.tensor_tensor(sh[:, u % 2, :].rearrange("p (h m) -> p h m", h=NH), f,
                                          cc[:, i, t, :].unsqueeze(2).to_broadcast([P, NH, M]), ALU.subtract).then_inc(shifted, 1)

                    def feature(u):
                        i, t = divmod(u, NT)
                        dve.wait_ge(exped, u + 1)
                        dve.tensor_scalar(phi[:, i, t, :], ph[:, u % 2, :], EPS, float(M) ** -0.5, ALU.add, ALU.mult).then_inc(phi_ready, 1)

                    shift(0)
                    for u in range(2 * NT):
                        if u + 1 < 2 * NT:
                            shift(u + 1)
                        feature(u)
                        if u == 3:
                            norm.next_statistics(dve, chain, b)
                        if u == 5:
                            norm.next_normalise(dve, chain, b)
                    blk = st.piece("blk").rearrange("p (j n) -> p j n", j=NF)
                    blkh = st.piece("blkh").rearrange("p (j n) -> p j n", j=NF)
                    for j in range(NF):
                        dve.wait_ge(kv_made, j + 1)
                        dve.tensor_tensor(KV[:, j, 0:D], ps_k[:, j % 2, 0:D], blk[:, j, :], ALU.mult).then_inc(kv_ready, 1)
                        dve.tensor_scalar(KV[:, j, D:D + NH], blkh[:, j, :], ps_k[:, j % 2, D:D + 1], None, ALU.mult).then_inc(kv_kept, 1)
                    for t in range(NT):
                        dve.wait_ge(weighted, t + 1)
                        chain.done(dve.tensor_scalar(rden[:, t, :], ps_o[:, t % 2, D:D + NH], EPS, None, ALU.add))
                        chain.wait()
                        chain.done(dve.reciprocal(rden[:, t, :], rden[:, t, :]))
                        chain.wait()
                        dve.tensor_tensor(O[:, t, :].rearrange("p (h d) -> p h d", h=NH), ps_o[:, t % 2, 0:D].rearrange("p (h d) -> p h d", h=NH),
                                          rden[:, t, :].unsqueeze(2).to_broadcast([P, NH, dh]), ALU.mult).then_inc(o_ready, 1)
                    dve.wait_ge(out_made, 1)
                    x = core.X[:, b].rearrange("p t d -> p (t d)")
                    dve.tensor_tensor(x, ps_n[:], x, ALU.add)

            st.end_pass()


def talking_attention(core, index):
    nc = core.nc
    pieces = TALK
    dh, NM, TOP = 64, 64, 64
    NJ = NH * dh // P
    Q = 64
    R = 8
    NUNIT, NG = S // Q, Q // R
    NGROUP = NUNIT * NG
    LAG_E, LAG_M = 2, 4
    scale = float(dh) ** -0.5
    ROUNDS = TOP // 8
    STEPS = 1 + ROUNDS + ROUNDS - 1 + 1
    NDT = 5
    NORM_AT = 40
    NC = NT + 1

    def unit(q):
        return (NUNIT - q) % NUNIT

    def rows_of(q, c):
        return NM if c == NT else max(0, min(P, Q * (unit(q) + 1) - P * c))

    def chunks(q):
        return [c for c in range(NC) if rows_of(q, c)]

    def width(g):
        return NM + Q * unit(g // NG) + R * (g % NG + 1)

    with ExitStack() as ctx:
        st = Step(core, ctx, index, pieces)
        norm = Norm(st)
        QB = st.sb("QB", [P, 2, NJ, 2, Q])
        KT = st.sb("KT", [P, NJ, S])
        spare = core.arena[(index + 1) % 2][:, NATT8:ARENA]
        V = spare[:, 0:NT * NJ * P].rearrange("p (t n) -> p t n", t=NT)
        W = spare[:, NT * NJ * P:NT * NJ * P + 2 * (NM + S)].rearrange("p (a n) -> p a n", a=2)
        S1 = spare[:, NT * NJ * P + 2 * (NM + S):NT * NJ * P + 4 * (NM + S)].rearrange("p (a n) -> p a n", a=2)
        at = NT * NJ * P + 4 * (NM + S)
        post = spare[:, at:at + 4 * P].rearrange("p (a n) -> p a n", a=4)
        OT = spare[:, at + 4 * P:at + 4 * P + NJ * Q].rearrange("p (j s) -> p j s", j=NJ)
        ST = st.sb("ST", [P, 2, NC, NG, NH, R])
        Dt = st.sb("Dt", [P, NDT, NM + S])
        Ex = st.sb("Ex", [P, 3, NM + S])
        A = st.sb("A", [P, 4, NM + S])
        top = st.sb("top", [P, 4, ROUNDS, 8])
        nb = st.sb("nb", [P, 4])
        den, rden = st.sb("den", [P, 2]), st.sb("rden", [P, 4])
        AT = st.sb("AT", [P, NC, NH, Q])
        ps_t = st.ps("ps_t", [P, 2, BANK])
        ps_m = st.ps("ps_m", [P, 2, BANK])
        ps_c = st.ps("ps_c", [P, 2, BANK])
        ps_o = st.ps("ps_o", [P, BANK])
        ps_x = st.ps("ps_x", [P, BANK])
        dve_done = st.sem("dve_done")
        made, kept, qk_made, st_kept, turned, s_kept, mixed, m_kept = (st.sem(n) for n in (
            "made", "kept", "qk_made", "st_kept", "turned", "s_kept", "mixed", "m_kept"))
        step = (st.sem("step_even"), st.sem("step_odd"))
        nb_ready, exped, chosen, cleared, post_ready, back, at_kept = (st.sem(n) for n in (
            "nb_ready", "exped", "chosen", "cleared", "post_ready", "back", "at_kept"))
        weighted, oT_ready, out_made, added, q_made, q_kept = (st.sem(n) for n in (
            "weighted", "oT_ready", "out_made", "added", "q_made", "q_kept"))
        ident = core.const("ident")
        begin(core, index, st)
        wcol = {n: pieces[n][0] for n in pieces}
        memk = st.piece("memk").rearrange("p (j m) -> p j m", j=NJ)

        def keys(j, c, n):
            return memk[:, j, :] if c == NT else KT[:, j, c * P:c * P + n]

        with nc.Block() as block:

            @block.vector
            def _(dve):
                dve.memset(QB[:], 0.0)

        def st_before(q):
            return sum(len(chunks(x)) for x in range(q))

        def back_parts(g):
            cs = chunks(g // NG)
            return [cs[:4], cs[4:]] if len(cs) > 4 else [cs]

        def back_before(g):
            return sum(len(back_parts(x)) for x in range(g))

        def v_parts(n):
            return [n] if n < 2 * NT else []

        def st_parts(n):
            q, k = n // NG + 1, n % NG
            if q >= NUNIT:
                return []
            first = NG - len(chunks(q))
            return [(q, k - first)] if k >= first else []

        def q_made_by(n):
            return 1 + sum(1 for x in range(min(n, NGROUP)) for _, i in st_parts(x) if i == 0)

        def outputs_by(n):
            return max(0, (n - LAG_M + 1) // NG)

        def st_done(n):
            return st_before(1) + sum(len(st_parts(x)) for x in range(n))

        with nc.Fori(0, B) as b:
            with nc.Block() as block:

                @block.gpsimd
                def _(pool):
                    def bias(g):
                        pool.wait_ge(step[g % 2], STEPS * (g // 2) + 2)
                        if g >= 4:
                            pool.wait_ge(exped, g - 3)
                        pool.tensor_scalar(nb[:, g % 4:g % 4 + 1], top[:, g % 4, 0, 0:1], -scale, 0.0, ALU.mult,
                                           ALU.add).then_inc(nb_ready, 1)

                    def clear(g):
                        w, wu = width(g), NM + Q * (unit(g // NG) + 1)
                        if w < wu:
                            if g >= 4:
                                pool.wait_ge(back, back_before(g - 3))
                            pool.memset(A[:, g % 4, w:wu], 0.0).then_inc(cleared, 1)

                    def weights(g):
                        pool.wait_ge(chosen, g + 1)
                        if g >= 4:
                            pool.wait_ge(back, back_before(g - 3))
                        pool.tensor_scalar(post[:, g % 4, :], st.piece("post"), rden[:, g % 4:g % 4 + 1], 0.0, ALU.mult,
                                           ALU.add).then_inc(post_ready, 1)

                    for g in range(0, NGROUP, 2):
                        for part in (bias, clear, weights):
                            part(g)
                            part(g + 1)
                        if g == NORM_AT:
                            norm.gpsimd(pool)

                @block.tensor
                def _(pe):
                    norm.tensor(pe, ps_x)
                    pe.wait_ge(norm.xnT_ready, 1)
                    for i in range(NJ):
                        if i >= 2:
                            pe.wait_ge(kept, i - 1)
                        c = wcol["wk"] + i * P
                        pe.matmul(ps_c[:, i % 2, :], st.w[:, c:c + P], norm.xnT[:], start=True, stop=True).then_inc(made, 1)

                    def values(i):
                        t, half = divmod(i, 2)
                        c = wcol["wv"] + half * BANK
                        pe.matmul(ps_c[:, 0, :], norm.xnT[:, t * P:(t + 1) * P], st.w[:, c:c + BANK],
                                  start=True, stop=True).then_inc(made, 1)

                    def queries(q, n):
                        if n > 0:
                            pe.wait_ge(oT_ready, 4 * outputs_by(n))
                        for j in range(NJ):
                            c = wcol["wq"] + j * P
                            ins = pe.matmul(ps_o[:, j * Q:(j + 1) * Q], st.w[:, c:c + P],
                                            norm.xnT[:, unit(q) * Q:(unit(q) + 1) * Q], start=True, stop=True)
                        ins.then_inc(q_made, 1)

                    def unit_scores(q, n, at):
                        if n == 0:
                            queries(q, at)
                            pe.wait_ge(q_kept, 2 * (q + 1))
                        c = chunks(q)[n]
                        r = rows_of(q, c)
                        for j in range(NJ):
                            ins = pe.matmul(ps_c[0:r, j // 4, (j % 4) * P:(j % 4 + 1) * P], keys(j, c, r),
                                            QB[:, q % 2, j].rearrange("p a s -> p (a s)"), start=True, stop=True)
                        ins.then_inc(qk_made, 1)

                    def turn(g):
                        q, k = divmod(g, NG)
                        cs = chunks(q)
                        pe.wait_ge(st_kept, st_before(q + 1))
                        if g >= 1:
                            pe.wait_ge(s_kept, 2 * g)
                        for c in cs:
                            r = rows_of(q, c)
                            out = ps_t[:, 1, 0:NM] if c == NT else ps_t[:, 0, c * P:c * P + r]
                            ins = pe.transpose(out, ST[0:r, q % 2, c, k].rearrange("p h r -> p (h r)"), ident[0:r, 0:r])
                        ins.then_inc(turned, 1)

                    def mix(g):
                        w = width(g)
                        pe.wait_ge(s_kept, 2 * (g + 1))
                        if g >= 1:
                            pe.wait_ge(m_kept, 2 * g)
                        pe.matmul(ps_m[:, 1, 0:NM], st.piece("pre"), S1[:, g % 2, 0:NM], start=True, stop=True)
                        pe.matmul(ps_m[:, 0, 0:w - NM], st.piece("pre"), S1[:, g % 2, NM:w], start=True, stop=True).then_inc(mixed, 1)

                    def mix_back(g):
                        q = g // NG
                        pe.wait_ge(post_ready, g + 1)
                        if g % NG != NG - 1:
                            pe.wait_ge(cleared, g + 1 - g // NG)
                        for i, part in enumerate(back_parts(g)):
                            n = back_before(g) + i
                            if n >= 2:
                                pe.wait_ge(at_kept, n - 1)
                            for x, c in enumerate(part):
                                r = rows_of(q, c)
                                cols = slice(0, NM) if c == NT else slice(NM + c * P, NM + c * P + r)
                                ins = pe.matmul(ps_c[0:r, n % 2, x * P:(x + 1) * P], A[:, g % 4, cols], post[:, g % 4, :],
                                                start=True, stop=True)
                            ins.then_inc(back, 1)

                    def unit_out(q):
                        pe.wait_ge(q_kept, 2 * q_made_by((q + 1) * NG - 1 + LAG_M))
                        if q >= 1:
                            pe.wait_ge(added, q)
                        pe.wait_ge(at_kept, back_before((q + 1) * NG))
                        cs = chunks(q)
                        for j in range(NJ):
                            bank = ps_o if j < 4 else ps_x
                            for n, c in enumerate(cs):
                                r = rows_of(q, c)
                                v = st.w[0:r, wcol["memv"] + j * P:wcol["memv"] + (j + 1) * P] if c == NT else V[0:r, c, j * P:(j + 1) * P]
                                ins = pe.matmul(bank[:, (j % 4) * P:(j % 4 + 1) * P], v,
                                                AT[0:r, c, 2 * j:2 * j + 2, :].rearrange("p h s -> p (h s)"),
                                                start=(n == 0), stop=(n == len(cs) - 1))
                        ins.then_inc(weighted, 1)
                        pe.wait_ge(oT_ready, 4 * (q + 1))
                        out = ps_x[64 * (unit(q) % 2):64 * (unit(q) % 2) + 64, 0:D]
                        for j in range(NJ):
                            c = wcol["wo"] + j * D
                            pe.matmul(out, OT[:, j, :], st.w[:, c:c + D], start=(j == 0), stop=False)
                        pe.matmul(out, core.ones[:, 0:Q], core.row("a2_bo"), start=False, stop=True).then_inc(out_made, 1)

                    pe.wait_ge(kept, NJ)
                    for n in range(len(chunks(0))):
                        pe.wait_ge(st_kept, n)
                        unit_scores(0, n, 0)
                    for n in range(NGROUP + LAG_M):
                        if n < NGROUP:
                            turn(n)
                            mix(n)
                        g = n - LAG_M
                        if g >= 0:
                            pe.wait_ge(st_kept, st_done(n))
                            pe.wait_ge(kept, NJ + min(2 * NT, n))
                            mix_back(g)
                            if g % NG == NG - 1:
                                unit_out(g // NG)
                        for i in v_parts(n):
                            pe.wait_ge(st_kept, st_done(n))
                            pe.wait_ge(kept, NJ + i)
                            if g >= 0:
                                pe.wait_ge(at_kept, back_before(g + 1))
                            values(i)
                        for q, i in st_parts(n):
                            pe.wait_ge(st_kept, st_done(n))
                            pe.wait_ge(kept, NJ + min(2 * NT, n + 1))
                            if g >= 0:
                                pe.wait_ge(at_kept, back_before(g + 1))
                            unit_scores(q, i, n)

                @block.scalar
                def _(act):
                    norm.scalar(act, ps_x)
                    for i in range(NJ):
                        act.wait_ge(made, i + 1)
                        act.activation(KT[:, i, :], ps_c[:, i % 2, :], ACT.Copy).then_inc(kept, 1)

                    def keep_values(i):
                        t, half = divmod(i, 2)
                        act.wait_ge(made, NJ + i + 1)
                        act.activation(V[:, t, half * BANK:(half + 1) * BANK], ps_c[:, 0, :], ACT.Copy).then_inc(kept, 1)

                    def keep_unit(q, n):
                        if n == 0:
                            act.wait_ge(q_made, q + 1)
                            made_q = ps_o[:].rearrange("p (j s) -> p j s", j=NJ)
                            for par in range(2):
                                rows = slice(64 * par, 64 * par + 64)
                                act.activation(QB[rows, q % 2, :, par, :], made_q[rows], ACT.Copy).then_inc(q_kept, 1)
                        c = chunks(q)[n]
                        r = rows_of(q, c)
                        act.wait_ge(qk_made, st_before(q) + n + 1)
                        if q >= 2:
                            act.wait_ge(turned, (q - 1) * NG)
                        act.activation(ST[0:r, q % 2, c].rearrange("p k h r -> p h k r"),
                                       ps_c[0:r].rearrange("p a (h k r) -> p (a h) k r", h=NJ, k=NG), ACT.Copy).then_inc(st_kept, 1)

                    def keep_scores(g):
                        w = width(g)
                        act.wait_ge(turned, g + 1)
                        if g >= 2:
                            act.wait_ge(mixed, g - 1)
                        act.activation(S1[:, g % 2, 0:NM], ps_t[:, 1, 0:NM], ACT.Copy).then_inc(s_kept, 1)
                        act.activation(S1[:, g % 2, NM:w], ps_t[:, 0, 0:w - NM], ACT.Copy).then_inc(s_kept, 1)
                        act.wait_ge(mixed, g + 1)
                        if g >= NDT:
                            act.wait_ge(chosen, g - NDT + 1)
                        act.activation(Dt[:, g % NDT, 0:NM], ps_m[:, 1, 0:NM], ACT.Copy).then_inc(m_kept, 1)
                        act.activation(Dt[:, g % NDT, NM:w], ps_m[:, 0, 0:w - NM], ACT.Copy).then_inc(m_kept, 1)

                    def exponentials(g):
                        w = width(g)
                        act.wait_ge(nb_ready, g + 1)
                        if g >= 3:
                            act.wait_ge(chosen, g - 2)
                        act.activation(Ex[:, g % 3, 0:w], Dt[:, g % NDT, 0:w], ACT.Exp, bias=nb[:, g % 4:g % 4 + 1],
                                       scale=scale).then_inc(exped, 1)

                    def keep_back(g):
                        q, k = divmod(g, NG)
                        for i, part in enumerate(back_parts(g)):
                            n = back_before(g) + i
                            act.wait_ge(back, n + 1)
                            if q >= 1:
                                act.wait_ge(weighted, q)
                            full = [x for x, c in enumerate(part) if rows_of(q, c) == P]
                            rest = [x for x, c in enumerate(part) if rows_of(q, c) != P]
                            src = ps_c[:, n % 2, :].rearrange("p (c h r) -> p c h r", c=4, h=NH)
                            todo = []
                            if full:
                                todo.append((P, part[full[0]], full[0], len(full)))
                            todo += [(rows_of(q, part[x]), part[x], x, 1) for x in rest]
                            for r, c, x, m in todo:
                                for y in range(m):
                                    ins = act.activation(AT[0:r, c + y, :, k * R:(k + 1) * R], src[0:r, x + y], ACT.Copy)
                            ins.then_inc(at_kept, 1)

                    for n in range(len(chunks(0))):
                        keep_unit(0, n)
                    for n in range(NGROUP + LAG_M):
                        if n < NGROUP:
                            keep_scores(n)
                        if 0 <= n - LAG_E < NGROUP:
                            exponentials(n - LAG_E)
                        g = n - LAG_M
                        if g >= 0:
                            keep_back(g)
                            if g % NG == NG - 1:
                                act.wait_ge(weighted, g // NG + 1)
                                for half, bank in enumerate((ps_o, ps_x)):
                                    o = bank[:].rearrange("p (j a s) -> p j a s", j=4, a=2)
                                    for par in range(2):
                                        rows = slice(64 * par, 64 * par + 64)
                                        act.activation(OT[rows, 4 * half:4 * half + 4, :], o[rows, :, par, :],
                                                       ACT.Copy).then_inc(oT_ready, 1)
                        for i in v_parts(n):
                            keep_values(i)
                        for q, i in st_parts(n):
                            keep_unit(q, i)

                @block.vector
                def _(dve):
                    chain = Chain(dve, dve_done)

                    def residual(q):
                        rows = slice(64 * (unit(q) % 2), 64 * (unit(q) % 2) + 64)
                        x = core.X[rows, b, unit(q) // 2, :]
                        dve.wait_ge(out_made, q + 1)
                        dve.tensor_tensor(x, ps_x[rows, 0:D], x, ALU.add).then_inc(added, 1)

                    def prepare(g):
                        w = width(g)
                        dve.wait_ge(m_kept, 2 * (g + 1))
                        own = Dt[:, g % NDT, w - R:w]
                        if g >= 4:
                            dve.wait_ge(nb_ready, g - 3)
                        dve.tensor_tensor(own, own, core.const("later"), ALU.add).then_inc(step[g % 2], 1)

                    def largest(g, r):
                        src = Dt[:, g % NDT, 0:width(g)] if r == 0 else W[:, g % 2, 0:width(g)]
                        dve.wait_ge(step[g % 2], STEPS * (g // 2) + 2 * r + 1)
                        ins = dve.max(top[:, g % 4, r, :], src).then_inc(step[g % 2], 1)

                    def take_out(g, r):
                        src = Dt[:, g % NDT, 0:width(g)] if r == 0 else W[:, g % 2, 0:width(g)]
                        dve.wait_ge(step[g % 2], STEPS * (g // 2) + 2 * r + 2)
                        dve.match_replace(W[:, g % 2, 0:width(g)], top[:, g % 4, r, :], src, -BIG).then_inc(step[g % 2], 1)

                    def choose(g):
                        w = width(g)
                        dve.wait_ge(step[g % 2], STEPS * (g // 2) + 2 * ROUNDS)
                        dve.wait_ge(exped, g + 1)
                        if g >= 4:
                            dve.wait_ge(back, back_before(g - 3))
                            dve.wait_ge(post_ready, g - 3)
                        dve.scalar_tensor_tensor(A[:, g % 4, 0:w], Dt[:, g % NDT, 0:w], top[:, g % 4, ROUNDS - 1, 7:8],
                                                 Ex[:, g % 3, 0:w], ALU.is_ge, ALU.mult,
                                                 accum_out=den[:, g % 2:g % 2 + 1]).then_inc(step[g % 2], 1)

                    def invert(g):
                        dve.wait_ge(step[g % 2], STEPS * (g // 2 + 1))
                        dve.reciprocal(rden[:, g % 4:g % 4 + 1], den[:, g % 2:g % 2 + 1]).then_inc(chosen, 1)

                    for g in range(0, NGROUP, 2):
                        pair = (g, g + 1)
                        for x in pair:
                            prepare(x)
                        for r in range(ROUNDS):
                            for x in pair:
                                largest(x, r)
                            if r < ROUNDS - 1:
                                for x in pair:
                                    take_out(x, r)
                        for x in pair:
                            choose(x)
                        for x in pair:
                            invert(x)
                        if (g + 2) % NG == 0 and g >= NG:
                            residual(g // NG - 1)
                        if g == NORM_AT:
                            norm.next_statistics(dve, chain, b)
                            norm.next_normalise(dve, chain, b)
                    residual(NUNIT - 1)

            st.end_pass()


def build(nc, ins, out):
    core = Core()
    core.nc = nc
    core.order = list(SUBLAYERS)
    core.packed = {i: ins[f"w{i}"] for i in core.order}
    with ExitStack() as ctx:
        def sb(name, shape, dt=F32):
            return ctx.enter_context(nc.sbuf_tensor(name, shape, dt))

        core.X = sb("X", [P, B, NT, D])
        core.ln_stats, core.ln_mv = sb("ln_stats", [P, NT, 6]), sb("ln_mv", [P, NT, 2])
        core.ln_var, core.ln_rstd = sb("ln_var", [P, NT]), sb("ln_rstd", [P, NT])
        core.xn = sb("xn", [P, NT, D])
        core.consts = sb("consts", [P, NCONST])
        core.rows = sb("rows", [1, NROWS])
        core.ones = sb("ones", [1, P])
        core.ctxT = sb("ctxT", [P, B, SC])
        core.indices = sb("indices", [P, NT, 2], I32)
        core.arena = [sb("arena_even", [P, ARENA]), sb("arena_odd", [P, ARENA])]
        core.arrived = [ctx.enter_context(nc.semaphore("arrived_even")), ctx.enter_context(nc.semaphore("arrived_odd"))]
        loaded = ctx.enter_context(nc.semaphore("loaded"))
        stored = ctx.enter_context(nc.semaphore("stored"))
        with nc.Block() as block:

            @block.sync
            def _(sp):
                first = core.order[0]
                sp.dma_start(core.X[:].rearrange("p b t d -> p (b t d)"), ins["x"]).then_inc(loaded, 16)
                sp.dma_start(core.consts[:], ins["consts"]).then_inc(loaded, 16)
                sp.dma_start(core.arena[first % 2][:, 0:WIDTHS[first]], core.packed[first]).then_inc(core.arrived[first % 2], 16)
                sp.dma_start(core.rows[:], ins["rows"]).then_inc(loaded, 16)
                sp.dma_start(core.ctxT[:].rearrange("p b s -> p (b s)"), ins["ctxT"]).then_inc(loaded, 16)
                sp.dma_start(core.indices[:].rearrange("p t k -> p (t k)"), ins["indices"]).then_inc(loaded, 16)
                sp.wait_ge(loaded, 5 * 16)

            @block.vector
            def _(dve):
                dve.memset(core.ones[:], 1.0)

        normalise_first(core, "first")
        for i in core.order:
            PROGRAMS[i](core, i)
        with nc.Block() as block:

            @block.sync
            def _(sp):
                sp.dma_start(out, core.X[:].rearrange("p b t d -> p (b t d)")).then_inc(stored, 16)
                sp.wait_ge(stored, 16)


PROGRAMS = {
    0: lambda c, i: self_attention(c, i, SELF_ROPE, {"bo": "zero"}, True),
    1: lambda c, i: cross_attention(c, i, ATT8, {"bv": "x0_bv", "bo": "x0_bo"}, 8),
    2: lambda c, i: feed_forward(c, i, FF0, "softmax2"),
    3: lambda c, i: favor_attention(c, i),
    4: lambda c, i: cross_attention(c, i, ATT64, {"bv": "x1_bv", "bo": "x1_bo"}, 64),
    5: lambda c, i: feed_forward(c, i, FF1, "given"),
    6: lambda c, i: talking_attention(c, i),
    7: lambda c, i: cross_attention(c, i, ATT8, {"bv": "x2_bv", "bo": "x2_bo"}, 8),
    8: lambda c, i: feed_forward(c, i, FF2, "argmax"),
    9: lambda c, i: self_attention(c, i, SELF_PRIOR, {"bo": "a3_bo"}, False),
    10: lambda c, i: cross_attention(c, i, ATT8, {"bv": "zero", "bo": "x3_bo"}, 8),
    11: lambda c, i: feed_forward(c, i, FF3, "top2softmax"),
}


def _tokens(x):
    return x.reshape(-1, P, x.shape[-1]).transpose(1, 0, 2).reshape(P, -1)


def _pack(pieces, given):
    total = max(c + n for c, n in pieces.values())
    out = np.zeros((P, total), np.float32)
    for name, (c, n) in pieces.items():
        if name in given:
            a = given[name]
            out[:a.shape[0], c:c + n] = a.reshape(a.shape[0], n)
    return out


def _spread_heads(w):
    out = np.zeros((NH, 8, NH, 8), np.float32)
    for i in range(8):
        out[:, i, :, i] = w
    return out.reshape(P, P)


def _constants():
    p = np.arange(P)
    consts = _pack(CONST, {
        "ident": np.eye(P, dtype=np.float32),
        "head8": (p[:, None] // 8 == np.arange(NH)[None]).astype(np.float32),
        "head64": (p[:, None] // 64 == np.arange(NH)[None] % 2).astype(np.float32),
        "expert_no": np.broadcast_to(np.arange(E, dtype=np.float32), (P, E)),
        "minus_half": np.full((P, NT), -0.5, np.float32),
        "later": np.where(np.arange(8)[None] > p[:, None] % 8, -BIG, 0.0).astype(np.float32),
    })
    pos = np.arange(S, dtype=np.float32)
    freq = np.float32(10000.0) ** (-np.arange(0, 8, 2, dtype=np.float32) / np.float32(8))
    angle = (pos[:, None] * freq[None]).astype(np.float32)[:, (p % 8) // 2].T
    sign = np.where(p % 2 == 0, -1.0, 1.0).astype(np.float32)[:, None]
    swap = (p[:, None] == (p ^ 1)[None]).astype(np.float32)
    q = (np.arange(NT)[None, :, None] * P + p[:, None, None]).astype(np.float32)
    k = np.arange(S, dtype=np.float32)[None, None]
    causal = np.where(k > q, BIG, 0.0).astype(np.float32)
    gauss = np.zeros((P, NT, S), np.float32)
    for period, weight, sigma in ((1.0, 0.8, 0.5), (30.0, 0.4, 2.0)):
        gauss = gauss + np.float32(weight) * np.exp(-(np.abs(q - k) - np.float32(period)) ** 2 / np.float32(2.0 * sigma ** 2))
    rope = {"cos": np.cos(angle), "sin": np.sin(angle) * sign, "swap": swap, "causal": causal.reshape(P, -1)}
    return consts, rope, gauss.reshape(P, -1).astype(np.float32)


def _layouts(a):
    consts, rope, gauss = _constants()

    p, j = np.arange(P), np.arange(4)
    own = (4 * j[None, :, None] + p[:, None, None] // 32 == np.arange(NH)[None, None]).astype(np.float32)
    favor_blocks, favor_heads = np.repeat(own, 8, axis=2).reshape(P, -1), own.reshape(P, -1)

    def att(prefix, names, bq=None, bk=None, bv=None):
        g = {k: a[prefix + n].T for k, n in zip(("wq", "wk", "wv", "wo"), names)}
        for k, n in (("bq", bq), ("bk", bk), ("bv", bv)):
            if n:
                g[k] = a[prefix + n].reshape(P, 1)
        return g

    def up(w):
        return w.transpose(1, 0, 2).reshape(P, -1)

    def down(w):
        e, h, d = w.shape
        return w.reshape(e, h // P, P, d).transpose(2, 0, 1, 3).reshape(P, -1)

    def tiles(w):
        return w.reshape(-1, P, w.shape[1]).transpose(1, 0, 2).reshape(P, -1)

    cap = ("Wq", "Wk", "Wv", "Wo")
    low = ("w_q", "w_k", "w_v", "w_o")
    spread = lambda v: np.broadcast_to(v, (P, v.shape[-1]))
    kv = a["L1_xattn_w_kv"]
    ins = {
        "w0": _pack(SELF_ROPE, {**att("L0_attn_", cap), **rope}),
        "w1": _pack(ATT8, att("L0_xattn_", cap, "bq", "bk")),
        "w2": _pack(FF0, {"w1": up(a["L0_ffn_w1"]), "w3": up(a["L0_ffn_w3"]), "w2": down(a["L0_ffn_w2"]),
                          "router": a["L0_ffn_gate_w"].T}),
        "w3": _pack(FAVOR, {**att("L1_attn_", cap), "proj": a["L1_attn_proj"].transpose(0, 2, 1).reshape(P, 32),
                            "blk": favor_blocks, "blkh": favor_heads}),
        "w4": _pack(ATT64, {"wq": a["L1_xattn_w_q"], "wk": kv[:, :1024], "wv": kv[:, 1024:], "wo": tiles(a["L1_xattn_w_out"]),
                            "gamma": spread(a["L1_xattn_ln_gamma"]), "beta": spread(a["L1_xattn_ln_beta"]),
                            "gate": spread(a["L1_xattn_gate"])}),
        "w5": _pack(FF1, {"w1": up(a["L1_ffn_w1"]), "w2": down(a["L1_ffn_w2"]),
                          "weights": _tokens(a["L1_ffn_expert_weights"])}),
        "w6": _pack(TALK, {"wq": a["L2_attn_Wq"].T, "wk": a["L2_attn_Wk"].T, "wv": a["L2_attn_Wv"].T,
                           "wo": tiles(a["L2_attn_Wout"].T),
                           "memk": a["L2_attn_mem_k"].reshape(8, 2, 64, 64).transpose(1, 3, 0, 2).reshape(P, 512),
                           "memv": a["L2_attn_mem_v"].transpose(1, 0, 2).reshape(64, 1024),
                           "pre": _spread_heads(a["L2_attn_pre_proj"]), "post": _spread_heads(a["L2_attn_post_proj"])}),
        "w7": _pack(ATT8, att("L2_xattn_", low, "b_q", "b_k")),
        "w8": _pack(FF2, {"w1": up(a["L2_ffn_w1"]), "w2": down(a["L2_ffn_w2"]), "router": a["L2_ffn_wr"],
                          "b1": a["L2_ffn_b1"].reshape(E, 4, P).transpose(2, 0, 1).reshape(P, -1)}),
        "w9": _pack(SELF_PRIOR, {**att("L3_attn_", cap, "bq", "bk", "bv"), "gauss": gauss,
                                 "lam": np.broadcast_to(a["L3_attn_prior_lambda"].reshape(1, 1), (P, 1))}),
        "w10": _pack(ATT8, att("L3_xattn_", cap)),
        "w11": _pack(FF3, {k: (up if k != "w2" else down)(np.concatenate([a["L3_ffn_" + k], a["L3_ffn_s" + k]]))
                           for k in ("w1", "w3", "w2")} | {"router": a["L3_ffn_router_w"].T}),
    }
    rows = np.zeros((1, NROWS), np.float32)
    for name, source in (("x0_bv", "L0_xattn_bv"), ("x0_bo", "L0_xattn_bo"), ("a1_bo", "L1_attn_bo"), ("x1_bo", "L1_xattn_b_out"),
                         ("f1_b", "L1_ffn_bias"), ("a2_bo", "L2_attn_bout"), ("x2_bv", "L2_xattn_b_v"), ("x2_bo", "L2_xattn_b_o"),
                         ("f2_br", "L2_ffn_br"), ("f2_b2", "L2_ffn_b2"), ("a3_bv", "L3_attn_bv"), ("a3_bo", "L3_attn_bo"),
                         ("x3_bo", "L3_xattn_bo"), ("f3_br", "L3_ffn_experts_bias")):
        c, n = ROWS[name]
        rows[0, c:c + n] = a[source].reshape(-1)
    ins |= {"x": _tokens(a["x"]), "consts": consts, "rows": rows, "ctxT": a["ctx_1024"].transpose(2, 0, 1).reshape(P, -1),
            "indices": _tokens(a["L1_ffn_expert_indices"])}
    return ins


def kernel(**inputs):
    import concourse.bacc as bacc
    from concourse.bass_utils import run_bass_kernel_spmd as run

    arrays = _layouts({k: np.asarray(v) for k, v in inputs.items()})
    nc = bacc.Bacc("TRN2", target_bir_lowering=False, num_devices=1)
    used = {k: np.ascontiguousarray(v) for k, v in arrays.items() if not (k[0] == "w" and int(k[1:]) not in SUBLAYERS)}
    ins = {k: nc.dram_tensor(f"{k}_dram", v.shape, mybir.dt.from_np(v.dtype), kind="ExternalInput").ap()
           for k, v in used.items()}
    out = nc.dram_tensor("out_dram", (P, B * NT * D), F32, kind="ExternalOutput").ap()
    build(nc, ins, out)
    r = run(nc, [{f"{k}_dram": v for k, v in used.items()}], core_ids=[0])
    return np.ascontiguousarray(r.results[0]["out_dram"].reshape(P, B, NT, D).transpose(1, 2, 0, 3).reshape(B, S, D))
```

```python
from contextlib import ExitStack

import numpy as np
import concourse.bass as bass
from concourse import mybir

F32 = mybir.dt.float32
I32 = mybir.dt.int32
ALU = mybir.AluOpType
ACT = mybir.ActivationFunctionType
AX = mybir.AxisListType.X

P = 128
D = 128
B = 4
S = 512
NT = S // P
NH = 16
SC = 77
E = 8
BANK = 512
BIG = 3.0e38
SUBLAYERS = range(12)
FIRST_SEM = 200


def columns(*pieces):
    at, out = 0, {}
    for name, n in pieces:
        out[name] = (at, n)
        at += n
    return out, at


CONST, NCONST = columns(("ident", P), ("head8", NH), ("head64", NH), ("expert_no", E), ("minus_half", NT), ("minus_one", 2), ("later", 8))
ROPE, NROPE = columns(("cos", S), ("sin", S), ("swap", P), ("causal", NT * S))
PRIOR, NPRIOR = columns(("gauss", NT * S), ("lam", 1))
ATT8, NATT8 = columns(("wq", D), ("wk", D), ("wv", D), ("wo", D), ("bq", 1), ("bk", 1), ("bv", 1))
FAVOR, NFAVOR = columns(("wq", D), ("wk", D), ("wv", D), ("wo", D), ("proj", 32), ("blk", D * 4), ("blkh", NH * 4))
ATT64, NATT64 = columns(("wq", 1024), ("wk", 1024), ("wv", 1024), ("wo", 1024), ("bq", 8), ("bk", 8),
                        ("gamma", D), ("beta", D), ("gate", 1))
TALK, NTALK = columns(("wq", 1024), ("wk", 1024), ("wv", 1024), ("wo", 1024), ("memk", 512), ("memv", 1024),
                      ("pre", P), ("post", P))
FF0, NFF0 = columns(("w1", E * 256), ("w3", E * 256), ("w2", E * 256), ("router", E))
FF1, NFF1 = columns(("w1", E * 512), ("w2", E * 512), ("weights", NT * 2))
FF2, NFF2 = columns(("w1", E * 512), ("w2", E * 512), ("router", E), ("b1", E * 4))
FF3, NFF3 = columns(("w1", 9 * 256), ("w3", 9 * 256), ("w2", 9 * 256), ("router", E))
SELF_ROPE = {**ATT8, **{k: (c + NATT8, n) for k, (c, n) in ROPE.items()}}
SELF_PRIOR = {**ATT8, **{k: (c + NATT8, n) for k, (c, n) in PRIOR.items()}}
ARENA = max(NATT8 + NROPE, NATT8 + NPRIOR, NFAVOR, NATT64, NTALK, NFF0, NFF1, NFF2, NFF3)
ROWS, NROWS = columns(("zero", D), ("x0_bv", D), ("x0_bo", D), ("a1_bo", D), ("x1_bo", D), ("f1_b", D), ("a2_bo", D),
                      ("x2_bv", D), ("x2_bo", D), ("f2_br", E), ("f2_b2", E * D), ("a3_bv", D), ("a3_bo", D),
                      ("x3_bo", D), ("f3_br", E), ("x1_bv", 1024))
WIDTHS = [NATT8 + NROPE, NATT8, NFF0, NFAVOR, NATT64, NFF1, NTALK, NATT8, NFF2, NATT8 + NPRIOR, NATT8, NFF3]


class Core:

    def row(self, name, at=0, n=None):
        c, w = ROWS[name]
        return self.rows[0:1, c + at:c + at + (w if n is None else n)]

    def const(self, name):
        c, w = CONST[name]
        return self.consts[:, c:c + w]


class Chain:

    def __init__(self, engine, sem):
        self.engine, self.sem, self.n = engine, sem, 0

    def done(self, ins):
        ins.then_inc(self.sem, 1)
        self.n += 1

    def wait(self):
        self.engine.wait_ge(self.sem, self.n)


class Step:

    def __init__(self, core, ctx, index, pieces):
        self.core, self.nc, self.ctx, self.index = core, core.nc, ctx, index
        self.pieces = pieces
        if pieces:
            self.w = core.arena[index % 2]
        self.sems = []

    def piece(self, name):
        c, w = self.pieces[name]
        return self.w[:, c:c + w]

    def sb(self, name, shape, dt=F32):
        return self.ctx.enter_context(self.nc.sbuf_tensor(f"{name}_{self.index}", shape, dt))

    def ps(self, name, shape):
        return self.ctx.enter_context(self.nc.psum_tensor(f"{name}_{self.index}", shape, F32))

    def sem(self, name):
        s = self.ctx.enter_context(self.nc.semaphore(f"{name}_{self.index}", num=FIRST_SEM + len(self.sems)))
        self.sems.append(s)
        return s

    def end_pass(self):
        nums = sorted(s.num for s in self.sems)
        assert nums == list(range(nums[0], nums[-1] + 1)), nums
        self.nc.all_engine_barrier(sems_to_clear=range(nums[0], nums[-1] + 1))


def begin(core, index, step):
    nc = core.nc
    with nc.Block() as block:

        @block.sync
        def _(sp):
            k = core.order.index(index)
            if k + 1 < len(core.order):
                nxt = core.order[k + 1]
                sp.dma_start(core.arena[nxt % 2][:, 0:WIDTHS[nxt]], core.packed[nxt]).then_inc(core.arrived[nxt % 2], 16)
            sp.wait_ge(core.arrived[index % 2], 16 * (k // 2 + 1))


class Norm:

    def __init__(self, st):
        self.st = st
        self.xnT = st.sb("xnT", [P, S])
        self.xn_ready = st.sem("xn_ready")
        self.var_ready = st.sem("ln_var_ready")
        self.rstd_ready = st.sem("ln_rstd_ready")
        self.turned = st.sem("ln_turned")
        self.xnT_ready = st.sem("xnT_ready")
        self.round = 0

    def statistics(self, dve, chain, src):
        core = self.st.core
        for t in range(NT):
            chain.done(dve.bn_stats(core.ln_stats[:, t, :], src[:, t, :]))
        chain.wait()
        for t in range(NT):
            chain.done(dve.bn_aggr(core.ln_mv[:, t, :], core.ln_stats[:, t, :]))
        chain.wait()
        dve.tensor_scalar(core.ln_var[:], core.ln_mv[:, :, 1], 1e-5, None, ALU.add).then_inc(self.var_ready, 1)
        self.round += 1

    def normalise(self, dve, chain, src, signal=False):
        core = self.st.core
        dve.wait_ge(self.rstd_ready, self.round)
        for t in range(NT):
            ins = dve.tensor_scalar(core.xn[:, t, :], src[:, t, :], core.ln_mv[:, t, 0:1], core.ln_rstd[:, t:t + 1],
                                    ALU.subtract, ALU.mult)
            if signal:
                ins.then_inc(self.xn_ready, 1)
            else:
                chain.done(ins)

    def second(self, dve, chain):
        xn = self.st.core.xn
        self.statistics(dve, chain, xn)
        self.normalise(dve, chain, xn)
        chain.wait()
        for t in range(NT):
            chain.done(dve.tensor_tensor(xn[:, t, :], xn[:, t, :], self.st.piece("gamma"), ALU.mult))
        chain.wait()
        for t in range(NT):
            dve.tensor_tensor(xn[:, t, :], xn[:, t, :], self.st.piece("beta"), ALU.add).then_inc(self.xn_ready, 1)

    def next_statistics(self, dve, chain, b):
        self.statistics(dve, chain, self.st.core.X[:, (b + 1) % B])

    def next_normalise(self, dve, chain, b):
        dve.wait_ge(self.turned, 1)
        self.normalise(dve, chain, self.st.core.X[:, (b + 1) % B])

    def gpsimd(self, pool, rounds=1):
        core = self.st.core
        for r in range(rounds):
            pool.wait_ge(self.var_ready, r + 1)
            pool.tensor_tensor(core.ln_rstd[:], core.ln_var[:], core.const("minus_half"), ALU.pow).then_inc(self.rstd_ready, 1)

    def tensor(self, pe, bank, ready=0):
        if ready:
            pe.wait_ge(self.xn_ready, ready)
        for t in range(NT):
            ins = pe.transpose(bank[:, t * P:(t + 1) * P], self.st.core.xn[:, t, :], self.st.core.const("ident"))
        ins.then_inc(self.turned, 1)

    def scalar(self, act, bank, turns=1):
        act.wait_ge(self.turned, turns)
        act.activation(self.xnT[:], bank[:, 0:S], ACT.Copy).then_inc(self.xnT_ready, 1)


def normalise_first(core, name):
    with ExitStack() as ctx:
        st = Step(core, ctx, name, {})
        norm = Norm(st)
        done = st.sem("dve_done")
        with core.nc.Block() as block:

            @block.vector
            def _(dve):
                chain = Chain(dve, done)
                norm.statistics(dve, chain, core.X[:, 0])
                norm.normalise(dve, chain, core.X[:, 0])

            @block.gpsimd
            def _(pool):
                norm.gpsimd(pool)

        st.end_pass()


def self_attention(core, index, pieces, rows, rope):
    nc = core.nc
    dh = 8
    scale = float(dh) ** -0.5
    NU = NH * NT
    width = [P * (t + 1) if rope else S for t in range(NT)]
    TURN, KEEP, WEIGH = 4, 4, 7
    NSC, NPR, NPT = 3, 6, 6
    with ExitStack() as ctx:
        st = Step(core, ctx, index, pieces)
        norm = Norm(st)
        QT, KT, VT = st.sb("QT", [P, S]), st.sb("KT", [P, S]), st.sb("VT", [P, S])
        KM = st.sb("KM", [P, NH, S])
        Vt = st.sb("Vt", [P, NT, D])
        raw = st.sb("raw", [P, 2, S])
        rot = st.sb("rot", [P, 2, S])
        addend = st.sb("addend", [P, NT, S])
        sc = st.sb("sc", [P, NSC, S])
        pr = st.sb("pr", [P, NPR, S])
        PTs = st.sb("PTs", [P, NPT, S])
        low = st.sb("low", [P, NU])
        den, rden = st.sb("den", [P, NH, NT]), st.sb("rden", [P, NH, NT])
        O, OT = st.sb("O", [P, NT, D]), st.sb("OT", [P, S])
        ps_s = st.ps("ps_s", [P, 3, BANK])
        ps_t = st.ps("ps_t", [P, 3, BANK])
        ps_o = st.ps("ps_o", [P, BANK])
        ps_m = st.ps("ps_m", [P, BANK])
        dve_done = st.sem("dve_done")
        qkv_made, qkv_kept, swapped = st.sem("qkv_made"), st.sem("qkv_kept"), st.sem("swapped")
        keys_ready = st.sem("keys_ready")
        scored, shifted = st.sem("scored"), st.sem("shifted")
        exped, turned, kept_a, kept_v, weighted = (st.sem(n) for n in ("exped", "turned", "kept_a", "kept_v", "weighted"))
        o_ready, o_turned, oT_ready, out_made, v_turned, v_ready = (st.sem(n) for n in (
            "o_ready", "o_turned", "oT_ready", "out_made", "v_turned", "v_ready"))
        ident = core.const("ident")
        begin(core, index, st)
        if rope:
            addend_v = st.piece("causal").rearrange("p (t s) -> p t s", t=NT)
        else:
            addend_v = addend
            with nc.Block() as block:

                @block.vector
                def _(dve):
                    gauss = st.piece("gauss").rearrange("p (t s) -> p t s", t=NT)
                    for t in range(NT):
                        dve.tensor_scalar(addend[:, t, :], gauss[:, t, :], st.piece("lam"), -1.0, ALU.mult, ALU.mult)

        def kept(engine, u):
            engine.wait_ge(kept_v if u % 2 else kept_a, u // 2 + 1)

        with nc.Fori(0, B) as b:
            with nc.Block() as block:

                @block.gpsimd
                def _(pool):
                    norm.gpsimd(pool)

                @block.tensor
                def _(pe):
                    norm.tensor(pe, ps_m)
                    pe.wait_ge(norm.xnT_ready, 1)
                    for name, bank in (("wk", ps_s[:, 1, :]), ("wq", ps_s[:, 0, :]), ("wv", ps_s[:, 2, :])):
                        pe.matmul(bank, st.piece(name), norm.xnT[:], start=True, stop=True).then_inc(qkv_made, 1)
                    if rope:
                        for i in (1, 0):
                            pe.wait_ge(qkv_kept, 2 - i)
                            pe.matmul(ps_t[:, i, :], st.piece("swap"), raw[:, i, :], start=True, stop=True).then_inc(swapped, 1)
                    pe.wait_ge(qkv_kept, 3)
                    for t in range(NT):
                        ins = pe.transpose(ps_m[:, t * P:(t + 1) * P], VT[:, t * P:(t + 1) * P], ident)
                    ins.then_inc(v_turned, 1)
                    for step in range(NU + WEIGH):
                        u = step
                        if u < NU:
                            h, t = divmod(u, NT)
                            if t == 0:
                                pe.wait_ge(keys_ready, h + 1 + (1 if rope else 0))
                            if u >= 3:
                                pe.wait_ge(shifted, u - 2)
                            pe.matmul(ps_s[:, u % 3, 0:width[t]], QT[:, t * P:(t + 1) * P], KM[:, h, 0:width[t]],
                                      start=True, stop=True).then_inc(scored, 1)
                        u = step - TURN
                        if 0 <= u < NU:
                            t = u % NT
                            pe.wait_ge(exped, u + 1)
                            if u >= 3:
                                kept(pe, u - 3)
                            for k in range(width[t] // P):
                                ins = pe.transpose(ps_t[:, u % 3, k * P:(k + 1) * P], pr[:, u % NPR, k * P:(k + 1) * P], ident)
                            ins.then_inc(turned, 1)
                        u = step - WEIGH
                        if u >= 0:
                            h, t = divmod(u, NT)
                            if u == 0:
                                pe.wait_ge(v_ready, 1)
                            kept(pe, u)
                            n = width[t] // P
                            for k in range(n):
                                ins = pe.matmul(ps_o[:, t * D + h * dh:t * D + (h + 1) * dh], PTs[:, u % NPT, k * P:(k + 1) * P],
                                                Vt[:, k, h * dh:(h + 1) * dh], start=(k == 0), stop=(k == n - 1))
                            ins.then_inc(weighted, 1)
                    for t in range(NT):
                        pe.wait_ge(o_ready, t + 1)
                        ins = pe.transpose(ps_m[:, t * P:(t + 1) * P], O[:, t, :], ident)
                    ins.then_inc(o_turned, 1)
                    pe.wait_ge(oT_ready, 1)
                    for t in range(NT):
                        pe.matmul(ps_s[:, 0, t * D:(t + 1) * D], OT[:, t * P:(t + 1) * P], st.piece("wo"), start=True, stop=False)
                        ins = pe.matmul(ps_s[:, 0, t * D:(t + 1) * D], core.ones[:, :], core.row(rows["bo"]), start=False, stop=True)
                    ins.then_inc(out_made, 1)

                @block.scalar
                def _(act):
                    norm.scalar(act, ps_m)
                    dest = (raw[:, 0, :], raw[:, 1, :]) if rope else (QT[:], KT[:])
                    for n, i in enumerate((1, 0)):
                        act.wait_ge(qkv_made, n + 1)
                        act.activation(dest[i], ps_s[:, i, :], ACT.Identity, bias=st.piece(("bq", "bk")[i])).then_inc(qkv_kept, 1)
                    act.wait_ge(qkv_made, 3)
                    act.activation(VT[:], ps_s[:, 2, :], ACT.Identity, bias=st.piece("bv")).then_inc(qkv_kept, 1)
                    for step in range(NU + KEEP):
                        u = step
                        if u < NU:
                            h, t = divmod(u, NT)
                            act.wait_ge(shifted, u + 1)
                            if u >= NPR:
                                act.wait_ge(turned, u - NPR + 1)
                            act.activation(pr[:, u % NPR, 0:width[t]], sc[:, u % NSC, 0:width[t]], ACT.Exp,
                                           bias=low[:, u:u + 1], scale=-1.0, accum_out=den[:, h, t:t + 1]).then_inc(exped, 1)
                        u = step - KEEP
                        if u >= 0 and u % 2 == 0:
                            act.wait_ge(turned, u + 1)
                            if u >= NPT:
                                act.wait_ge(weighted, u - NPT + 1)
                            n = width[u % NT]
                            act.activation(PTs[:, u % NPT, 0:n], ps_t[:, u % 3, 0:n], ACT.Copy).then_inc(kept_a, 1)
                    act.wait_ge(o_turned, 1)
                    act.activation(OT[:], ps_m[:], ACT.Copy).then_inc(oT_ready, 1)

                @block.vector
                def _(dve):
                    chain = Chain(dve, dve_done)
                    if rope:
                        for n, i in enumerate((1, 0)):
                            dve.wait_ge(qkv_kept, n + 1)
                            chain.done(dve.tensor_tensor((QT, KT)[i][:], raw[:, i, :], st.piece("cos"), ALU.mult))
                            dve.wait_ge(swapped, n + 1)
                            chain.done(dve.tensor_tensor(rot[:, i, :], ps_t[:, i, :], st.piece("sin"), ALU.mult))
                        chain.wait()
                        chain.done(dve.tensor_tensor(KT[:], KT[:], rot[:, 1, :], ALU.add))
                        dve.tensor_tensor(QT[:], QT[:], rot[:, 0, :], ALU.add).then_inc(keys_ready, 1)
                        chain.wait()
                    else:
                        dve.wait_ge(qkv_kept, 2)

                    def mask_keys(h):
                        dve.tensor_scalar(KM[:, h, :], KT[:], core.const("head8")[:, h:h + 1], -scale, ALU.mult,
                                          ALU.mult).then_inc(keys_ready, 1)

                    mask_keys(0)
                    mask_keys(1)
                    dve.wait_ge(v_turned, 1)
                    dve.tensor_copy(Vt[:].rearrange("p t d -> p (t d)"), ps_m[:]).then_inc(v_ready, 1)
                    for step in range(NU + KEEP):
                        u = step
                        if u < NU:
                            h, t = divmod(u, NT)
                            if t == 0 and h + 2 < NH:
                                mask_keys(h + 2)
                            dve.wait_ge(scored, u + 1)
                            if u >= NSC:
                                dve.wait_ge(exped, u - NSC + 1)
                            dve.tensor_tensor_reduce(sc[:, u % NSC, 0:width[t]], ps_s[:, u % 3, 0:width[t]],
                                                     addend_v[:, t, 0:width[t]], 1.0, BIG, ALU.add, ALU.min,
                                                     low[:, u:u + 1]).then_inc(shifted, 1)
                        u = step - KEEP
                        if u >= 0 and u % 2 == 1:
                            dve.wait_ge(turned, u + 1)
                            if u >= NPT:
                                dve.wait_ge(weighted, u - NPT + 1)
                            n = width[u % NT]
                            dve.tensor_copy(PTs[:, u % NPT, 0:n], ps_t[:, u % 3, 0:n]).then_inc(kept_v, 1)
                        if step == NU - 8:
                            norm.next_statistics(dve, chain, b)
                        if step == NU - 4:
                            norm.next_normalise(dve, chain, b)
                    dve.wait_ge(exped, NU)
                    chain.done(dve.reciprocal(rden[:].rearrange("p h t -> p (h t)"), den[:].rearrange("p h t -> p (h t)")))
                    chain.wait()
                    dve.wait_ge(weighted, NU)
                    ov = O[:].rearrange("p t (h d) -> p t h d", h=NH)
                    pv = ps_o[:].rearrange("p (t h d) -> p t h d", t=NT, h=NH)
                    for t in range(NT):
                        dve.tensor_tensor(ov[:, t], pv[:, t], rden[:, :, t].unsqueeze(2).to_broadcast([P, NH, dh]),
                                          ALU.mult).then_inc(o_ready, 1)
                    dve.wait_ge(out_made, 1)
                    x = core.X[:, b].rearrange("p t d -> p (t d)")
                    dve.tensor_tensor(x, ps_s[:, 0, :], x, ALU.add)

            st.end_pass()


def cross_attention(core, index, pieces, rows, dh):
    nc = core.nc
    NJ = NH * dh // P
    scale = float(dh) ** -0.5
    wide = dh == 64
    G, HU = 4, NH // 2
    NSEQ = 2
    NU = 2 * NT * NSEQ
    NB = 2
    n_v = min(BANK, NJ * P)
    NV = NJ * P // n_v
    head_mask = "head64" if wide else "head8"
    dv = dh if wide else dh + 1

    def turns_o(u):
        return wide or u % 2 == 1

    def queries(r):
        return range(2 * (r - 4), min(NJ, 2 * (r - 3))) if r >= 4 else range(0)

    program = []
    for r in range(NU + 4):
        for kind, u in (("out", r - 4), ("scores", r), ("turn", r - 1), ("turn_x", r), ("queries", r), ("turn_o", r - 3), ("weigh", r - 2)):
            if kind == "queries":
                program += [(kind, j) for j in queries(r)]
            elif kind == "turn_x":
                program += [(kind, 0)] if r == 3 else []
            elif 0 <= u < NU and (kind != "out" or u % 2 == 1) and (kind != "turn_o" or turns_o(u)):
                program.append((kind, u))
    in_t = ("turn", "turn_x", "queries") + (("out", "turn_o") if wide else ())
    uses = [(kind, u, g) for kind, u in program if kind in in_t for g in range(2 if kind == "turn" else 1)]
    use_no = {use: n for n, use in enumerate(uses)}

    with ExitStack() as ctx:
        st = Step(core, ctx, index, pieces)
        norm = Norm(st)
        QT = st.sb("QT", [P, NSEQ, NJ, S])
        KM = st.sb("KM", [P, B, NH, SC])
        V = st.sb("V", [SC, B, NH, dv])
        sc = st.sb("sc", [P, 2, HU, SC])
        pr = st.sb("pr", [P, 3, HU, SC])
        PTs = st.sb("PTs", [SC, 3, HU, P])
        mx, den, rden = (st.sb(n, [P, NU, HU]) for n in ("mx", "den", "rden"))
        O, OT = st.sb("O", [P, 4, HU * dh]), st.sb("OT", [P, 2, NJ, P])
        gate = st.sb("gate", [P, 1])
        ps_s = st.ps("ps_s", [P, 4, BANK])
        ps_t = st.ps("ps_t", [P, NB, BANK])
        ps_o = st.ps("ps_o", [P, 2, BANK])
        dve_done = st.sem("dve_done")
        k_made, k_kept, v_made, v_kept = (st.sem(n) for n in ("k_made", "k_kept", "v_made", "v_kept"))
        q_made, q_kept_a, q_kept_v = (st.sem(n) for n in ("q_made", "q_kept_a", "q_kept_v"))
        scored, shifted, exped, summed, turned, kept_a, kept_v = (st.sem(n) for n in (
            "scored", "shifted", "exped", "summed", "turned", "kept_a", "kept_v"))
        weighted, o_ready, o_turned, oT_ready, out_made, added = (st.sem(n) for n in (
            "weighted", "o_ready", "o_turned", "oT_ready", "out_made", "added"))
        ident = core.const("ident")
        begin(core, index, st)

        def weight(name, j):
            c, _ = pieces[name]
            return st.w[:, c + j * P:c + (j + 1) * P]

        with nc.Block() as block:

            @block.tensor
            def _(pe):
                for j in range(NJ):
                    if j >= NB:
                        pe.wait_ge(k_kept, (j - NB + 1) * (NH // NJ))
                    pe.matmul(ps_t[:, j % NB, 0:B * SC], weight("wk", j), core.ctxT[:].rearrange("p b s -> p (b s)"),
                              start=True, stop=True).then_inc(k_made, 1)
                c, _ = pieces["wv"]
                for i in range(B * NV):
                    b, j = divmod(i, NV)
                    if i >= 4:
                        pe.wait_ge(v_kept, i - 3)
                    pe.matmul(ps_s[0:SC, i % 4, 0:n_v], core.ctxT[:, b], st.w[:, c + j * n_v:c + (j + 1) * n_v], start=True, stop=False)
                    pe.matmul(ps_s[0:SC, i % 4, 0:n_v], core.ones[:, 0:SC], core.row(rows["bv"], j * n_v, n_v),
                              start=False, stop=True).then_inc(v_made, 1)

            @block.scalar
            def _(act):
                if wide:
                    act.activation(gate[:], st.piece("gate"), ACT.Tanh)
                for i in range(B * NV):
                    b, j = divmod(i, NV)
                    act.wait_ge(v_made, i + 1)
                    act.activation(V[:, b, j * n_v // dh:(j + 1) * n_v // dh, 0:dh],
                                   ps_s[0:SC, i % 4, 0:n_v].rearrange("p (h d) -> p h d", d=dh), ACT.Copy).then_inc(v_kept, 1)

            @block.vector
            def _(dve):
                if not wide:
                    dve.memset(V[:, :, :, dh:dv], 1.0)
                for j in range(NJ):
                    dve.wait_ge(k_made, j + 1)
                    for h in range(j * (NH // NJ), (j + 1) * (NH // NJ)):
                        dve.tensor_scalar(KM[:, :, h, :], ps_t[:, j % NB, 0:B * SC].rearrange("p (b s) -> p b s", b=B),
                                          st.piece("bk")[:, j:j + 1], core.const(head_mask)[:, h:h + 1],
                                          ALU.add, ALU.mult).then_inc(k_kept, 1)

        st.end_pass()

        def kept(engine, u, g):
            engine.wait_ge((kept_a, kept_v)[g], u + 1)

        def query_kept(engine, seq, j):
            engine.wait_ge((q_kept_a, q_kept_v)[j % 2], seq * ((NJ + 1 - j % 2) // 2) + j // 2 + 1)

        def keep_query_a(act, seq, j, bank):
            act.wait_ge(q_made, seq * NJ + j + 1)
            act.activation(QT[:, seq, j, :], bank, ACT.Identity, bias=st.piece("bq")[:, j:j + 1]).then_inc(q_kept_a, 1)

        def keep_query_v(dve, seq, j, bank):
            dve.wait_ge(q_made, seq * NJ + j + 1)
            dve.tensor_scalar(QT[:, seq, j, :], bank, st.piece("bq")[:, j:j + 1], None, ALU.add).then_inc(q_kept_v, 1)

        def freed(engine, n):
            kind, u, g = uses[n]
            if kind == "turn":
                kept(engine, u, g)
            elif kind == "turn_x":
                engine.wait_ge(norm.xnT_ready, 2)
            elif kind == "queries":
                query_kept(engine, 1, u)
            elif kind == "turn_o":
                engine.wait_ge(oT_ready, turns_before(u) + 1)
            else:
                engine.wait_ge(added, u // 2 + 1)

        def turns_before(u):
            return u if wide else u // 2

        def bank_s(u):
            return ps_s[:, 2 * (u % 2):2 * (u % 2) + 2, 0:G * SC].rearrange("p g (h s) -> p g h s", h=G)

        def bank_o(kind, u):
            if wide:
                return ps_t[:, use_no[kind, u, 0] % NB, :]
            return ps_o[:, u % 2, P:2 * P] if kind == "turn_o" else ps_o[:, u % 2, 2 * P:3 * P]

        def outputs(u):
            return ps_o[:, u % 2, 0:HU * dv].rearrange("p (h d) -> p h d", h=HU)

        def bank_q(j):
            return ps_t[:, use_no["queries", j, 0] % NB, :]

        with nc.Fori(0, B // NSEQ) as pair:
            with nc.Block() as block:

                @block.gpsimd
                def _(pool):
                    norm.gpsimd(pool, 4 if wide else 2)

                @block.tensor
                def _(pe):
                    norm.tensor(pe, ps_t[:, 0, :], ready=NT if wide else 0)
                    pe.wait_ge(norm.xnT_ready, 1)
                    for j in range(NJ):
                        if j >= 4:
                            query_kept(pe, 0, j - 4)
                        pe.matmul(ps_s[:, j % 4, :], weight("wq", j), norm.xnT[:], start=True, stop=True).then_inc(q_made, 1)
                    for j in range(max(0, NJ - 2), NJ):
                        query_kept(pe, 0, j)

                    def bank(kind, u, g=0):
                        n = use_no[kind, u, g]
                        if n >= NB:
                            freed(pe, n - NB)
                        return n % NB

                    for kind, u in program:
                        seq, t, half = u // (2 * NT), u // 2 % NT, u % 2
                        b = pair * NSEQ + seq
                        if kind == "turn_x":
                            bank("turn_x", 0)
                            norm.tensor(pe, ps_t[:, use_no["turn_x", 0, 0] % NB, :], ready=2 * NT if wide else NT)
                        elif kind == "queries":
                            bank("queries", u)
                            pe.wait_ge(norm.xnT_ready, 2)
                            pe.matmul(bank_q(u), weight("wq", u), norm.xnT[:], start=True, stop=True).then_inc(q_made, 1)
                        elif kind == "scores":
                            if u == 2 * NT:
                                for j in range(max(0, NJ - 2), NJ):
                                    query_kept(pe, 1, j)
                            if u >= 2:
                                pe.wait_ge(shifted, u - 1)
                            for g in range(2):
                                h0 = half * HU + g * G
                                at = 2 * (u % 2) + g
                                if wide:
                                    for h in range(h0, h0 + G, 2):
                                        ins = pe.matmul(ps_s[:, at, (h % G) * SC:(h % G + 2) * SC], QT[:, seq, h // 2, t * P:(t + 1) * P],
                                                        KM[:, b, h:h + 2, :].rearrange("p h s -> p (h s)"), start=True, stop=True)
                                else:
                                    ins = pe.matmul(ps_s[:, at, 0:G * SC], QT[:, seq, 0, t * P:(t + 1) * P],
                                                    KM[:, b, h0:h0 + G, :].rearrange("p h s -> p (h s)"), start=True, stop=True)
                            ins.then_inc(scored, 1)
                        elif kind == "turn":
                            pe.wait_ge(exped, u + 1)
                            for g in range(2):
                                at = bank("turn", u, g)
                                for h in range(G):
                                    ins = pe.transpose(ps_t[0:SC, at, h * P:(h + 1) * P], pr[:, u % 3, g * G + h, :], ident)
                                ins.then_inc(turned, 1)
                        elif kind == "weigh":
                            kept(pe, u, 0)
                            kept(pe, u, 1)
                            if u >= 2:
                                pe.wait_ge(o_ready, u - 1)
                            if not wide and u >= 3 and u % 2 == 1:
                                pe.wait_ge(added, (u - 1) // 2)
                            for h in range(HU):
                                ins = pe.matmul(ps_o[:, u % 2, h * dv:(h + 1) * dv], PTs[:, u % 3, h, :],
                                                V[:, b, half * HU + h, :], start=True, stop=True)
                            ins.then_inc(weighted, 1)
                        elif kind == "turn_o":
                            pe.wait_ge(o_ready, u + 1)
                            turned_o = bank_o("turn_o", u)
                            if wide:
                                bank("turn_o", u)
                                for j in range(4):
                                    ins = pe.transpose(turned_o[:, j * P:(j + 1) * P], O[:, u % 4, j * P:(j + 1) * P], ident)
                            else:
                                both = O[:, u % 4 - 1:u % 4 + 1, :].rearrange("p u n -> p (u n)")
                                ins = pe.transpose(turned_o, both, ident)
                            ins.then_inc(o_turned, 1)
                        else:
                            if wide:
                                bank("out", u)
                            pe.wait_ge(oT_ready, turns_before(u) + 1)
                            result = bank_o("out", u)[:, 0:D]
                            for j in range(NJ):
                                pe.matmul(result, OT[:, u // 2 % 2, j, :], weight("wo", j), start=(j == 0), stop=False)
                            pe.matmul(result, core.ones[:, :], core.row(rows["bo"]), start=False, stop=True).then_inc(out_made, 1)

                @block.scalar
                def _(act):
                    norm.scalar(act, ps_t[:, 0, :])
                    for j in range(0, NJ, 2):
                        keep_query_a(act, 0, j, ps_s[:, j % 4, :])
                    for r in range(NU + 4):
                        u = r - 1
                        if 0 <= u < NU:
                            if u >= 3:
                                act.wait_ge(weighted, u - 2)
                            act.wait_ge(turned, 2 * u + 1)
                            act.activation(PTs[:, u % 3, 0:G, :].rearrange("p h s -> p (h s)"),
                                           ps_t[0:SC, use_no["turn", u, 0] % NB, :], ACT.Copy).then_inc(kept_a, 1)
                        u = r
                        if u < NU:
                            act.wait_ge(shifted, u + 1)
                            if u >= 3:
                                act.wait_ge(turned, 2 * (u - 2))
                                if wide:
                                    act.wait_ge(summed, u - 2)
                            act.activation(pr[:, u % 3], sc[:, u % 2], ACT.Exp, scale=scale).then_inc(exped, 1)
                        if r == 3:
                            norm.scalar(act, ps_t[:, use_no["turn_x", 0, 0] % NB, :], turns=2)
                        for j in queries(r):
                            if j % 2 == 0:
                                keep_query_a(act, 1, j, bank_q(j))
                        u = r - 3
                        if 0 <= u < NU and turns_o(u):
                            act.wait_ge(o_turned, turns_before(u) + 1)
                            if u // 2 >= 2:
                                act.wait_ge(out_made, u // 2 - 1)
                            m = 4 if wide else 1
                            j = (u % 2) * 4 if wide else 0
                            act.activation(OT[:, (u // 2) % 2, j:j + m, :].rearrange("p j s -> p (j s)"),
                                           bank_o("turn_o", u)[:, 0:m * P], ACT.Copy).then_inc(oT_ready, 1)

                @block.vector
                def _(dve):
                    chain = Chain(dve, dve_done)
                    if wide:
                        norm.second(dve, chain)
                    for j in range(1, NJ, 2):
                        keep_query_v(dve, 0, j, ps_s[:, j % 4, :])
                    for r in range(NU + 4):
                        u = r - 4
                        if 0 <= u < NU and u % 2 == 1:
                            x = core.X[:, pair * NSEQ + u // (2 * NT), u // 2 % NT, :]
                            result = bank_o("out", u)[:, 0:D]
                            dve.wait_ge(out_made, u // 2 + 1)
                            if wide:
                                dve.scalar_tensor_tensor(x, result, gate[:], x, ALU.mult, ALU.add).then_inc(added, 1)
                            else:
                                dve.tensor_tensor(x, result, x, ALU.add).then_inc(added, 1)
                        u = r
                        if u < NU:
                            dve.wait_ge(scored, u + 1)
                            top = mx[:, u, :].rearrange("p (g h) -> p g h", g=2)
                            chain.done(dve.tensor_reduce(top, bank_s(u), AX, ALU.max))
                            chain.wait()
                            if u >= 2:
                                dve.wait_ge(exped, u - 1)
                            dve.tensor_tensor(sc[:, u % 2].rearrange("p (g h) s -> p g h s", g=2), bank_s(u),
                                              top.unsqueeze(3).to_broadcast([P, 2, G, SC]), ALU.subtract).then_inc(shifted, 1)
                        u = r - 1
                        if 0 <= u < NU:
                            dve.wait_ge(turned, 2 * u + 2)
                            if u >= 3:
                                dve.wait_ge(weighted, u - 2)
                            dve.tensor_copy(PTs[:, u % 3, G:HU, :].rearrange("p h s -> p (h s)"),
                                            ps_t[0:SC, use_no["turn", u, 1] % NB, :]).then_inc(kept_v, 1)
                            if wide:
                                dve.tensor_reduce(den[:, u, :], pr[:, u % 3], AX, ALU.add).then_inc(summed, 1)
                        for j in queries(r):
                            if j % 2 == 1:
                                keep_query_v(dve, 1, j, bank_q(j))
                        u = r - 2
                        if 0 <= u < NU:
                            if wide:
                                dve.wait_ge(summed, u + 1)
                                chain.done(dve.reciprocal(rden[:, u, :], den[:, u, :]))
                                dve.wait_ge(weighted, u + 1)
                            else:
                                dve.wait_ge(weighted, u + 1)
                                chain.done(dve.reciprocal(rden[:, u, :], outputs(u)[:, :, dh]))
                            chain.wait()
                            if u >= 4:
                                dve.wait_ge(o_turned, u - 3 if wide else (u - 4) // 2 + 1)
                            dve.tensor_tensor(O[:, u % 4, :].rearrange("p (h d) -> p h d", h=HU),
                                              outputs(u)[:, :, 0:dh],
                                              rden[:, u, :].unsqueeze(2).to_broadcast([P, HU, dh]), ALU.mult).then_inc(o_ready, 1)
                        second = core.X[:, pair * NSEQ + 1]
                        following = core.X[:, (pair * NSEQ + NSEQ) % B]
                        if r == 0:
                            norm.statistics(dve, chain, second)
                        if r == 1:
                            dve.wait_ge(norm.turned, 1)
                            norm.normalise(dve, chain, second, signal=not wide)
                            if wide:
                                chain.wait()
                                norm.second(dve, chain)
                        if r == NU:
                            norm.statistics(dve, chain, following)
                        if r == NU + 2:
                            dve.wait_ge(norm.turned, 2)
                            norm.normalise(dve, chain, following)

            st.end_pass()


def feed_forward(core, index, pieces, routing):
    nc = core.nc
    gated = "w3" in pieces
    NE = pieces["w1"][1] // (256 if gated else 512)
    H = pieces["w1"][1] // NE
    NK = H // P
    given = routing == "given"
    passes = 1 if given else B
    picks = {"softmax2": 2, "top2softmax": 2, "argmax": 1, "given": 0}[routing]
    with ExitStack() as ctx:
        st = Step(core, ctx, index, pieces)
        norm = Norm(st)
        hT = st.sb("hT", [P, 2, NK, S])
        act_h = st.sb("act_h", [P, 2, S])
        logit = st.sb("logit", [P, NT, 15])
        top = st.sb("top", [P, NT, 8])
        hit = st.sb("hit", [P, NT, 15])
        e_x = st.sb("e_x", [P, NT, E])
        small = st.sb("small", [P, 3, NT])
        cw = st.sb("cw", [P, NT, NE])
        idx = st.sb("idx", [P, NT, 2])
        cw2 = st.sb("cw2", [P, NT, E])
        ps_r = st.ps("ps_r", [P, BANK])
        ps_a = st.ps("ps_a", [P, 2, BANK])
        ps_g = st.ps("ps_g", [P, 2, BANK])
        ps_y = st.ps("ps_y", [P, 2, BANK])
        dve_done = st.sem("dve_done")
        routed, lx_ready, ex_ready, up_made, act_made, hid_ready, down_made, added = (st.sem(n) for n in (
            "routed", "lx_ready", "ex_ready", "up_made", "act_made", "hid_ready", "down_made", "added"))
        begin(core, index, st)

        def w_up(name, e, k):
            c, _ = pieces[name]
            return st.w[:, c + (e * NK + k) * P:c + (e * NK + k + 1) * P]

        with nc.Fori(0, passes) as b:
            with nc.Block() as block:

                @block.gpsimd
                def _(pool):
                    norm.gpsimd(pool, 0 if given else 1)

                @block.tensor
                def _(pe):
                    norm.tensor(pe, ps_r)
                    pe.wait_ge(norm.xnT_ready, 1)
                    if not given:
                        c, _ = pieces["router"]
                        for t in range(NT):
                            bias = {"argmax": "f2_br", "top2softmax": "f3_br"}.get(routing)
                            ins = pe.matmul(ps_r[:, t * E:(t + 1) * E], norm.xnT[:, t * P:(t + 1) * P], st.w[:, c:c + E],
                                            start=True, stop=bias is None)
                            if bias:
                                ins = pe.matmul(ps_r[:, t * E:(t + 1) * E], core.ones[:, :], core.row(bias), start=False, stop=True)
                        ins.then_inc(routed, 1)

                    def up(e, k):
                        i = e * NK + k
                        if i >= 2:
                            pe.wait_ge(hid_ready, i - 1)
                        ins = pe.matmul(ps_a[:, i % 2, :], w_up("w1", e, k), norm.xnT[:], start=True, stop=True)
                        if gated:
                            ins = pe.matmul(ps_g[:, i % 2, :], w_up("w3", e, k), norm.xnT[:], start=True, stop=True)
                        ins.then_inc(up_made, 1)

                    def down(e):
                        pe.wait_ge(hid_ready, (e + 1) * NK)
                        if e >= 2:
                            pe.wait_ge(added, NT * (e - 1))
                        for t in range(NT):
                            for k in range(NK):
                                ins = pe.matmul(ps_y[:, e % 2, t * D:(t + 1) * D], hT[:, e % 2, k, t * P:(t + 1) * P],
                                                w_up("w2", e, k), start=(k == 0), stop=(k == NK - 1 and routing != "argmax"))
                            if routing == "argmax":
                                ins = pe.matmul(ps_y[:, e % 2, t * D:(t + 1) * D], core.ones[:, :],
                                                core.row("f2_b2", e * D, D), start=False, stop=True)
                        ins.then_inc(down_made, 1)

                    for e in range(NE + 1):
                        for k in range(NK):
                            if e < NE:
                                up(e, k)
                            if k == 0 and e >= 1:
                                down(e - 1)

                @block.scalar
                def _(act):
                    norm.scalar(act, ps_r)
                    if routing in ("softmax2", "top2softmax"):
                        act.wait_ge(lx_ready, 1)
                        act.activation(e_x[:], e_x[:], ACT.Exp).then_inc(ex_ready, 1)
                    for e in range(NE):
                        for k in range(NK):
                            i = e * NK + k
                            act.wait_ge(up_made, i + 1)
                            if gated:
                                if i >= 2:
                                    act.wait_ge(hid_ready, i - 1)
                                act.activation(act_h[:, i % 2, :], ps_a[:, i % 2, :], ACT.Silu).then_inc(act_made, 1)
                            else:
                                if e >= 2:
                                    act.wait_ge(down_made, e - 1)
                                bias = st.piece("b1")[:, i:i + 1] if "b1" in pieces else 0.0
                                act.activation(hT[:, e % 2, k, :], ps_a[:, i % 2, :], ACT.Gelu, bias=bias).then_inc(hid_ready, 1)

                @block.vector
                def _(dve):
                    chain = Chain(dve, dve_done)
                    if NE > E:
                        chain.done(dve.memset(cw[:, :, E:NE], 1.0))
                    if given:
                        wt = st.piece("weights").rearrange("p (t k) -> p t k", t=NT)
                        chain.done(dve.tensor_copy(idx[:], core.indices[:]))
                        chain.wait()
                        for t in range(NT):
                            chain.done(dve.tensor_scalar(cw[:, t, :], core.const("expert_no"), idx[:, t, 0:1], wt[:, t, 0:1], ALU.is_equal, ALU.mult))
                            chain.done(dve.tensor_scalar(cw2[:, t, :], core.const("expert_no"), idx[:, t, 1:2], wt[:, t, 1:2], ALU.is_equal, ALU.mult))
                        chain.wait()
                        chain.done(dve.tensor_tensor(cw[:], cw[:], cw2[:], ALU.add))
                        chain.wait()
                    else:
                        chain.done(dve.memset(logit[:, :, E:15], -BIG))
                        dve.wait_ge(routed, 1)
                        chain.done(dve.tensor_copy(logit[:, :, 0:E], ps_r[:, 0:NT * E].rearrange("p (t e) -> p t e", t=NT)))
                        chain.wait()

                        def softmax():
                            chain.done(dve.tensor_reduce(small[:, 0, :], e_src(), AX, ALU.max))
                            chain.wait()
                            dve.tensor_tensor(e_x[:], e_src(), small[:, 0, :].unsqueeze(2).to_broadcast([P, NT, E]),
                                              ALU.subtract).then_inc(lx_ready, 1)
                            dve.wait_ge(ex_ready, 1)
                            chain.done(dve.tensor_reduce(small[:, 1, :], e_x[:], AX, ALU.add))
                            chain.wait()
                            chain.done(dve.reciprocal(small[:, 2, :], small[:, 1, :]))
                            chain.wait()
                            chain.done(dve.tensor_tensor(softmax_out(), e_x[:], small[:, 2, :].unsqueeze(2).to_broadcast([P, NT, E]), ALU.mult))
                            chain.wait()

                        def choose():
                            for t in range(NT):
                                chain.done(dve.max(top[:, t, :], logit[:, t, 0:E]))
                            chain.wait()
                            chain.done(dve.memset(top[:, :, picks:8], -BIG))
                            chain.wait()
                            for t in range(NT):
                                chain.done(dve.match_replace(hit[:, t, 0:15], top[:, t, :], logit[:, t, :], BIG))
                            chain.wait()
                            chain.done(dve.tensor_scalar(hit[:, :, 0:E], hit[:, :, 0:E], BIG, None, ALU.is_ge))
                            chain.wait()

                        if routing == "softmax2":
                            e_src = softmax_out = lambda: logit[:, :, 0:E]
                            softmax()
                            choose()
                            chain.done(dve.tensor_tensor(cw[:, :, 0:E], hit[:, :, 0:E], logit[:, :, 0:E], ALU.mult))
                        elif routing == "top2softmax":
                            choose()
                            chain.done(dve.tensor_scalar(cw2[:], hit[:, :, 0:E], BIG, BIG, ALU.mult, ALU.subtract))
                            chain.done(dve.tensor_tensor(logit[:, :, 0:E], logit[:, :, 0:E], hit[:, :, 0:E], ALU.mult))
                            chain.wait()
                            chain.done(dve.tensor_tensor(logit[:, :, 0:E], logit[:, :, 0:E], cw2[:], ALU.add))
                            chain.wait()
                            e_src = lambda: logit[:, :, 0:E]
                            softmax_out = lambda: cw[:, :, 0:E]
                            softmax()
                        else:
                            choose()
                            chain.done(dve.tensor_copy(cw[:], hit[:, :, 0:E]))
                        chain.wait()

                    def accumulate(e):
                        dve.wait_ge(down_made, e + 1)
                        for t in range(NT):
                            x = core.X[:, b, t, :]
                            if e >= 1:
                                dve.wait_ge(added, NT * (e - 1) + t + 1)
                            dve.scalar_tensor_tensor(x, ps_y[:, e % 2, t * D:(t + 1) * D], cw[:, t, e:e + 1], x,
                                                     ALU.mult, ALU.add).then_inc(added, 1)

                    for e in range(NE):
                        if gated:
                            for k in range(NK):
                                i = e * NK + k
                                dve.wait_ge(act_made, i + 1)
                                if e >= 2:
                                    dve.wait_ge(down_made, e - 1)
                                dve.tensor_tensor(hT[:, e % 2, k, :], act_h[:, i % 2, :], ps_g[:, i % 2, :], ALU.mult).then_inc(hid_ready, 1)
                        if e >= 1:
                            accumulate(e - 1)
                        if e == 4 and not given:
                            norm.next_statistics(dve, chain, b)
                        if e == 5 and not given:
                            norm.next_normalise(dve, chain, b)
                    accumulate(NE - 1)

            st.end_pass()
        if given:
            with nc.Block() as block:

                @block.tensor
                def _(pe):
                    pe.matmul(ps_r[:, 0:D], core.ones[:, :], core.row("f1_b"), start=True, stop=True).then_inc(routed, 1)

                @block.vector
                def _(dve):
                    dve.wait_ge(routed, 1)
                    x = core.X[:].rearrange("p b t d -> p (b t) d")
                    dve.tensor_tensor(x, ps_r[:, 0:D].unsqueeze(1).to_broadcast([P, B * NT, D]), x, ALU.add)

            st.end_pass()
    if given:
        normalise_first(core, f"after_{index}")


def favor_attention(core, index):
    nc = core.nc
    pieces = FAVOR
    dh, M = 8, 32
    EPS = 1e-6
    F = NH * M
    NF = F // P
    with ExitStack() as ctx:
        st = Step(core, ctx, index, pieces)
        norm = Norm(st)
        proj = st.sb("proj", [P, NH, M])
        qkT = st.sb("qkT", [P, 2, S])
        sq = st.sb("sq", [P, 2, S])
        V1 = st.sb("V1", [P, NT, D + 1])
        sh = st.sb("sh", [P, 2, F])
        ph = st.sb("ph", [P, 2, F])
        phi = st.sb("phi", [P, 2, NT, F])
        mx, cc = st.sb("mx", [P, 2, NT, NH]), st.sb("cc", [P, 2, NT, NH])
        phT = st.sb("phT", [P, 2, NF, P])
        KV = st.sb("KV", [P, NF, D + NH])
        rden = st.sb("rden", [P, NT, NH])
        O, OT = st.sb("O", [P, NT, D]), st.sb("OT", [P, S])
        ps_f = st.ps("ps_f", [P, 2, BANK])
        ps_n = st.ps("ps_n", [P, BANK])
        ps_k = st.ps("ps_k", [P, 2, BANK])
        ps_t = st.ps("ps_t", [P, BANK])
        ps_o = st.ps("ps_o", [P, 2, BANK])
        dve_done = st.sem("dve_done")
        qkv_made, qkv_kept, v_turned, v_ready, n_made, f_made = (st.sem(n) for n in (
            "qkv_made", "qkv_kept", "v_turned", "v_ready", "n_made", "f_made"))
        shifted, exped, phi_ready, kv_made, kv_kept, kv_ready = (st.sem(n) for n in (
            "shifted", "exped", "phi_ready", "kv_made", "kv_kept", "kv_ready"))
        q_turned, qT_ready, weighted, o_ready, o_turned, oT_ready, out_made = (st.sem(n) for n in (
            "q_turned", "qT_ready", "weighted", "o_ready", "o_turned", "oT_ready", "out_made"))
        ident = core.const("ident")
        begin(core, index, st)
        with nc.Block() as block:

            @block.vector
            def _(dve):
                for h in range(NH):
                    dve.tensor_scalar(proj[:, h, :], st.piece("proj"), core.const("head8")[:, h:h + 1], None, ALU.mult)
                for t in range(NT):
                    dve.memset(V1[:, t, D:D + 1], 1.0)

        def bank_t(t):
            return ps_f[:, 0, :] if t % 2 else ps_t[:]

        with nc.Fori(0, B) as b:
            with nc.Block() as block:

                @block.gpsimd
                def _(pool):
                    for u in range(2 * NT):
                        i, t = divmod(u, NT)
                        pool.wait_ge(exped, u + 1)
                        pool.tensor_scalar(phi[:, i, t, :], ph[:, u % 2, :], EPS, float(M) ** -0.5, ALU.add, ALU.mult).then_inc(phi_ready, 1)
                    norm.gpsimd(pool)

                @block.tensor
                def _(pe):
                    norm.tensor(pe, ps_t)
                    pe.wait_ge(norm.xnT_ready, 1)
                    for name, bank in (("wk", ps_f[:, 0, :]), ("wq", ps_f[:, 1, :]), ("wv", ps_k[:, 0, :])):
                        pe.matmul(bank, st.piece(name), norm.xnT[:], start=True, stop=True).then_inc(qkv_made, 1)
                    pe.wait_ge(qkv_kept, 5)
                    for t in range(NT):
                        ins = pe.transpose(ps_t[:, t * P:(t + 1) * P], O[:, t, :], ident)
                    ins.then_inc(v_turned, 1)
                    for i in range(2):
                        for t in range(NT):
                            ins = pe.matmul(ps_n[:, (i * NT + t) * NH:(i * NT + t + 1) * NH], sq[:, i, t * P:(t + 1) * P],
                                            core.const("head8"), start=True, stop=True)
                    ins.then_inc(n_made, 1)
                    def features(u):
                        i, t = divmod(u, NT)
                        if u >= 2:
                            pe.wait_ge(shifted, u - 1)
                        pe.matmul(ps_f[:, u % 2, :], qkT[:, i, t * P:(t + 1) * P], proj[:].rearrange("p h m -> p (h m)"),
                                  start=True, stop=True).then_inc(f_made, 1)

                    def sums(j):
                        pe.wait_ge(phi_ready, NT)
                        pe.wait_ge(v_ready, 1)
                        if j >= 2:
                            pe.wait_ge(kv_kept, j - 1)
                        for t in range(NT):
                            ins = pe.matmul(ps_k[:, j % 2, 0:D + 1], phi[:, 0, t, j * P:(j + 1) * P], V1[:, t, :],
                                            start=(t == 0), stop=(t == NT - 1))
                        ins.then_inc(kv_made, 1)

                    def turn(t):
                        pe.wait_ge(phi_ready, NT + t + 1)
                        if t % 2:
                            pe.wait_ge(shifted, 2 * NT - 1)
                        if t >= 2:
                            pe.wait_ge(qT_ready, t - 1)
                        for j in range(NF):
                            ins = pe.transpose(bank_t(t)[:, j * P:(j + 1) * P], phi[:, 1, t, j * P:(j + 1) * P], ident)
                        ins.then_inc(q_turned, 1)

                    def weigh(t):
                        pe.wait_ge(kv_ready, NF)
                        pe.wait_ge(kv_kept, NF)
                        pe.wait_ge(qT_ready, t + 1)
                        if t >= 2:
                            pe.wait_ge(o_ready, t - 1)
                        for j in range(NF):
                            ins = pe.matmul(ps_o[:, t % 2, 0:D + NH], phT[:, t % 2, j, :], KV[:, j, :],
                                            start=(j == 0), stop=(j == NF - 1))
                        ins.then_inc(weighted, 1)

                    for u in range(2 * NT):
                        features(u)
                        if u >= NT + 2:
                            sums(u - NT - 2)
                    sums(2)
                    turn(0)
                    sums(3)
                    turn(1)
                    for t in range(NT):
                        weigh(t)
                        if t + 2 < NT:
                            turn(t + 2)
                    pe.wait_ge(o_ready, NT)
                    for t in range(NT):
                        ins = pe.transpose(ps_t[:, t * P:(t + 1) * P], O[:, t, :], ident)
                    ins.then_inc(o_turned, 1)
                    pe.wait_ge(oT_ready, 1)
                    for t in range(NT):
                        pe.matmul(ps_n[:, t * D:(t + 1) * D], OT[:, t * P:(t + 1) * P], st.piece("wo"), start=True, stop=False)
                        ins = pe.matmul(ps_n[:, t * D:(t + 1) * D], core.ones[:, :], core.row("a1_bo"), start=False, stop=True)
                    ins.then_inc(out_made, 1)

                @block.scalar
                def _(act):
                    norm.scalar(act, ps_t)
                    scale = float(dh) ** -0.5
                    for i in range(2):
                        act.wait_ge(qkv_made, i + 1)
                        act.activation(qkT[:, i, :], ps_f[:, i, :], ACT.Copy, scale=scale).then_inc(qkv_kept, 1)
                        act.activation(sq[:, i, :], ps_f[:, i, :], ACT.Square, scale=scale).then_inc(qkv_kept, 1)
                    act.wait_ge(qkv_made, 3)
                    act.activation(O[:].rearrange("p t d -> p (t d)"), ps_k[:, 0, :], ACT.Copy).then_inc(qkv_kept, 1)
                    act.wait_ge(v_turned, 1)
                    act.activation(V1[:, :, 0:D], ps_t[:].rearrange("p (t d) -> p t d", t=NT), ACT.Copy).then_inc(v_ready, 1)
                    for u in range(2 * NT):
                        act.wait_ge(shifted, u + 1)
                        if u >= 2:
                            act.wait_ge(phi_ready, u - 1)
                        act.activation(ph[:, u % 2, :], sh[:, u % 2, :], ACT.Exp).then_inc(exped, 1)
                    for t in range(NT):
                        act.wait_ge(q_turned, t + 1)
                        if t >= 2:
                            act.wait_ge(weighted, t - 1)
                        act.activation(phT[:, t % 2].rearrange("p j s -> p (j s)"), bank_t(t), ACT.Copy).then_inc(qT_ready, 1)
                    act.wait_ge(o_turned, 1)
                    act.activation(OT[:], ps_t[:], ACT.Copy).then_inc(oT_ready, 1)

                @block.vector
                def _(dve):
                    chain = Chain(dve, dve_done)
                    dve.wait_ge(n_made, 1)

                    def shift(u):
                        i, t = divmod(u, NT)
                        dve.wait_ge(f_made, u + 1)
                        f = ps_f[:, u % 2, :].rearrange("p (h m) -> p h m", h=NH)
                        chain.done(dve.tensor_reduce(mx[:, i, t, :], f, AX, ALU.max))
                        chain.wait()
                        chain.done(dve.scalar_tensor_tensor(cc[:, i, t, :], ps_n[:, u * NH:(u + 1) * NH], 0.5, mx[:, i, t, :],
                                                            ALU.mult, ALU.add))
                        chain.wait()
                        if u >= 2:
                            dve.wait_ge(exped, u - 1)
                        dve.tensor_tensor(sh[:, u % 2, :].rearrange("p (h m) -> p h m", h=NH), f,
                                          cc[:, i, t, :].unsqueeze(2).to_broadcast([P, NH, M]), ALU.subtract).then_inc(shifted, 1)

                    for u in range(2 * NT):
                        shift(u)
                    blk = st.piece("blk").rearrange("p (j n) -> p j n", j=NF)
                    blkh = st.piece("blkh").rearrange("p (j n) -> p j n", j=NF)
                    for j in range(NF):
                        dve.wait_ge(kv_made, j + 1)
                        dve.tensor_tensor(KV[:, j, 0:D], ps_k[:, j % 2, 0:D], blk[:, j, :], ALU.mult).then_inc(kv_ready, 1)
                        dve.tensor_scalar(KV[:, j, D:D + NH], blkh[:, j, :], ps_k[:, j % 2, D:D + 1], None, ALU.mult).then_inc(kv_kept, 1)
                    for t in range(NT):
                        dve.wait_ge(weighted, t + 1)
                        chain.done(dve.tensor_scalar(rden[:, t, :], ps_o[:, t % 2, D:D + NH], EPS, None, ALU.add))
                        chain.wait()
                        chain.done(dve.reciprocal(rden[:, t, :], rden[:, t, :]))
                        chain.wait()
                        dve.tensor_tensor(O[:, t, :].rearrange("p (h d) -> p h d", h=NH), ps_o[:, t % 2, 0:D].rearrange("p (h d) -> p h d", h=NH),
                                          rden[:, t, :].unsqueeze(2).to_broadcast([P, NH, dh]), ALU.mult).then_inc(o_ready, 1)
                    norm.next_statistics(dve, chain, b)
                    norm.next_normalise(dve, chain, b)
                    dve.wait_ge(out_made, 1)
                    x = core.X[:, b].rearrange("p t d -> p (t d)")
                    dve.tensor_tensor(x, ps_n[:], x, ALU.add)

            st.end_pass()


def talking_attention(core, index):
    nc = core.nc
    pieces = TALK
    dh, NM, TOP = 64, 64, 64
    NJ = NH * dh // P
    Q = 64
    R = 8
    NUNIT, NG = S // Q, Q // R
    NGROUP = NUNIT * NG
    LAG_E, LAG_M = 2, 4
    scale = float(dh) ** -0.5
    ROUNDS = TOP // 8
    SPLIT = 384
    NDT = 5
    NORM_AT = 40
    NC = NT + 1

    MIDDLE = NUNIT // 2 + 1
    ORDER = [MIDDLE] + [u for u in reversed(range(NUNIT)) if u != MIDDLE]

    def unit(q):
        return ORDER[q % NUNIT]

    def rows_of(q, c):
        return NM if c == NT else max(0, min(P, Q * (unit(q) + 1) - P * c))

    def chunks(q):
        return [c for c in range(NC) if rows_of(q, c)]

    def width(g):
        return NM + Q * unit(g // NG) + R * (g % NG + 1)

    def is_split(g):
        return width(g) >= SPLIT

    def rounds(half):
        return ROUNDS // (1 + half)

    def marks(g):
        halves = (0, 1) if is_split(g) else (0,)
        out = ["mask"] + [("split", half) for half in halves if is_split(g)]
        for r in range(ROUNDS):
            out += [("top", r, half) for half in halves if r < rounds(half)]
            out += [("out", r, half) for half in halves if r < rounds(half) - 1]
        return out + (["pair_up", "merge"] if is_split(g) else []) + ["choose"]

    MARKS = [marks(g) for g in range(NGROUP)]

    def mark(g, name):
        return sum(len(MARKS[x]) for x in range(g % 2, g, 2)) + MARKS[g].index(name) + 1

    with ExitStack() as ctx:
        st = Step(core, ctx, index, pieces)
        norm = Norm(st)
        QB = st.sb("QB", [P, 2, NJ, 2, Q])
        KT = st.sb("KT", [P, NJ, S])
        spare = core.arena[(index + 1) % 2][:, NATT8:ARENA]
        V = spare[:, 0:NT * NJ * P].rearrange("p (t n) -> p t n", t=NT)
        W = spare[:, NT * NJ * P:NT * NJ * P + 2 * (NM + S)].rearrange("p (a n) -> p a n", a=2)
        S1 = spare[:, NT * NJ * P + 2 * (NM + S):NT * NJ * P + 4 * (NM + S)].rearrange("p (a n) -> p a n", a=2)
        at = NT * NJ * P + 4 * (NM + S)
        post = spare[:, at:at + 4 * P].rearrange("p (a n) -> p a n", a=4)
        OT = spare[:, at + 4 * P:at + 4 * P + NJ * Q].rearrange("p (j s) -> p j s", j=NJ)
        ST = st.sb("ST", [P, 2, NC, NG, NH, R])
        Dt = st.sb("Dt", [P, NDT, NM + S])
        Ex = st.sb("Ex", [P, 3, NM + S])
        A = st.sb("A", [P, 4, NM + S])
        top = st.sb("top", [P, 4, ROUNDS, 8])
        top1 = st.sb("top1", [P, 4, 1 + TOP // 2])
        least = st.sb("least", [P, 4, 1 + TOP // 2])
        kth = st.sb("kth", [P, 4])
        nb = st.sb("nb", [P, 4])
        den, rden = st.sb("den", [P, 2]), st.sb("rden", [P, 4])
        AT = st.sb("AT", [P, NC, NH, Q])
        ps_t = st.ps("ps_t", [P, 2, BANK])
        ps_m = st.ps("ps_m", [P, 2, BANK])
        ps_c = st.ps("ps_c", [P, 2, BANK])
        ps_o = st.ps("ps_o", [P, BANK])
        ps_x = st.ps("ps_x", [P, BANK])
        dve_done = st.sem("dve_done")
        made, kept, qk_made, st_kept, turned, s_kept, mixed, m_kept = (st.sem(n) for n in (
            "made", "kept", "qk_made", "st_kept", "turned", "s_kept", "mixed", "m_kept"))
        k_made, k_kept = st.sem("k_made"), st.sem("k_kept")
        step = (st.sem("step_even"), st.sem("step_odd"))
        nb_ready, exped, chosen, cleared, post_ready, back, at_kept = (st.sem(n) for n in (
            "nb_ready", "exped", "chosen", "cleared", "post_ready", "back", "at_kept"))
        weighted, oT_ready, out_made, added, q_made, q_kept = (st.sem(n) for n in (
            "weighted", "oT_ready", "out_made", "added", "q_made", "q_kept"))
        ident = core.const("ident")
        begin(core, index, st)
        wcol = {n: pieces[n][0] for n in pieces}
        memk = st.piece("memk").rearrange("p (j m) -> p j m", j=NJ)

        def keys(j, c, n):
            return memk[:, j, :] if c == NT else KT[:, j, c * P:c * P + n]

        with nc.Block() as block:

            @block.vector
            def _(dve):
                dve.memset(QB[:], 0.0)
                dve.memset(top1[:, :, 0:1], BIG)

        def st_before(q):
            return sum(len(chunks(x)) for x in range(q))

        def back_parts(g):
            cs = chunks(g // NG)
            return [cs[:4], cs[4:]] if len(cs) > 4 else [cs]

        def back_before(g):
            return sum(len(back_parts(x)) for x in range(g))

        def v_parts(n):
            return [n] if n < 2 * NT else []

        def st_parts(n):
            q, k = n // NG + 1, n % NG
            if q >= NUNIT:
                return []
            first = NG - len(chunks(q))
            return [(q, k - first)] if k >= first else []

        def new_queries(n):
            return [q for q, i in st_parts(n + 1) if i == 0]

        def q_made_by(n):
            return sum(1 for x in range(min(n, NGROUP)) for _ in new_queries(x)) + (n > NGROUP + 1)

        def outputs_by(n):
            return max(0, (n - LAG_M + 1) // NG)

        def st_done(n):
            return sum(len(st_parts(x)) for x in range(n))

        def st_no(q):
            return st_before(q) - st_before(1) if q else 0

        def q_no(q):
            return max(q, 1)

        def bank_k(i):
            return (ps_t, ps_m)[i % 4 // 2][:, i % 2, :]

        def bank_s(q, n):
            return (ps_t, ps_m)[n % 2] if q % NUNIT == 0 else ps_c

        def reached(engine, sem, n):
            if n > 0:
                engine.wait_ge(sem, n)

        def queries(pe, q, n):
            reached(pe, oT_ready, 4 * outputs_by(n) - 2)
            for j in range(NJ):
                c = wcol["wq"] + j * P
                ins = pe.matmul(ps_o[:, j * Q:(j + 1) * Q], st.w[:, c:c + P],
                                norm.xnT[:, unit(q) * Q:(unit(q) + 1) * Q], start=True, stop=True)
            ins.then_inc(q_made, 1)

        def keep_queries(act, q):
            act.wait_ge(q_made, q_no(q))
            made_q = ps_o[:].rearrange("p (j s) -> p j s", j=NJ)
            for par in range(2):
                rows = slice(64 * par, 64 * par + 64)
                act.activation(QB[rows, q % 2, :, par, :], made_q[rows], ACT.Copy).then_inc(q_kept, 1)

        def unit_scores(pe, q, n):
            if n == 0:
                pe.wait_ge(q_kept, 2 * q_no(q))
            c = chunks(q)[n]
            r = rows_of(q, c)
            for j in range(NJ):
                ins = pe.matmul(bank_s(q, n)[0:r, j // 4, (j % 4) * P:(j % 4 + 1) * P], keys(j, c, r),
                                QB[:, q % 2, j].rearrange("p a s -> p (a s)"), start=True, stop=True)
            ins.then_inc(qk_made, 1)

        def keep_unit(act, q, n):
            c = chunks(q)[n]
            r = rows_of(q, c)
            act.wait_ge(qk_made, st_no(q) + n + 1)
            if q >= 2:
                act.wait_ge(turned, (q - 1) * NG)
            act.activation(ST[0:r, q % 2, c].rearrange("p k h r -> p h k r"),
                           bank_s(q, n)[0:r].rearrange("p a (h k r) -> p (a h) k r", h=NJ, k=NG), ACT.Copy).then_inc(st_kept, 1)

        def first_scores(part):
            return range(2 * (part - 2), min(2 * (part - 1), len(chunks(0))))

        def open_tensor(pe, part, q, n):
            if part == 0:
                norm.tensor(pe, ps_m[:, 0, :], ready=NT if q else 0)
                pe.wait_ge(norm.xnT_ready, 1)
            if part < 2:
                for i in range(4 * part, 4 * part + 4):
                    reached(pe, k_kept, i - 3)
                    c = wcol["wk"] + i * P
                    pe.matmul(bank_k(i), st.w[:, c:c + P], norm.xnT[:], start=True, stop=True).then_inc(k_made, 1)
            if part == 1:
                queries(pe, q, n)
            if part == 2:
                pe.wait_ge(k_kept, NJ)
            if part >= 2:
                for x in first_scores(part):
                    if x >= 2:
                        pe.wait_ge(st_kept, st_no(q) + x - 1)
                    unit_scores(pe, q, x)

        def open_scalar(act, part, q):
            if part == 0:
                norm.scalar(act, ps_m[:, 0, :])
            if part < 2:
                for i in range(4 * part, 4 * part + 4):
                    act.wait_ge(k_made, i + 1)
                    act.activation(KT[:, i, :], bank_k(i), ACT.Copy).then_inc(k_kept, 1)
            if part == 1:
                keep_queries(act, q)
            if part >= 2:
                for x in first_scores(part):
                    keep_unit(act, q, x)

        with nc.Block() as block:

            @block.tensor
            def _(pe):
                for part in range(5):
                    open_tensor(pe, part, 0, 0)

            @block.scalar
            def _(act):
                for part in range(5):
                    open_scalar(act, part, 0)

        st.end_pass()

        with nc.Fori(0, B) as b:
            with nc.Block() as block:

                @block.gpsimd
                def _(pool):
                    def bias(g):
                        pool.wait_ge(step[g % 2], mark(g, ("top", 0, 0)))
                        if g >= 4:
                            pool.wait_ge(exped, g - 3)
                        pool.tensor_scalar(nb[:, g % 4:g % 4 + 1], top[:, g % 4, 0, 0:1], -scale, 0.0, ALU.mult,
                                           ALU.add).then_inc(nb_ready, 1)

                    def clear(g):
                        w, wu = width(g), NM + Q * (unit(g // NG) + 1)
                        if w < wu:
                            if g >= 4:
                                pool.wait_ge(back, back_before(g - 3))
                            pool.memset(A[:, g % 4, w:wu], 0.0).then_inc(cleared, 1)

                    def weights(g):
                        pool.wait_ge(chosen, g + 1)
                        if g >= 4:
                            pool.wait_ge(back, back_before(g - 3))
                        pool.tensor_scalar(post[:, g % 4, :], st.piece("post"), rden[:, g % 4:g % 4 + 1], 0.0, ALU.mult,
                                           ALU.add).then_inc(post_ready, 1)

                    for g in range(0, NGROUP, 2):
                        for part in (bias, clear, weights):
                            part(g)
                            part(g + 1)
                        if g == NORM_AT:
                            norm.gpsimd(pool)

                @block.tensor
                def _(pe):
                    def values(i):
                        t, half = divmod(i, 2)
                        c = wcol["wv"] + half * BANK
                        pe.matmul(ps_c[:, 0, :], norm.xnT[:, t * P:(t + 1) * P], st.w[:, c:c + BANK],
                                  start=True, stop=True).then_inc(made, 1)

                    def turn(g):
                        q, k = divmod(g, NG)
                        cs = chunks(q)
                        reached(pe, st_kept, st_no(q) + (len(cs) if q else 0))
                        if g >= 1:
                            pe.wait_ge(s_kept, 2 * g)
                        for c in cs:
                            r = rows_of(q, c)
                            out = ps_t[:, 1, 0:NM] if c == NT else ps_t[:, 0, c * P:c * P + r]
                            ins = pe.transpose(out, ST[0:r, q % 2, c, k].rearrange("p h r -> p (h r)"), ident[0:r, 0:r])
                        ins.then_inc(turned, 1)

                    def mix(g):
                        w = width(g)
                        pe.wait_ge(s_kept, 2 * (g + 1))
                        if g >= 1:
                            pe.wait_ge(m_kept, 2 * g)
                        pe.matmul(ps_m[:, 1, 0:NM], st.piece("pre"), S1[:, g % 2, 0:NM], start=True, stop=True)
                        pe.matmul(ps_m[:, 0, 0:w - NM], st.piece("pre"), S1[:, g % 2, NM:w], start=True, stop=True).then_inc(mixed, 1)

                    def mix_back(g):
                        q = g // NG
                        pe.wait_ge(post_ready, g + 1)
                        if g % NG != NG - 1:
                            pe.wait_ge(cleared, g + 1 - g // NG)
                        for i, part in enumerate(back_parts(g)):
                            n = back_before(g) + i
                            if n >= 2:
                                pe.wait_ge(at_kept, n - 1)
                            for x, c in enumerate(part):
                                r = rows_of(q, c)
                                cols = slice(0, NM) if c == NT else slice(NM + c * P, NM + c * P + r)
                                ins = pe.matmul(ps_c[0:r, n % 2, x * P:(x + 1) * P], A[:, g % 4, cols], post[:, g % 4, :],
                                                start=True, stop=True)
                            ins.then_inc(back, 1)

                    def unit_out(q, half):
                        if half == 0:
                            pe.wait_ge(q_kept, 2 * q_made_by((q + 1) * NG - 1 + LAG_M))
                        elif q >= 1:
                            pe.wait_ge(added, q)
                        pe.wait_ge(at_kept, back_before((q + 1) * NG))
                        cs = chunks(q)
                        for j in range(4 * half, 4 * half + 4):
                            for n, c in enumerate(cs):
                                r = rows_of(q, c)
                                v = st.w[0:r, wcol["memv"] + j * P:wcol["memv"] + (j + 1) * P] if c == NT else V[0:r, c, j * P:(j + 1) * P]
                                ins = pe.matmul((ps_o, ps_x)[half][:, (j % 4) * P:(j % 4 + 1) * P], v,
                                                AT[0:r, c, 2 * j:2 * j + 2, :].rearrange("p h s -> p (h s)"),
                                                start=(n == 0), stop=(n == len(cs) - 1))
                        ins.then_inc(weighted, 1)

                    def project(q):
                        pe.wait_ge(oT_ready, 4 * (q + 1))
                        out = ps_x[64 * (unit(q) % 2):64 * (unit(q) % 2) + 64, 0:D]
                        for j in range(NJ):
                            c = wcol["wo"] + j * D
                            pe.matmul(out, OT[:, j, :], st.w[:, c:c + D], start=(j == 0), stop=False)
                        pe.matmul(out, core.ones[:, 0:Q], core.row("a2_bo"), start=False, stop=True).then_inc(out_made, 1)

                    for n in range(NGROUP + LAG_M + 1):
                        if n < NGROUP:
                            turn(n)
                            mix(n)
                        g = n - LAG_M
                        ended = g // NG - 1 if g > 0 and g % NG == 0 else None
                        if ended is not None:
                            unit_out(ended, 1)
                        if 0 <= g < NGROUP:
                            reached(pe, st_kept, st_done(n))
                            pe.wait_ge(kept, min(2 * NT, n))
                            mix_back(g)
                            if g % NG == NG - 1:
                                unit_out(g // NG, 0)
                        if ended is not None:
                            project(ended)
                        for i in v_parts(n):
                            reached(pe, st_kept, st_done(n))
                            reached(pe, kept, i)
                            if g >= 0:
                                pe.wait_ge(at_kept, back_before(g + 1))
                            values(i)
                        for q, i in st_parts(n):
                            reached(pe, st_kept, st_done(n))
                            pe.wait_ge(kept, min(2 * NT, n + 1))
                            if g >= 0:
                                pe.wait_ge(at_kept, back_before(g + 1))
                            unit_scores(pe, q, i)
                        for q in new_queries(n):
                            queries(pe, q, n)
                        if n >= NGROUP:
                            if n == NGROUP:
                                pe.wait_ge(s_kept, 2 * NGROUP)
                                pe.wait_ge(m_kept, 2 * NGROUP)
                            open_tensor(pe, n - NGROUP, NUNIT, n)

                @block.scalar
                def _(act):
                    def keep_values(i):
                        t, half = divmod(i, 2)
                        act.wait_ge(made, i + 1)
                        act.activation(V[:, t, half * BANK:(half + 1) * BANK], ps_c[:, 0, :], ACT.Copy).then_inc(kept, 1)

                    def keep_scores(g):
                        w = width(g)
                        act.wait_ge(turned, g + 1)
                        if g >= 2:
                            act.wait_ge(mixed, g - 1)
                        act.activation(S1[:, g % 2, 0:NM], ps_t[:, 1, 0:NM], ACT.Copy).then_inc(s_kept, 1)
                        act.activation(S1[:, g % 2, NM:w], ps_t[:, 0, 0:w - NM], ACT.Copy).then_inc(s_kept, 1)
                        act.wait_ge(mixed, g + 1)
                        if g >= NDT:
                            act.wait_ge(chosen, g - NDT + 1)
                        act.activation(Dt[:, g % NDT, 0:NM], ps_m[:, 1, 0:NM], ACT.Copy).then_inc(m_kept, 1)
                        act.activation(Dt[:, g % NDT, NM:w], ps_m[:, 0, 0:w - NM], ACT.Copy).then_inc(m_kept, 1)

                    def exponentials(g):
                        w = width(g)
                        act.wait_ge(nb_ready, g + 1)
                        if g >= 3:
                            act.wait_ge(chosen, g - 2)
                        act.activation(Ex[:, g % 3, 0:w], Dt[:, g % NDT, 0:w], ACT.Exp, bias=nb[:, g % 4:g % 4 + 1],
                                       scale=scale).then_inc(exped, 1)

                    def keep_back(g):
                        q, k = divmod(g, NG)
                        for i, part in enumerate(back_parts(g)):
                            n = back_before(g) + i
                            act.wait_ge(back, n + 1)
                            if q >= 1:
                                act.wait_ge(weighted, 2 * q)
                            full = [x for x, c in enumerate(part) if rows_of(q, c) == P]
                            rest = [x for x, c in enumerate(part) if rows_of(q, c) != P]
                            src = ps_c[:, n % 2, :].rearrange("p (c h r) -> p c h r", c=4, h=NH)
                            todo = []
                            if full:
                                todo.append((P, part[full[0]], full[0], len(full)))
                            todo += [(rows_of(q, part[x]), part[x], x, 1) for x in rest]
                            for r, c, x, m in todo:
                                for y in range(m):
                                    ins = act.activation(AT[0:r, c + y, :, k * R:(k + 1) * R], src[0:r, x + y], ACT.Copy)
                            ins.then_inc(at_kept, 1)

                    def keep_outputs(q, half):
                        act.wait_ge(weighted, 2 * q + half + 1)
                        if q >= 1 and half == 0:
                            act.wait_ge(out_made, q)
                        o = (ps_o, ps_x)[half][:].rearrange("p (j a s) -> p j a s", j=4, a=2)
                        for par in range(2):
                            rows = slice(64 * par, 64 * par + 64)
                            act.activation(OT[rows, 4 * half:4 * half + 4, :], o[rows, :, par, :],
                                           ACT.Copy).then_inc(oT_ready, 1)

                    for n in range(NGROUP + LAG_M + 1):
                        if n < NGROUP:
                            keep_scores(n)
                        if 0 <= n - LAG_E < NGROUP:
                            exponentials(n - LAG_E)
                        g = n - LAG_M
                        if g > 0 and g % NG == 0:
                            keep_outputs(g // NG - 1, 1)
                        if 0 <= g < NGROUP:
                            keep_back(g)
                            if g % NG == NG - 1:
                                keep_outputs(g // NG, 0)
                        for i in v_parts(n):
                            keep_values(i)
                        for q, i in st_parts(n):
                            keep_unit(act, q, i)
                        for q in new_queries(n):
                            keep_queries(act, q)
                        if n >= NGROUP:
                            open_scalar(act, n - NGROUP, NUNIT)

                @block.vector
                def _(dve):
                    chain = Chain(dve, dve_done)

                    def residual(q):
                        rows = slice(64 * (unit(q) % 2), 64 * (unit(q) % 2) + 64)
                        x = core.X[rows, b, unit(q) // 2, :]
                        dve.wait_ge(out_made, q + 1)
                        dve.tensor_tensor(x, ps_x[rows, 0:D], x, ALU.add).then_inc(added, 1)

                    def prepare(g):
                        w = width(g)
                        dve.wait_ge(m_kept, 2 * (g + 1))
                        own = Dt[:, g % NDT, w - R:w]
                        if g >= 4:
                            dve.wait_ge(nb_ready, g - 3)
                        dve.tensor_tensor(own, own, core.const("later"), ALU.add).then_inc(step[g % 2], 1)

                    def split(g, half):
                        m = width(g) // 2
                        dve.wait_ge(step[g % 2], mark(g, "mask"))
                        dve.tensor_tensor(W[:, g % 2, half * m:half * m + m], Dt[:, g % NDT, 0:m], Dt[:, g % NDT, m:2 * m],
                                          (ALU.max, ALU.min)[half]).then_inc(step[g % 2], 1)

                    def source(g, r, half):
                        w = width(g)
                        if is_split(g):
                            return W[:, g % 2, half * (w // 2):(half + 1) * (w // 2)]
                        return Dt[:, g % NDT, 0:w] if r == 0 else W[:, g % 2, 0:w]

                    def eight(g, r, half):
                        return top1[:, g % 4, 1 + 8 * r:9 + 8 * r] if half else top[:, g % 4, r, :]

                    def largest(g, r, half):
                        before = ("out", r - 1, half) if r else ("split", half) if is_split(g) else "mask"
                        dve.wait_ge(step[g % 2], mark(g, before))
                        dve.max(eight(g, r, half), source(g, r, half)).then_inc(step[g % 2], 1)

                    def take_out(g, r, half):
                        dve.wait_ge(step[g % 2], mark(g, ("top", r, half)))
                        dve.match_replace(source(g, 1, half), eight(g, r, half), source(g, r, half), -BIG).then_inc(step[g % 2], 1)

                    def pair_up(g):
                        dve.wait_ge(step[g % 2], mark(g, ("top", ROUNDS - 1, 0)))
                        falling = top[:, g % 4].rearrange("p r n -> p (r n)")[:, TOP - 1:TOP // 2 - 2:-1]
                        dve.tensor_tensor(least[:, g % 4, :], falling, top1[:, g % 4, :], ALU.min).then_inc(step[g % 2], 1)

                    def merge(g):
                        dve.wait_ge(step[g % 2], mark(g, "pair_up"))
                        dve.tensor_reduce(kth[:, g % 4:g % 4 + 1], least[:, g % 4, :], AX, ALU.max).then_inc(step[g % 2], 1)

                    def choose(g):
                        w = width(g)
                        dve.wait_ge(step[g % 2], mark(g, MARKS[g][-2]))
                        dve.wait_ge(exped, g + 1)
                        if g >= 4:
                            dve.wait_ge(back, back_before(g - 3))
                            dve.wait_ge(post_ready, g - 3)
                        least_kept = kth[:, g % 4:g % 4 + 1] if is_split(g) else top[:, g % 4, ROUNDS - 1, 7:8]
                        dve.scalar_tensor_tensor(A[:, g % 4, 0:w], Dt[:, g % NDT, 0:w], least_kept,
                                                 Ex[:, g % 3, 0:w], ALU.is_ge, ALU.mult,
                                                 accum_out=den[:, g % 2:g % 2 + 1]).then_inc(step[g % 2], 1)

                    def invert(g):
                        dve.wait_ge(step[g % 2], mark(g, "choose"))
                        dve.reciprocal(rden[:, g % 4:g % 4 + 1], den[:, g % 2:g % 2 + 1]).then_inc(chosen, 1)

                    for g in range(0, NGROUP, 2):
                        pair = (g, g + 1)
                        for x in pair:
                            prepare(x)
                        halves = [(x, half) for half in (0, 1) for x in pair if half == 0 or is_split(x)]
                        for x, half in halves:
                            if is_split(x):
                                split(x, half)
                        for r in range(ROUNDS):
                            for x, half in halves:
                                if r < rounds(half):
                                    largest(x, r, half)
                            for x, half in halves:
                                if r < rounds(half) - 1:
                                    take_out(x, r, half)
                        for x in pair:
                            if is_split(x):
                                pair_up(x)
                        for x in pair:
                            if is_split(x):
                                merge(x)
                        for x in pair:
                            choose(x)
                        for x in pair:
                            invert(x)
                        if (g + 2) % NG == 0 and g >= NG:
                            residual(g // NG - 1)
                        if g == NORM_AT:
                            norm.next_statistics(dve, chain, b)
                            norm.normalise(dve, chain, core.X[:, (b + 1) % B], signal=True)
                    residual(NUNIT - 1)

            st.end_pass()


def build(nc, ins, out):
    core = Core()
    core.nc = nc
    core.order = list(SUBLAYERS)
    core.packed = {i: ins[f"w{i}"] for i in core.order}
    with ExitStack() as ctx:
        def sb(name, shape, dt=F32):
            return ctx.enter_context(nc.sbuf_tensor(name, shape, dt))

        core.X = sb("X", [P, B, NT, D])
        core.ln_stats, core.ln_mv = sb("ln_stats", [P, NT, 6]), sb("ln_mv", [P, NT, 2])
        core.ln_var, core.ln_rstd = sb("ln_var", [P, NT]), sb("ln_rstd", [P, NT])
        core.xn = sb("xn", [P, NT, D])
        core.consts = sb("consts", [P, NCONST])
        core.rows = sb("rows", [1, NROWS])
        core.ones = sb("ones", [1, P])
        core.ctxT = sb("ctxT", [P, B, SC])
        core.indices = sb("indices", [P, NT, 2], I32)
        core.arena = [sb("arena_even", [P, ARENA]), sb("arena_odd", [P, ARENA])]
        core.arrived = [ctx.enter_context(nc.semaphore("arrived_even")), ctx.enter_context(nc.semaphore("arrived_odd"))]
        loaded = ctx.enter_context(nc.semaphore("loaded"))
        stored = ctx.enter_context(nc.semaphore("stored"))
        with nc.Block() as block:

            @block.sync
            def _(sp):
                first = core.order[0]
                sp.dma_start(core.X[:].rearrange("p b t d -> p (b t d)"), ins["x"]).then_inc(loaded, 16)
                sp.dma_start(core.consts[:], ins["consts"]).then_inc(loaded, 16)
                sp.dma_start(core.arena[first % 2][:, 0:WIDTHS[first]], core.packed[first]).then_inc(core.arrived[first % 2], 16)
                sp.dma_start(core.rows[:], ins["rows"]).then_inc(loaded, 16)
                sp.dma_start(core.ctxT[:].rearrange("p b s -> p (b s)"), ins["ctxT"]).then_inc(loaded, 16)
                sp.dma_start(core.indices[:].rearrange("p t k -> p (t k)"), ins["indices"]).then_inc(loaded, 16)
                sp.wait_ge(loaded, 5 * 16)

            @block.vector
            def _(dve):
                dve.memset(core.ones[:], 1.0)

        normalise_first(core, "first")
        for i in core.order:
            PROGRAMS[i](core, i)
        with nc.Block() as block:

            @block.sync
            def _(sp):
                sp.dma_start(out, core.X[:].rearrange("p b t d -> p (b t d)")).then_inc(stored, 16)
                sp.wait_ge(stored, 16)


PROGRAMS = {
    0: lambda c, i: self_attention(c, i, SELF_ROPE, {"bo": "zero"}, True),
    1: lambda c, i: cross_attention(c, i, ATT8, {"bv": "x0_bv", "bo": "x0_bo"}, 8),
    2: lambda c, i: feed_forward(c, i, FF0, "softmax2"),
    3: lambda c, i: favor_attention(c, i),
    4: lambda c, i: cross_attention(c, i, ATT64, {"bv": "x1_bv", "bo": "x1_bo"}, 64),
    5: lambda c, i: feed_forward(c, i, FF1, "given"),
    6: lambda c, i: talking_attention(c, i),
    7: lambda c, i: cross_attention(c, i, ATT8, {"bv": "x2_bv", "bo": "x2_bo"}, 8),
    8: lambda c, i: feed_forward(c, i, FF2, "argmax"),
    9: lambda c, i: self_attention(c, i, SELF_PRIOR, {"bo": "a3_bo"}, False),
    10: lambda c, i: cross_attention(c, i, ATT8, {"bv": "zero", "bo": "x3_bo"}, 8),
    11: lambda c, i: feed_forward(c, i, FF3, "top2softmax"),
}


def _tokens(x):
    return x.reshape(-1, P, x.shape[-1]).transpose(1, 0, 2).reshape(P, -1)


def _pack(pieces, given):
    total = max(c + n for c, n in pieces.values())
    out = np.zeros((P, total), np.float32)
    for name, (c, n) in pieces.items():
        if name in given:
            a = given[name]
            out[:a.shape[0], c:c + n] = a.reshape(a.shape[0], n)
    return out


def _spread_heads(w):
    out = np.zeros((NH, 8, NH, 8), np.float32)
    for i in range(8):
        out[:, i, :, i] = w
    return out.reshape(P, P)


def _constants():
    p = np.arange(P)
    consts = _pack(CONST, {
        "ident": np.eye(P, dtype=np.float32),
        "head8": (p[:, None] // 8 == np.arange(NH)[None]).astype(np.float32),
        "head64": (p[:, None] // 64 == np.arange(NH)[None] % 2).astype(np.float32),
        "expert_no": np.broadcast_to(np.arange(E, dtype=np.float32), (P, E)),
        "minus_half": np.full((P, NT), -0.5, np.float32),
        "minus_one": np.full((P, 2), -1.0, np.float32),
        "later": np.where(np.arange(8)[None] > p[:, None] % 8, -BIG, 0.0).astype(np.float32),
    })
    pos = np.arange(S, dtype=np.float32)
    freq = np.float32(10000.0) ** (-np.arange(0, 8, 2, dtype=np.float32) / np.float32(8))
    angle = (pos[:, None] * freq[None]).astype(np.float32)[:, (p % 8) // 2].T
    sign = np.where(p % 2 == 0, -1.0, 1.0).astype(np.float32)[:, None]
    swap = (p[:, None] == (p ^ 1)[None]).astype(np.float32)
    q = (np.arange(NT)[None, :, None] * P + p[:, None, None]).astype(np.float32)
    k = np.arange(S, dtype=np.float32)[None, None]
    causal = np.where(k > q, BIG, 0.0).astype(np.float32)
    gauss = np.zeros((P, NT, S), np.float32)
    for period, weight, sigma in ((1.0, 0.8, 0.5), (30.0, 0.4, 2.0)):
        gauss = gauss + np.float32(weight) * np.exp(-(np.abs(q - k) - np.float32(period)) ** 2 / np.float32(2.0 * sigma ** 2))
    rope = {"cos": np.cos(angle), "sin": np.sin(angle) * sign, "swap": swap, "causal": causal.reshape(P, -1)}
    return consts, rope, gauss.reshape(P, -1).astype(np.float32)


def _layouts(a):
    consts, rope, gauss = _constants()

    p, j = np.arange(P), np.arange(4)
    own = (4 * j[None, :, None] + p[:, None, None] // 32 == np.arange(NH)[None, None]).astype(np.float32)
    favor_blocks, favor_heads = np.repeat(own, 8, axis=2).reshape(P, -1), own.reshape(P, -1)

    def att(prefix, names, bq=None, bk=None, bv=None):
        g = {k: a[prefix + n].T for k, n in zip(("wq", "wk", "wv", "wo"), names)}
        for k, n in (("bq", bq), ("bk", bk), ("bv", bv)):
            if n:
                g[k] = a[prefix + n].reshape(P, 1)
        return g

    def up(w):
        return w.transpose(1, 0, 2).reshape(P, -1)

    def down(w):
        e, h, d = w.shape
        return w.reshape(e, h // P, P, d).transpose(2, 0, 1, 3).reshape(P, -1)

    def tiles(w):
        return w.reshape(-1, P, w.shape[1]).transpose(1, 0, 2).reshape(P, -1)

    cap = ("Wq", "Wk", "Wv", "Wo")
    low = ("w_q", "w_k", "w_v", "w_o")
    spread = lambda v: np.broadcast_to(v, (P, v.shape[-1]))
    kv = a["L1_xattn_w_kv"]
    ins = {
        "w0": _pack(SELF_ROPE, {**att("L0_attn_", cap), **rope}),
        "w1": _pack(ATT8, att("L0_xattn_", cap, "bq", "bk")),
        "w2": _pack(FF0, {"w1": up(a["L0_ffn_w1"]), "w3": up(a["L0_ffn_w3"]), "w2": down(a["L0_ffn_w2"]),
                          "router": a["L0_ffn_gate_w"].T}),
        "w3": _pack(FAVOR, {**att("L1_attn_", cap), "proj": a["L1_attn_proj"].transpose(0, 2, 1).reshape(P, 32),
                            "blk": favor_blocks, "blkh": favor_heads}),
        "w4": _pack(ATT64, {"wq": a["L1_xattn_w_q"], "wk": kv[:, :1024], "wv": kv[:, 1024:], "wo": tiles(a["L1_xattn_w_out"]),
                            "gamma": spread(a["L1_xattn_ln_gamma"]), "beta": spread(a["L1_xattn_ln_beta"]),
                            "gate": spread(a["L1_xattn_gate"])}),
        "w5": _pack(FF1, {"w1": up(a["L1_ffn_w1"]), "w2": down(a["L1_ffn_w2"]),
                          "weights": _tokens(a["L1_ffn_expert_weights"])}),
        "w6": _pack(TALK, {"wq": a["L2_attn_Wq"].T, "wk": a["L2_attn_Wk"].T, "wv": a["L2_attn_Wv"].T,
                           "wo": tiles(a["L2_attn_Wout"].T),
                           "memk": a["L2_attn_mem_k"].reshape(8, 2, 64, 64).transpose(1, 3, 0, 2).reshape(P, 512),
                           "memv": a["L2_attn_mem_v"].transpose(1, 0, 2).reshape(64, 1024),
                           "pre": _spread_heads(a["L2_attn_pre_proj"]), "post": _spread_heads(a["L2_attn_post_proj"])}),
        "w7": _pack(ATT8, att("L2_xattn_", low, "b_q", "b_k")),
        "w8": _pack(FF2, {"w1": up(a["L2_ffn_w1"]), "w2": down(a["L2_ffn_w2"]), "router": a["L2_ffn_wr"],
                          "b1": a["L2_ffn_b1"].reshape(E, 4, P).transpose(2, 0, 1).reshape(P, -1)}),
        "w9": _pack(SELF_PRIOR, {**att("L3_attn_", cap, "bq", "bk", "bv"), "gauss": gauss,
                                 "lam": np.broadcast_to(a["L3_attn_prior_lambda"].reshape(1, 1), (P, 1))}),
        "w10": _pack(ATT8, att("L3_xattn_", cap)),
        "w11": _pack(FF3, {k: (up if k != "w2" else down)(np.concatenate([a["L3_ffn_" + k], a["L3_ffn_s" + k]]))
                           for k in ("w1", "w3", "w2")} | {"router": a["L3_ffn_router_w"].T}),
    }
    rows = np.zeros((1, NROWS), np.float32)
    for name, source in (("x0_bv", "L0_xattn_bv"), ("x0_bo", "L0_xattn_bo"), ("a1_bo", "L1_attn_bo"), ("x1_bo", "L1_xattn_b_out"),
                         ("f1_b", "L1_ffn_bias"), ("a2_bo", "L2_attn_bout"), ("x2_bv", "L2_xattn_b_v"), ("x2_bo", "L2_xattn_b_o"),
                         ("f2_br", "L2_ffn_br"), ("f2_b2", "L2_ffn_b2"), ("a3_bv", "L3_attn_bv"), ("a3_bo", "L3_attn_bo"),
                         ("x3_bo", "L3_xattn_bo"), ("f3_br", "L3_ffn_experts_bias")):
        c, n = ROWS[name]
        rows[0, c:c + n] = a[source].reshape(-1)
    ins |= {"x": _tokens(a["x"]), "consts": consts, "rows": rows, "ctxT": a["ctx_1024"].transpose(2, 0, 1).reshape(P, -1),
            "indices": _tokens(a["L1_ffn_expert_indices"])}
    return ins


def kernel(**inputs):
    import concourse.bacc as bacc
    from concourse.bass_utils import run_bass_kernel_spmd as run

    arrays = _layouts({k: np.asarray(v) for k, v in inputs.items()})
    nc = bacc.Bacc("TRN2", target_bir_lowering=False, num_devices=1)
    used = {k: np.ascontiguousarray(v) for k, v in arrays.items() if not (k[0] == "w" and int(k[1:]) not in SUBLAYERS)}
    ins = {k: nc.dram_tensor(f"{k}_dram", v.shape, mybir.dt.from_np(v.dtype), kind="ExternalInput").ap()
           for k, v in used.items()}
    out = nc.dram_tensor("out_dram", (P, B * NT * D), F32, kind="ExternalOutput").ap()
    build(nc, ins, out)
    r = run(nc, [{f"{k}_dram": v for k, v in used.items()}], core_ids=[0])
    return np.ascontiguousarray(r.results[0]["out_dram"].reshape(P, B, NT, D).transpose(1, 2, 0, 3).reshape(B, S, D))
```
